# Optimizing a Trainium2 kernel written in Bass

```python
import numpy as np
import jax
import jax.numpy as jnp

def _softmax(x, axis=-1):
    return jax.nn.softmax(x, axis=axis)

def _gelu(x):
    return jax.nn.gelu(x, approximate=True)

def _silu(x):
    return jax.nn.silu(x)

def _sigmoid(x):
    return jax.nn.sigmoid(x)

def _layernorm(x, axis=-1, eps=1e-05):
    m = jnp.mean(x, axis=axis, keepdims=True)
    v = jnp.var(x, axis=axis, keepdims=True)
    return (x - m) / jnp.sqrt(v + eps)

def _scatter_add(tgt, idx, src, axis=0):
    return tgt.at[idx].add(src)

def _segment_sum(src, seg, n):
    return jax.ops.segment_sum(src, seg, n)
kernel_name = 'mk_decoder_postln_d1_seqx_r8_e41e57'

def setup_inputs(seed: int=0):
    np.random.seed(seed)
    _w = jnp.asarray

    def _rec_inputs():
        import jax
        import jax.numpy as jnp
        _rk = jax.random.key(seed)
        x = -0.0003929 + 0.9999 * jax.random.normal(jax.random.fold_in(_rk, 1), (8, 128, 512), jnp.float32)
        _lenS = 128 - jax.random.randint(jax.random.fold_in(_rk, 7), (8,), 0, max(1, 128 // 4) + 1, jnp.int32)
        _lenS2 = 128 - jax.random.randint(jax.random.fold_in(_rk, 8), (8,), 0, max(1, 128 // 4) + 1, jnp.int32)
        _ctx_4096P = jax.random.normal(jax.random.fold_in(_rk, 11), (8, 16, 512), jnp.float32)
        _ctx_4096c = jax.random.dirichlet(jax.random.fold_in(_rk, 511), 0.3 * jnp.ones((16,), jnp.float32), (8, 128))
        _ctx_4096t = jnp.einsum('bsk,bkd->bsd', _ctx_4096c, _ctx_4096P)
        _ctx_4096t = _ctx_4096t * jax.lax.rsqrt(jnp.mean(jnp.square(_ctx_4096t)) + 1e-12) * 0.953939
        ctx_4096 = 2.81802e-05 + 1.00001 * (_ctx_4096t + 0.3 * jax.random.normal(jax.random.fold_in(_rk, 611), (8, 128, 512), jnp.float32))
        return (x, ctx_4096)
    x, ctx_4096 = _rec_inputs()

    def _L0_attn_setup():
        import jax, jax.numpy as jnp
        import numpy as np
        N_HEADS = 32
        N_KV_HEADS = 8
        DIM = 512
        HEAD_DIM = DIM // N_HEADS
        N_REP = N_HEADS // N_KV_HEADS
        ROPE_THETA = 10000.0

        def _apply_rope(x):
            seq = x.shape[2]
            hd = x.shape[-1]
            inv_freq = 1.0 / ROPE_THETA ** (jnp.arange(0, hd, 2, dtype=jnp.float32) / hd)
            angles = jnp.arange(seq, dtype=jnp.float32)[:, None] * inv_freq[None, :]
            cos = jnp.cos(angles)[None, None]
            sin = jnp.sin(angles)[None, None]
            x1 = x[..., 0::2]
            x2 = x[..., 1::2]
            r1 = x1 * cos - x2 * sin
            r2 = x1 * sin + x2 * cos
            return jnp.stack([r1, r2], axis=-1).reshape(x.shape)
        key = jax.random.key(seed)
        k1, k2, k3 = jax.random.split(key, 3)
        bs, seq = (1, 256)
        x = jax.random.normal(k1, (bs, seq, DIM), dtype=jnp.float32)
        w_qkv = jax.random.normal(k2, (DIM, HEAD_DIM * (N_HEADS + 2 * N_KV_HEADS)), dtype=jnp.float32) * 0.02
        w_o = jax.random.normal(k3, (N_HEADS * HEAD_DIM, DIM), dtype=jnp.float32) * 0.02
        return {'x': x, 'w_qkv': w_qkv, 'w_o': w_o}
    _L0_attn_all = _L0_attn_setup()
    _L0_attn_in = {k: v for k, v in _L0_attn_all.items() if k in ('w_qkv', 'w_o')}
    del _L0_attn_all

    def _L0_xattn_setup():
        import jax, jax.numpy as jnp
        import numpy as np
        B, D, N, H, K = (4, 128, 512, 16, 32)
        HD = D // H

        def _conv1x1(x, W, b):
            return jnp.einsum('od,bdn->bon', W, x) + b[None, :, None]
        key = jax.random.key(seed)
        ks = jax.random.split(key, 12)
        std_w = 1.0 / np.sqrt(D)
        std_p = 1.0 / np.sqrt(K)
        u = lambda k, shape, s: jax.random.uniform(k, shape, jnp.float32, -s, s)
        return {'query': jax.random.normal(ks[0], (B, D, N), jnp.float32), 'key': jax.random.normal(ks[1], (B, D, N), jnp.float32), 'value': jax.random.normal(ks[2], (B, D, N), jnp.float32), 'Wq': u(ks[3], (D, D), std_w), 'bq': u(ks[4], (D,), std_w), 'Wk': u(ks[5], (D, D), std_w), 'bk': u(ks[6], (D,), std_w), 'Wv': u(ks[7], (D, D), std_w), 'bv': u(ks[8], (D,), std_w), 'proj_k': u(ks[9], (N, K), std_p), 'proj_v': u(ks[10], (N, K), std_p), 'Wm': u(ks[11], (D, D), std_w), 'bm': u(jax.random.fold_in(key, 99), (D,), std_w)}
    _L0_xattn_all = _L0_xattn_setup()
    _L0_xattn_in = {k: v for k, v in _L0_xattn_all.items() if k in ('Wq', 'bq', 'Wk', 'bk', 'Wv', 'bv', 'proj_k', 'proj_v', 'Wm', 'bm')}
    del _L0_xattn_all

    def _L0_ffn_setup():
        import jax, jax.numpy as jnp
        import numpy as np
        H = 512
        I = 256
        E = 16
        TOPK = 4
        SI = 256
        key = jax.random.key(seed)
        ks = jax.random.split(key, 9)
        s = 0.02
        return {'hidden_states': jax.random.normal(ks[0], (2, 256, H), dtype=jnp.float32), 'gate_w': jax.random.normal(ks[1], (E, H), dtype=jnp.float32) * s, 'bias': jnp.zeros((E,), dtype=jnp.float32), 'Wg': jax.random.normal(ks[2], (E, I, H), dtype=jnp.float32) * s, 'Wu': jax.random.normal(ks[3], (E, I, H), dtype=jnp.float32) * s, 'Wd': jax.random.normal(ks[4], (E, H, I), dtype=jnp.float32) * s, 'Sg': jax.random.normal(ks[5], (SI, H), dtype=jnp.float32) * s, 'Su': jax.random.normal(ks[6], (SI, H), dtype=jnp.float32) * s, 'Sd': jax.random.normal(ks[7], (H, SI), dtype=jnp.float32) * s}
    _L0_ffn_all = _L0_ffn_setup()
    _L0_ffn_in = {k: v for k, v in _L0_ffn_all.items() if k in ('gate_w', 'bias', 'Wg', 'Wu', 'Wd', 'Sg', 'Su', 'Sd')}
    del _L0_ffn_all
    return {'x': x, 'ctx_4096': ctx_4096, 'L0_attn_w_qkv': _L0_attn_in['w_qkv'], 'L0_attn_w_o': _L0_attn_in['w_o'], 'L0_xattn_Wq': _L0_xattn_in['Wq'], 'L0_xattn_bq': _L0_xattn_in['bq'], 'L0_xattn_Wk': _L0_xattn_in['Wk'], 'L0_xattn_bk': _L0_xattn_in['bk'], 'L0_xattn_Wv': _L0_xattn_in['Wv'], 'L0_xattn_bv': _L0_xattn_in['bv'], 'L0_xattn_proj_k': _L0_xattn_in['proj_k'], 'L0_xattn_proj_v': _L0_xattn_in['proj_v'], 'L0_xattn_Wm': _L0_xattn_in['Wm'], 'L0_xattn_bm': _L0_xattn_in['bm'], 'L0_ffn_gate_w': _L0_ffn_in['gate_w'], 'L0_ffn_bias': _L0_ffn_in['bias'], 'L0_ffn_Wg': _L0_ffn_in['Wg'], 'L0_ffn_Wu': _L0_ffn_in['Wu'], 'L0_ffn_Wd': _L0_ffn_in['Wd'], 'L0_ffn_Sg': _L0_ffn_in['Sg'], 'L0_ffn_Su': _L0_ffn_in['Su'], 'L0_ffn_Sd': _L0_ffn_in['Sd']}

def reference(x, ctx_4096, L0_attn_w_qkv, L0_attn_w_o, L0_xattn_Wq, L0_xattn_bq, L0_xattn_Wk, L0_xattn_bk, L0_xattn_Wv, L0_xattn_bv, L0_xattn_proj_k, L0_xattn_proj_v, L0_xattn_Wm, L0_xattn_bm, L0_ffn_gate_w, L0_ffn_bias, L0_ffn_Wg, L0_ffn_Wu, L0_ffn_Wd, L0_ffn_Sg, L0_ffn_Su, L0_ffn_Sd):
    import jax
    import jax.numpy as jnp

    def _L0_attn_ref(x, w_qkv, w_o):
        import jax, jax.numpy as jnp
        import numpy as np
        N_HEADS = 32
        N_KV_HEADS = 8
        DIM = 512
        HEAD_DIM = DIM // N_HEADS
        N_REP = N_HEADS // N_KV_HEADS
        ROPE_THETA = 10000.0

        def _apply_rope(x):
            seq = x.shape[2]
            hd = x.shape[-1]
            inv_freq = 1.0 / ROPE_THETA ** (jnp.arange(0, hd, 2, dtype=jnp.float32) / hd)
            angles = jnp.arange(seq, dtype=jnp.float32)[:, None] * inv_freq[None, :]
            cos = jnp.cos(angles)[None, None]
            sin = jnp.sin(angles)[None, None]
            x1 = x[..., 0::2]
            x2 = x[..., 1::2]
            r1 = x1 * cos - x2 * sin
            r2 = x1 * sin + x2 * cos
            return jnp.stack([r1, r2], axis=-1).reshape(x.shape)
        bs, seq, _ = x.shape
        qkv = x @ w_qkv
        q_sz = N_HEADS * HEAD_DIM
        kv_sz = N_KV_HEADS * HEAD_DIM
        xq = qkv[..., :q_sz].reshape(bs, seq, N_HEADS, HEAD_DIM).transpose(0, 2, 1, 3)
        xk = qkv[..., q_sz:q_sz + kv_sz].reshape(bs, seq, N_KV_HEADS, HEAD_DIM).transpose(0, 2, 1, 3)
        xv = qkv[..., q_sz + kv_sz:].reshape(bs, seq, N_KV_HEADS, HEAD_DIM).transpose(0, 2, 1, 3)
        xq = _apply_rope(xq)
        xk = _apply_rope(xk)
        keys = jnp.repeat(xk, N_REP, axis=1)
        values = jnp.repeat(xv, N_REP, axis=1)
        scale = 1.0 / jnp.sqrt(jnp.float32(HEAD_DIM))
        scores = jnp.einsum('bhsd,bhtd->bhst', xq, keys) * scale
        causal = jnp.tril(jnp.ones((seq, seq), dtype=bool))[None, None]
        scores = jnp.where(causal, scores, -jnp.inf)
        probs = jax.nn.softmax(scores, axis=-1)
        out = jnp.einsum('bhst,bhtd->bhsd', probs, values)
        out = out.transpose(0, 2, 1, 3).reshape(bs, seq, N_HEADS * HEAD_DIM)
        return out @ w_o

    def _L0_xattn_ref(query, key, value, Wq, bq, Wk, bk, Wv, bv, proj_k, proj_v, Wm, bm):
        import jax, jax.numpy as jnp
        import numpy as np
        B, D, N, H, K = (4, 128, 512, 16, 32)
        HD = D // H

        def _conv1x1(x, W, b):
            return jnp.einsum('od,bdn->bon', W, x) + b[None, :, None]
        b = query.shape[0]
        q = _conv1x1(query, Wq, bq)
        k = _conv1x1(key, Wk, bk)
        v = _conv1x1(value, Wv, bv)
        k = jnp.einsum('bdn,nk->bdk', k, proj_k)
        v = jnp.einsum('bdn,nk->bdk', v, proj_v)
        q = q.reshape(b, HD, H, -1)
        k = k.reshape(b, HD, H, -1)
        v = v.reshape(b, HD, H, -1)
        scores = jnp.einsum('bdhn,bdhk->bhnk', q, k) / HD ** 0.5
        prob = jax.nn.softmax(scores, axis=-1)
        x = jnp.einsum('bhnk,bdhk->bdhn', prob, v)
        return _conv1x1(x.reshape(b, HD * H, -1), Wm, bm)

    def _L0_ffn_ref(hidden_states, gate_w, bias, Wg, Wu, Wd, Sg, Su, Sd):
        import jax, jax.numpy as jnp
        import numpy as np
        H = 512
        I = 256
        E = 16
        TOPK = 4
        SI = 256
        orig_shape = hidden_states.shape
        x = hidden_states.reshape(-1, orig_shape[-1])
        scores = jax.nn.sigmoid(x @ gate_w.T) + bias
        topk_w, topk_idx = jax.lax.top_k(scores, TOPK)
        topk_w = topk_w / (jnp.sum(topk_w, axis=-1, keepdims=True) + 1e-20)
        cw = jnp.sum(jax.nn.one_hot(topk_idx, E, dtype=x.dtype) * topk_w[..., None], axis=1)
        g = jnp.einsum('th,eih->eti', x, Wg)
        u = jnp.einsum('th,eih->eti', x, Wu)
        z = jax.nn.silu(g) * u
        zw = z * cw.T[:, :, None]
        out = jnp.einsum('eti,ehi->th', zw, Wd)
        out = out + jax.nn.silu(x @ Sg.T) * (x @ Su.T) @ Sd.T
        return out.reshape(orig_shape)
    x = _layernorm(x + _L0_attn_ref(x, L0_attn_w_qkv, L0_attn_w_o), axis=-1)
    x = _layernorm(x + _L0_xattn_ref(x, ctx_4096, ctx_4096, L0_xattn_Wq, L0_xattn_bq, L0_xattn_Wk, L0_xattn_bk, L0_xattn_Wv, L0_xattn_bv, L0_xattn_proj_k, L0_xattn_proj_v, L0_xattn_Wm, L0_xattn_bm), axis=-1)
    x = _layernorm(x + _L0_ffn_ref(x, L0_ffn_gate_w, L0_ffn_bias, L0_ffn_Wg, L0_ffn_Wu, L0_ffn_Wd, L0_ffn_Sg, L0_ffn_Su, L0_ffn_Sd), axis=-1)
    return x

_drawn_inputs = setup_inputs


def setup_inputs(seed=0):
    import zlib

    import numpy as np

    out = dict(_drawn_inputs(seed))
    spreads = {'L0_ffn_bias': (0.0, 0.528)}
    factors = {'L0_xattn_bq': 7.934,
     'L0_xattn_bk': 4.882,
     'L0_xattn_bv': 6.917,
     'L0_xattn_bm': 8.0,
     'L0_ffn_gate_w': 4.337,
     'L0_ffn_Wg': 3.302,
     'L0_ffn_Wu': 3.251,
     'L0_ffn_Wd': 3.233}
    for name, (base, spread) in spreads.items():
        noise = np.random.default_rng([zlib.crc32(name.encode()), seed]).standard_normal(out[name].shape)
        drawn = base * np.exp(spread * noise) if base else spread * noise
        out[name] = jnp.asarray(drawn.astype(out[name].dtype))
    for name, factor in factors.items():
        out[name] = (out[name] * factor).astype(out[name].dtype)
    return out
```

```python
from contextlib import ExitStack

import numpy as np

import concourse.bass as bass
from concourse import mybir

F32 = mybir.dt.float32
F32R = mybir.dt.float32r
BF16 = mybir.dt.bfloat16
F16 = mybir.dt.float16
I32 = mybir.dt.int32
ALU = mybir.AluOpType
ACT = mybir.ActivationFunctionType
AX = mybir.AxisListType

B, S, D = 8, 128, 512
KC = D // 128
HD, NQ, NKV = 16, 32, 8
REP = NQ // NKV
QKV = HD * (NQ + 2 * NKV)
QK_HEADS = NQ + NKV
STACK = 4 * HD
XH, XD, XK = 16, 8, 32
HPT = 128 // XK
NE, TOPK, FF = 16, 4, 256
FC = FF // 128
TOKENS = B * S
SLOT = 128
REGION = TOKENS + SLOT
IDLE_ROW = NE * REGION
SLOTS = (TOKENS * TOPK + NE * (SLOT - 1)) // SLOT
HB = B // 2
WCH = KC + FC
EPS = 1e-5
MASKED = -1e30


def tables():
    inv_freq = (1.0 / np.float32(10000.0) ** (np.arange(0, HD, 2, dtype=np.float32) / np.float32(HD))).astype(np.float32)
    angles = np.arange(S, dtype=np.float32)[:, None] * inv_freq[None, :]
    cos, sin = np.cos(angles).astype(np.float32), np.sin(angles).astype(np.float32)
    rope = np.stack([np.concatenate([cos, cos], 1), np.concatenate([sin, sin], 1)], 1)
    return {
        "rope": np.ascontiguousarray(rope),
        "head_mask": (np.arange(128)[:, None] // XD == np.arange(XH)[None]).astype(np.float32),
        "value_mask": (np.arange(128)[:, None] // XK == np.arange(HPT)[None]).astype(np.float32),
        "region": np.broadcast_to(np.arange(NE, dtype=np.float32) * REGION, (128, NE)),
        "iota16": np.broadcast_to(np.arange(NE, dtype=np.float32) - NE, (128, NE)),
        "tri": (np.arange(128)[:, None] < np.arange(128)[None]).astype(np.float32),
        "thresholds": np.broadcast_to(np.array([-1] + [128 * k for k in range(1, 8)], np.float32), (128, 8)),
        "upto_mask": np.broadcast_to((np.arange(NE)[None] <= np.arange(NE)[:, None]).astype(np.float32), (128, NE, NE)),
        "slot_no": np.arange(SLOTS, dtype=np.float32)[None],
        "alternate": np.array([[(-1.0) ** e for e in range(NE - 1)] + [0.0]], np.float32),
        "ident": np.eye(128, dtype=np.float32),
        "causal": np.where(np.arange(S)[None, :] > np.arange(S)[:, None], np.float32(MASKED), np.float32(0)).astype(np.float32),
    }


def program(nc, T):
    T["xs"] = nc.dram_tensor("dispatched", (NE * REGION + SLOT, D), F32).ap()
    T["ys"] = nc.dram_tensor("slot_results", (SLOTS * SLOT, D), F32).ap()
    with ExitStack() as ctx:
        def sb(name, shape, dt=F32):
            return ctx.enter_context(nc.sbuf_tensor(name, shape, dt))

        def sem(name):
            return ctx.enter_context(nc.semaphore(name))

        ident = sb("ident", [128, 128])
        neg_half = sb("neg_half", [128, 1])
        eps = sb("eps", [128, 1])
        x1 = sb("x1", [128, B, D])
        base = x1
        x2 = sb("x2", [128, B, D])
        bias_e = sb("bias_e", [128, NE]); region = sb("region", [128, NE])
        iota16 = sb("iota16", [128, NE]); tri = sb("tri", [128, 128]); tri_bf = sb("tri_bf", [128, 128], BF16)
        e_score = sb("e_score", [128, HB, NE]); e_eq = sb("e_eq", [128, HB, NE]); e_low = sb("e_low", [128, HB])
        picked = sb("picked", [128, TOPK, B, NE])
        weight = sb("weight", [128, TOPK, B]); w_sum = sb("w_sum", [128, HB]); w_rec = sb("w_rec", [128, HB])
        chosen = sb("chosen", [128, HB, NE]); chosen_bf = sb("chosen_bf", [128, HB, NE], BF16)
        before = sb("before", [128, B + 1, NE]); before_bf = sb("before_bf", [128, B + 1, NE], BF16)
        rank = sb("rank", [128, B, NE]); place = sb("place", [128, B, NE])
        picked_place = sb("picked_place", [128, TOPK, B, NE]); row_f = sb("row_f", [128, TOPK, B])
        row_of = sb("row_of", [128, TOPK, B], I32); yrow_of = sb("yrow_of", [128, TOPK, B], I32)
        x2T_hi = sb("x2T_hi", [128, KC, B // 2, 128], F32R)
        x2T_lo = sb("x2T_lo", [128, KC, B // 2, 128], F32R)
        ones_bf = sb("ones_bf", [128, 128], BF16)

        self_scope = ExitStack()
        outer_sb = sb

        def sb(name, shape, dt=F32):
            return self_scope.enter_context(nc.sbuf_tensor(name, shape, dt))

        ident_bf = sb("ident_bf", [128, 128], BF16)
        causal = sb("causal", [128, 128])
        causal_bf = sb("causal_bf", [128, REP, 128], BF16)
        rope = sb("rope", [128, 2, HD])
        wst = sb("wst", [128, KC, QKV])
        wqkv_hi = sb("wqkv_hi", [128, KC, QKV], F32R)
        wqkv_lo = sb("wqkv_lo", [128, KC, QKV], F32R)
        wo_in = sb("wo_in", [128, KC, D])
        wo_hi = sb("wo_hi", [128, KC, D], F32R)
        wo_lo = sb("wo_lo", [128, KC, D], F32R)
        xT = sb("xT", [128, 2, KC, 128])
        xT_hi = [sb(f"xT_hi{p}", [128, KC, 128], F32R) for p in (0, 1)]
        xT_lo = [sb(f"xT_lo{p}", [128, KC, 128], F32R) for p in (0, 1)]
        x_in = sb("x_in", [128, 2, D])
        rope_cos = sb("rope_cos", [128, QK_HEADS, 2, HD // 2])
        rope_sin = sb("rope_sin", [128, QK_HEADS, 2, HD // 2])
        rotated = sb("rotated", [128, QK_HEADS, HD])
        stack = sb("stack", [128, QK_HEADS, 4, HD], F32R)
        v_ones = [sb(f"v_ones{p}", [128, NKV, 32]) for p in (0, 1)]
        qT = [sb(f"qT{p}", [128, NQ // 2, 128], F32R) for p in (0, 1)]
        kT = [sb(f"kT{p}", [128, NKV // 2, 128], F32R) for p in (0, 1)]
        qT_half = sb("qT_half", [128, NQ // 2, 128], F16)
        kT_half = sb("kT_half", [128, NKV // 2, 128], F16)
        pv_sb = [sb(f"pv_sb{h}", [128, REP, 128]) for h in (0, 1)]
        neg_max = sb("neg_max", [128, NKV, REP])
        neg_max_parts = sb("neg_max_parts", [128, 4, 2, NKV // 2, REP], F32R)
        maxT = sb("maxT", [64, 128], F32R)
        probs = [sb(f"probs{r}", [128, REP, 128]) for r in range(4)]
        attn_rsum = sb("attn_rsum", [128, 2, REP, 4])
        attn_out = sb("attn_out", [128, 2, NQ // 2, HD])
        oT_hi = sb("oT_hi", [128, KC, 128], F32R)
        oT_lo = sb("oT_lo", [128, KC, 128], F32R)
        y1 = sb("y1", [128, D])
        bn6 = sb("bn6", [128, 6])
        mean_var = sb("mean_var", [128, 2])
        rstd = sb("rstd", [128, 1])
        self_scope.close()
        sb = outer_sb

        gate_in = sb("gate_in", [128, KC, NE]); gate_hi = sb("gate_hi", [128, KC, NE], F32R); gate_lo = sb("gate_lo", [128, KC, NE], F32R)
        logitT = sb("logitT", [NE, HB * 128])
        w_raw = sb("w_raw", [128, 2, WCH, D])
        w_hi = sb("w_hi", [128, 2, WCH, D], F32R); w_lo = sb("w_lo", [128, 2, WCH, D], F32R)
        count = sb("count", [128, NE]); thresholds = sb("thresholds", [128, 8]); over = sb("over", [128, NE, 8])
        n_slots = sb("n_slots", [128, NE]); slots_to = sb("slots_to", [128, NE]); slot_base = sb("slot_base", [128, NE])
        upto_mask = sb("upto_mask", [128, NE, NE]); prod = sb("prod", [128, NE, NE])
        slot_no = sb("slot_no", [1, SLOTS]); passed_e = sb("passed_e", [1, SLOTS, NE]); passed_w = sb("passed_w", [1, SLOTS, NE]); alternate = sb("alternate", [1, NE])
        tab_f = sb("tab_f", [1, 6, SLOTS + 1]); tab = sb("tab", [1, 4, SLOTS], I32); pad_f = sb("pad_f", [1, NE]); pad_row = sb("pad_row", [1, NE], I32)
        zeros = sb("zeros", [128, D])
        sh_silu = sb("sh_silu", [128, D]); sh_z = sb("sh_z", [128, D])
        shT_hi = sb("shT_hi", [128, FC, D], F32R); shT_lo = sb("shT_lo", [128, FC, D], F32R)
        gathered = [w_raw[:, q, 0:TOPK] for q in (0, 1)]
        out_sb = [w_raw[:, q, TOPK] for q in (0, 1)]
        y3 = w_raw[:, 0, TOPK + 1]
        bn6c = sb("bn6c", [128, 6]); mean_var3 = sb("mean_var3", [128, 2]); rstd3 = sb("rstd3", [128, 1])
        xs_dram, ys_dram = T["xs"], T["ys"]
        cross_scope = ExitStack()

        def sb(name, shape, dt=F32):
            return cross_scope.enter_context(nc.sbuf_tensor(name, shape, dt))

        wq_in = sb("wq_in", [128, 128]); wq_hi = sb("wq_hi", [128, 128], F32R); wq_lo = sb("wq_lo", [128, 128], F32R)
        wm_in = sb("wm_in", [128, 128]); wm_hi = sb("wm_hi", [128, 128], F32R); wm_lo = sb("wm_lo", [128, 128], F32R)
        wk = sb("wk", [128, 128]); wv = sb("wv", [128, 128])
        bias_q = sb("bias_q", [128, 1]); bias_m = sb("bias_m", [128, 1])
        bias_k_row = sb("bias_k_row", [1, 128]); bias_v_row = sb("bias_v_row", [1, 128])
        proj = sb("proj", [128, KC, 2 * XK])
        head_mask = sb("head_mask", [128, XH]); value_mask = sb("value_mask", [128, HPT])
        ones_col = sb("ones_col", [128, 1])
        proj_sum_k = sb("proj_sum_k", [1, XK]); proj_sum_v = sb("proj_sum_v", [1, HPT, XK])
        ctxT = [sb(f"ctxT{p}", [128, KC, 128]) for p in (0, 1)]
        ctx_k = sb("ctx_k", [128, XK]); ctx_v = sb("ctx_v", [128, HPT, XK])
        keys = sb("keys", [128, XH, XK])
        keys_hi = [sb(f"keys_hi{p}", [128, XH * XK], F32R) for p in (0, 1)]
        keys_lo = [sb(f"keys_lo{p}", [128, XH * XK], F32R) for p in (0, 1)]
        values = [sb(f"values{p}", [128, XH // HPT, HPT, XD]) for p in (0, 1)]
        x1_hi = sb("x1_hi", [128, D], F32R); x1_lo = sb("x1_lo", [128, D], F32R)
        xq_hi = sb("xq_hi", [128, D], F32R); xq_lo = sb("xq_lo", [128, D], F32R)
        xmax = sb("xmax", [128, 2, XH]); xsum = sb("xsum", [128, 2, XH]); xrec = sb("xrec", [128, 2, XH])
        xprob = [sb(f"xprob{t}", [128, XH, XK]) for t in (0, 1)]
        xprobT = sb("xprobT", [128, XH // HPT, D])
        xo_hi = sb("xo_hi", [128, D], F32R); xo_lo = sb("xo_lo", [128, D], F32R)
        y2 = sb("y2", [128, D]); x2s = sb("x2s", [128, D])
        bn6b = sb("bn6b", [128, 6]); mean_var2 = sb("mean_var2", [128, 2]); rstd2 = sb("rstd2", [128, 1])
        cross_scope.close()
        sb = outer_sb
        xs_in = [sb(f"xs_in{q}", [128, D]) for q in (0, 1)]
        xsT_hi = [sb(f"xsT_hi{q}", [128, KC, 128], F32R) for q in (0, 1)]
        xsT_lo = [sb(f"xsT_lo{q}", [128, KC, 128], F32R) for q in (0, 1)]
        silu_g = sb("silu_g", [128, FF]); z = sb("z", [128, FF])
        zT_hi = sb("zT_hi", [128, FC, 128], F32R); zT_lo = sb("zT_lo", [128, FC, 128], F32R)
        y_sb = [sb(f"y_sb{q}", [128, D]) for q in (0, 1)]

        bank = [ctx.enter_context(nc.psum_tensor(f"bank{i}", [128, 512], F32)) for i in range(2, 8)]
        qkv_ps = ctx.enter_context(nc.psum_tensor("qkv_ps", [128, 1024], F32))
        turn = [bank[0], bank[1]]
        score = [bank[2], bank[3]]
        out_a, out_b = bank[4], bank[5]

        consts_in = sem("consts_in"); wqkv_in = [sem(f"wqkv_in{c}") for c in range(KC)]; wo_loaded = sem("wo_loaded")
        xT_in = [sem(f"xT_in{p}") for p in (0, 1)]; x_loaded = [sem(f"x_loaded{p}") for p in (0, 1)]
        consts_ready = sem("consts_ready")
        wqkv_hi_ready = sem("wqkv_hi_ready"); wqkv_lo_ready = sem("wqkv_lo_ready")
        wo_hi_ready = sem("wo_hi_ready"); wo_lo_ready = sem("wo_lo_ready")
        xT_hi_ready = sem("xT_hi_ready"); xT_lo_ready = sem("xT_lo_ready")
        qkv_done = sem("qkv_done"); rope_read = sem("rope_read"); v_ready = sem("v_ready")
        rot_ready = sem("rot_ready"); stack_hi = sem("stack_hi"); stack_lo = sem("stack_lo")
        qkT_turned = sem("qkT_turned"); qkT_by_act = sem("qkT_by_act"); qkT_by_dve = sem("qkT_by_dve")
        pass1_done = sem("pass1_done"); max_done = sem("max_done")
        max_hi = sem("max_hi"); max_parts = sem("max_parts"); max_turned = sem("max_turned")
        maxT_ready = sem("maxT_ready"); max_rows = sem("max_rows")
        pass2_done = sem("pass2_done"); exp_done = sem("exp_done"); causal_done = sem("causal_done")
        pv_done = sem("pv_done"); halves_ready = sem("halves_ready"); pv_copied = sem("pv_copied"); pv_turned = sem("pv_turned"); rsum_ready = sem("rsum_ready"); attn_normed = sem("attn_normed")
        oT_turned = sem("oT_turned"); oT_hi_ready = sem("oT_hi_ready"); oT_lo_ready = sem("oT_lo_ready")
        wo_done = sem("wo_done"); y1_ready = sem("y1_ready"); stats1 = sem("stats1"); mv1 = sem("mv1")
        ve1 = sem("ve1"); rstd1 = sem("rstd1"); x1_ready = sem("x1_ready")
        cross_in = sem("cross_in"); cross_hi = sem("cross_hi"); cross_lo = sem("cross_lo"); cross_masks = sem("cross_masks")
        proj_summed = sem("proj_summed"); proj_sums = sem("proj_sums")
        ctxT_in = [sem(f"ctxT_in{p}") for p in (0, 1)]
        ctx_done = sem("ctx_done"); ctx_copied = sem("ctx_copied"); kv_done = sem("kv_done")
        keys_ready = sem("keys_ready"); values_ready = sem("values_ready"); keys_hi_ready = sem("keys_hi_ready"); keys_lo_ready = sem("keys_lo_ready")
        x1_hi_ready = sem("x1_hi_ready"); x1_lo_ready = sem("x1_lo_ready"); xq_done = sem("xq_done")
        xq_hi_ready = sem("xq_hi_ready"); xq_lo_ready = sem("xq_lo_ready")
        xscore_done = sem("xscore_done"); xmax_ready = sem("xmax_ready"); xsub_done = sem("xsub_done"); xexp_done = sem("xexp_done")
        xsum_ready = sem("xsum_ready"); xrec_ready = sem("xrec_ready"); xprob_ready = sem("xprob_ready")
        xprob_turned = sem("xprob_turned"); xprobT_ready = sem("xprobT_ready"); xpv_done = sem("xpv_done")
        xo_hi_ready = sem("xo_hi_ready"); xo_lo_ready = sem("xo_lo_ready"); wm_done = sem("wm_done")
        y2_ready = sem("y2_ready"); stats2 = sem("stats2"); mv2 = sem("mv2"); ve2 = sem("ve2"); rstd2_ready = sem("rstd2_ready")
        x2s_ready = sem("x2s_ready"); x2_ready = sem("x2_ready"); x2_turned = sem("x2_turned")
        x2T_hi_ready = sem("x2T_hi_ready"); x2T_lo_ready = sem("x2T_lo_ready")
        moe_in = sem("moe_in"); gate_hi_ready = sem("gate_hi_ready"); gate_lo_ready = sem("gate_lo_ready"); tri_ready = sem("tri_ready")
        logits_done = sem("logits_done"); logitT_ready = sem("logitT_ready"); logits_turned = sem("logits_turned"); logit_exp = sem("logit_exp")
        route = sem("route"); chosen_ready = sem("chosen_ready"); ranks_done = sem("ranks_done"); ranks_read = sem("ranks_read"); rows_ready = sem("rows_ready")
        scattered = sem("scattered"); counts_done = sem("counts_done"); tables_ready = sem("tables_ready"); yrows_ready = sem("yrows_ready"); padded = sem("padded")
        zeros_ready = sem("zeros_ready")
        w_in = sem("w_in"); w_hi_ready = sem("w_hi_ready"); w_lo_ready = sem("w_lo_ready")
        sh_hi_ready = sem("sh_hi_ready"); sh_lo_ready = sem("sh_lo_ready")
        sh_gate_done = sem("sh_gate_done"); sh_up_done = sem("sh_up_done"); sh_silu_done = sem("sh_silu_done"); sh_z_ready = sem("sh_z_ready")
        shT_hi_ready = sem("shT_hi_ready"); shT_lo_ready = sem("shT_lo_ready"); sh_down_done = sem("sh_down_done"); base_ready = sem("base_ready")
        xs_loaded = [sem(f"xs_loaded{q}") for q in (0, 1)]; xs_turned = sem("xs_turned"); xs_hi_ready = sem("xs_hi_ready"); xs_lo_ready = sem("xs_lo_ready")
        gate_up_done = sem("gate_up_done"); silu_done = sem("silu_done"); z_ready = sem("z_ready"); z_turned = sem("z_turned")
        zT_hi_ready = sem("zT_hi_ready"); zT_lo_ready = sem("zT_lo_ready"); slot_done = sem("slot_done"); y_copied = sem("y_copied")
        y_stored = [sem(f"y_stored{q}") for q in (0, 1)]
        gathered_in = [sem(f"gathered_in{q}") for q in (0, 1)]; combined = sem("combined"); stats3 = sem("stats3"); mv3 = sem("mv3"); ve3 = sem("ve3"); rstd3_ready = sem("rstd3_ready")
        out_ready = sem("out_ready"); out_in = [sem(f"out_in{q}") for q in (0, 1)]
        passed = sem("passed")

        block = ctx.enter_context(nc.Block())

        def over_batches(eng, step, first, last_):
            step(0, 0)
            with eng.Fori(0, (B - 2) // 2) as i:
                step(i * 2 + 1, 1)
                step(i * 2 + 2, 0)
            step(B - 1, 1)

        @block.sync
        def _(sp):
            def load_batch(b, p):
                sp.dma_start(xT[:, p], T["xT"][bass.ds(b, 1)].rearrange("o p c s -> (o p) c s")).then_inc(xT_in[p], 16)
                sp.dma_start(x_in[:, p], T["x"][bass.ds(b, 1)].rearrange("o s d -> (o s) d")).then_inc(x_loaded[p], 16)

            load_batch(0, 0)
            for c in range(KC):
                sp.dma_start(wst[:, c], T["w_qkv"][:, c]).then_inc(wqkv_in[c], 16)
            sp.dma_start(rope[:], T["rope"]).then_inc(consts_in, 16)
            sp.dma_start(ident[:], T["ident"]).then_inc(consts_in, 16)
            sp.dma_start(causal[:], T["causal"]).then_inc(consts_in, 16)
            load_batch(1, 1)
            sp.dma_start(wo_in[:], T["w_o"]).then_inc(wo_loaded, 16)

            def step(b, p, more=True):
                if more:
                    sp.wait_ge(xT_hi_ready, b + 1)
                    sp.wait_ge(xT_lo_ready, b + 1)
                sp.wait_ge(maxT_ready, b + 1)
                for a in (0, 1):
                    for part in (0, 1):
                        q = 16 * (2 * a + part)
                        row = 64 * a + 3 * HD + part
                        sp.dma_start(qT[p][row:row + 1, :, :].bitcast(F32), maxT[q:q + 16, :].bitcast(F32)).then_inc(max_rows, 16)
                if more:
                    sp.dma_start(xT[:, p], T["xT"][bass.ds(b + 2, 1)].rearrange("o p c s -> (o p) c s")).then_inc(xT_in[p], 16)
                    sp.wait_ge(y1_ready, b + 1)
                    sp.dma_start(x_in[:, p], T["x"][bass.ds(b + 2, 1)].rearrange("o s d -> (o s) d")).then_inc(x_loaded[p], 16)

            with sp.Fori(0, (B - 2) // 2) as i:
                step(i * 2, 0)
                step(i * 2 + 1, 1)
            step(B - 2, 0, False)
            step(B - 1, 1, False)
            sp.wait_ge(x1_ready, B)
            sp.wait_ge(wo_done, B)
            for tile, name in ((wq_in, "wq"), (wm_in, "wm"), (wk, "wk"), (wv, "wv"), (bias_q, "bq"), (bias_m, "bm"),
                               (bias_k_row, "bk"), (bias_v_row, "bv"), (proj, "proj"), (head_mask, "head_mask"),
                               (value_mask, "value_mask")):
                sp.dma_start(tile[:], T[name]).then_inc(cross_in, 16)

            def load_ctx(b, p):
                if not isinstance(b, int) or b > 1:
                    sp.wait_ge(ctx_done, b - 1)
                sp.dma_start(ctxT[p][:], T["ctxT"][bass.ds(b, 1)].rearrange("o p c s -> (o p) c s")).then_inc(ctxT_in[p], 16)

            load_ctx(0, 0)
            load_ctx(1, 1)
            MOE_CONSTS = ((gate_in, "gate"), (bias_e, "bias_e"), (region, "region"), (iota16, "iota16"), (tri, "tri"),
                          (thresholds, "thresholds"), (upto_mask, "upto_mask"), (slot_no, "slot_no"), (alternate, "alternate"))
            for tile, name in MOE_CONSTS:
                sp.dma_start(tile[:], T[name]).then_inc(moe_in, 16)
            with sp.Fori(1, B // 2) as i:
                load_ctx(i * 2, 0)
                load_ctx(i * 2 + 1, 1)
            sp.wait_ge(zeros_ready, 1)
            sp.dma_start(xs_dram[IDLE_ROW:IDLE_ROW + SLOT, :], zeros[:]).then_inc(padded, 16)
            sp.wait_ge(tables_ready, 1)
            with sp.Fori(0, NE) as e:
                row = sp.value_load(pad_row[0:1, bass.ds(e, 1)], min_val=0, max_val=IDLE_ROW - SLOT)
                sp.dma_start(xs_dram[bass.ds(row, SLOT), :], zeros[:]).then_inc(padded, 16)
            sp.wait_ge(padded, 16 * (NE + 1))
            sp.wait_ge(scattered, 16 * TOPK * B)

            def load_slot(t, q):
                row = sp.value_load(tab[0:1, 2, bass.ds(t, 1)], min_val=0, max_val=IDLE_ROW)
                sp.dma_start(xs_in[q][:], xs_dram[bass.ds(row, SLOT), :]).then_inc(xs_loaded[q], 16)

            def store_slot(t, q):
                sp.wait_ge(y_copied, t + 1)
                sp.dma_start(ys_dram[bass.ds(t * SLOT, SLOT), :], y_sb[q][:]).then_inc(y_stored[q], 16)

            load_slot(0, 0)
            load_slot(1, 1)

            def step(t, q):
                if not isinstance(t, int) or t < SLOTS - 2:
                    sp.wait_ge(xs_turned, t + 1)
                    load_slot(t + 2, q)
                if not isinstance(t, int) or t > 0:
                    store_slot(t - 1, 1 - q)

            step(0, 0)
            with sp.Fori(0, (SLOTS - 3) // 2) as i:
                step(i * 2 + 1, 1)
                step(i * 2 + 2, 0)
            step(SLOTS - 2, 1)
            step(SLOTS - 1, 0)
            store_slot(SLOTS - 1, 0)
            def store_out(b, p):
                sp.wait_ge(out_ready, b + 1)
                sp.dma_start(T["out"][bass.ds(b, 1)].rearrange("o s d -> (o s) d"), out_sb[p]).then_inc(out_in[p], 16)

            with sp.Fori(0, B // 2) as i:
                store_out(i * 2, 0)
                store_out(i * 2 + 1, 1)
            sp.wait_ge(out_in[0], 16 * (B // 2))
            sp.wait_ge(out_in[1], 16 * (B // 2))

        @block.tensor
        def _(pe):
            def split_product(out, stat_hi, stat_lo, mov_hi, mov_lo, start, stop):
                pe.matmul(out, stat_hi, mov_lo, start=start, stop=False)
                pe.matmul(out, stat_lo, mov_hi, start=False, stop=False)
                return pe.matmul(out, stat_hi, mov_hi, start=False, stop=stop)

            def qkv_chunk(b, p, c):
                if c == 0:
                    pe.wait_ge(xT_hi_ready, b + 1)
                    pe.wait_ge(xT_lo_ready, b + 1)
                    if not isinstance(b, int) or b > 0:
                        pe.wait_ge(rope_read, b)
                        pe.wait_ge(v_ready, b)
                if isinstance(b, int) and b == 0:
                    pe.wait_ge(wqkv_hi_ready, c + 1)
                    pe.wait_ge(wqkv_lo_ready, c + 1)
                for lo, hi in ((0, 512), (512, QKV)):
                    last = split_product(qkv_ps[:, lo:hi], xT_hi[p][:, c], xT_lo[p][:, c],
                                         wqkv_hi[:, c, lo:hi], wqkv_lo[:, c, lo:hi], c == 0, c == KC - 1)
                if c == KC - 1:
                    last.then_inc(qkv_done, 1)

            def turn_qk(b, p):
                pe.wait_ge(stack_hi, 2 * b + 2)
                pe.wait_ge(stack_lo, 2 * b + 2)
                pairs = stack[:].rearrange("s (j two) a e -> s j (two a e)", two=2).bitcast(F32)
                later = not isinstance(b, int) or b > 0
                for r in range(5):
                    if r == 1:
                        if not isinstance(b, int) or b > 1:
                            pe.wait_ge(oT_lo_ready, b - 1)
                    elif r == 3:
                        pe.wait_ge(qkT_by_dve, 2 * b + 1)
                    elif r > 0 or later:
                        pe.wait_ge(qkT_by_act, 3 * b + r // 2)
                    for j in range(4):
                        t = pe.transpose(turn[r % 2][:, 128 * j:128 * j + 128], pairs[:, 4 * r + j], ident[:])
                    t.then_inc(qkT_turned, 1)

            def pass1(b, p, g):
                u, a = g // 2, g % 2
                rows = slice(64 * a, 64 * a + HD)
                if g == 0:
                    pe.wait_ge(halves_ready, 2 * b + 2)
                if g < 2:
                    if not isinstance(b, int) or b > 0:
                        pe.wait_ge(exp_done, 8 * b - 1 + g)
                else:
                    pe.wait_ge(max_done, 8 * b + g - 1)
                pe.matmul(score[g % 2][:], ident_bf[:], causal_bf[:].rearrange("s r t -> s (r t)"), start=True, stop=False)
                for r in range(REP):
                    m = pe.matmul(score[g % 2][:, 128 * r:128 * r + 128], qT_half[rows, 4 * u + r], kT_half[rows, u],
                                  start=False, stop=(r == REP - 1))
                m.then_inc(pass1_done, 1)

            def turn_max(b):
                pe.wait_ge(max_parts, b + 1)
                if not isinstance(b, int) or b > 0:
                    pe.wait_ge(attn_normed, 2 * b)
                pe.transpose(out_b[:, 0:128], neg_max_parts[:].rearrange("s a q u r -> s (a q u r)").bitcast(F32),
                             ident[:]).then_inc(max_turned, 1)

            def pass2(b, p, g):
                u, a = g // 2, g % 2
                rows = slice(64 * a, 64 * a + 3 * HD + 2)
                if g == 0:
                    pe.wait_ge(max_rows, 64 * b + 64)
                if g < 2:
                    pe.wait_ge(max_done, 8 * b + 7 + g)
                else:
                    pe.wait_ge(exp_done, 8 * b + g - 1)
                pe.matmul(score[g % 2][:], kT[p][rows, u], qT[p][rows, 4 * u:4 * u + 4].rearrange("k r s -> k (r s)"),
                          start=True, stop=True).then_inc(pass2_done, 1)

            def pv(b, p, g):
                pe.wait_ge(causal_done, 8 * b + g + 1)
                if g == 0:
                    pe.wait_ge(v_ready, b + 1)
                    if not isinstance(b, int) or b > 0:
                        pe.wait_ge(y1_ready, b)
                if g == 4:
                    pe.wait_ge(maxT_ready, b + 1)
                dst = out_a if g < 4 else out_b
                j = 32 * (g % 4)
                pe.matmul(dst[j:j + 32, :], v_ones[p][:, g], probs[g % 4][:].rearrange("t r s -> t (r s)"),
                          start=True, stop=True).then_inc(pv_done, 1)

            def turn_pv(b, half):
                pe.wait_ge(pv_copied, 2 * b + half + 1)
                for r in range(REP):
                    t = pe.transpose((out_a, out_b)[half][:, 128 * r:128 * r + 128], pv_sb[half][:, r], ident[:])
                t.then_inc(pv_turned, 1)

            def turn_o(b):
                pe.wait_ge(attn_normed, 2 * b + 2)
                pe.wait_ge(qkT_by_dve, 2 * b + 4 if not (isinstance(b, int) and b == B - 1) else 2 * B)
                if isinstance(b, int) and b == B - 1:
                    pe.wait_ge(oT_lo_ready, B - 1)
                o = attn_out[:].rearrange("s a h e -> s (a h e)")
                for c in range(KC):
                    t = pe.transpose(turn[1][:, 128 * c:128 * c + 128], o[:, 128 * c:128 * c + 128], ident[:])
                t.then_inc(oT_turned, 1)

            def w_o(b):
                pe.wait_ge(oT_hi_ready, b + 1)
                pe.wait_ge(oT_lo_ready, b + 1)
                if isinstance(b, int) and b == 0:
                    pe.wait_ge(wo_hi_ready, 1)
                    pe.wait_ge(wo_lo_ready, 1)
                for c in range(KC):
                    last = split_product(out_a[:], oT_hi[:, c], oT_lo[:, c], wo_hi[:, c], wo_lo[:, c], c == 0, c == KC - 1)
                last.then_inc(wo_done, 1)

            pe.wait_ge(consts_ready, 4)
            for c in range(KC):
                qkv_chunk(0, 0, c)
            turn_qk(0, 0)

            def step(b, p):
                first, final = isinstance(b, int) and b == 0, isinstance(b, int) and b == B - 1
                for g in range(NKV):
                    pass1(b, p, g)
                    if g % 2 and not final:
                        qkv_chunk(b + 1, 1 - p, g // 2)
                turn_max(b)
                if not first:
                    w_o(b - 1)
                pass2(b, p, 0)
                for g in range(1, NKV):
                    pass2(b, p, g)
                    pv(b, p, g - 1)
                pv(b, p, NKV - 1)
                turn_pv(b, 0)
                turn_pv(b, 1)
                if not final:
                    turn_qk(b + 1, 1 - p)
                turn_o(b)

            over_batches(pe, step, None, None)
            w_o(B - 1)

            def context(b, p):
                pe.wait_ge(ctxT_in[p], 8 * (b - p) + 16)
                if not isinstance(b, int) or b > 0:
                    pe.wait_ge(ctx_copied, 2 * b)
                for c in range(KC):
                    m = pe.matmul(qkv_ps[:, 0:2 * XK], ctxT[p][:, c], proj[:, c], start=(c == 0), stop=(c == KC - 1))
                m.then_inc(ctx_done, 1)

            def keys_values(b):
                pe.wait_ge(ctx_copied, 2 * b + 2)
                if not isinstance(b, int) or b > 0:
                    pe.wait_ge(values_ready, b)
                k_ps, v_ps = qkv_ps[:, 512:512 + XK], qkv_ps[:, 640:768]
                pe.matmul(k_ps, wk[:], ctx_k[:], start=True, stop=False)
                pe.matmul(k_ps, bias_k_row[:], proj_sum_k[:], start=False, stop=True)
                pe.matmul(v_ps, ctx_v[:].rearrange("d h k -> d (h k)"), wv[:], start=True, stop=False)
                pe.matmul(v_ps, proj_sum_v[:].rearrange("o h k -> o (h k)"), bias_v_row[:], start=False, stop=True).then_inc(kv_done, 1)

            def cross_q(b):
                pe.wait_ge(x1_hi_ready, b + 1)
                pe.wait_ge(x1_lo_ready, b + 1)
                if isinstance(b, int) and b == 0:
                    pe.wait_ge(y1_ready, B)
                else:
                    pe.wait_ge(y2_ready, b)
                split_product(out_a[:], wq_hi[:], wq_lo[:], x1_hi[:], x1_lo[:], True, True).then_inc(xq_done, 1)

            def cross_score(b, p, t):
                if t == 0:
                    pe.wait_ge(xq_lo_ready, b + 1)
                    pe.wait_ge(keys_lo_ready, b + 1)
                if isinstance(b, int) and b == 0 and t < 2:
                    pe.wait_ge(exp_done, 8 * B)
                else:
                    pe.wait_ge(xsub_done, 4 * b + t - 1)
                n = slice(128 * t, 128 * t + 128)
                split_product(score[t % 2][:], xq_hi[:, n], xq_lo[:, n], keys_hi[p][:], keys_lo[p][:], True, True).then_inc(xscore_done, 1)

            def turn_xprob(b, t):
                pe.wait_ge(xprob_ready, 4 * b + t + 1)
                if not (isinstance(b, int) and b == 0 and t < 2):
                    pe.wait_ge(xprobT_ready, 4 * b + t - 1)
                    if t == 0:
                        pe.wait_ge(x2T_lo_ready, b)
                for j in range(XH // HPT):
                    m = pe.transpose(turn[t % 2][:, 128 * j:128 * j + 128], xprob[t % 2][:, HPT * j:HPT * (j + 1)].rearrange("n h k -> n (h k)"), ident[:])
                m.then_inc(xprob_turned, 1)

            def cross_pv(b, p):
                pe.wait_ge(xprobT_ready, 4 * b + 4)
                pe.wait_ge(values_ready, b + 1)
                if isinstance(b, int) and b == 0:
                    pe.wait_ge(attn_normed, 2 * B)
                else:
                    pe.wait_ge(xo_lo_ready, b)
                for j in range(XH // HPT):
                    m = pe.matmul(out_b[32 * j:32 * j + 32, :], values[p][:, j].rearrange("k h d -> k (h d)"), xprobT[:, j], start=True, stop=True)
                m.then_inc(xpv_done, 1)

            def cross_m(b):
                pe.wait_ge(xo_lo_ready, b + 1)
                split_product(out_a[:], wm_hi[:], wm_lo[:], xo_hi[:], xo_lo[:], True, True).then_inc(wm_done, 1)

            def turn_x2(b):
                pe.wait_ge(x2s_ready, b + 1)
                pe.wait_ge(xprobT_ready, 4 * b + 4)
                for c in range(KC):
                    m = pe.transpose(turn[0][:, 128 * c:128 * c + 128], x2s[:, 128 * c:128 * c + 128], ident[:])
                m.then_inc(x2_turned, 1)

            pe.wait_ge(cross_in, 16 * 11)
            pe.wait_ge(cross_lo, 2)
            pe.wait_ge(cross_masks, 1)
            pe.wait_ge(oT_lo_ready, B)
            pe.wait_ge(rope_read, B)
            pe.wait_ge(v_ready, B)
            for c in range(KC):
                m = pe.matmul(qkv_ps[0:1, 0:2 * XK], ones_col[:], proj[:, c], start=(c == 0), stop=(c == KC - 1))
            m.then_inc(proj_summed, 1)
            pe.wait_ge(proj_sums, 2)

            def cross_step(b, p):
                context(b, p)
                cross_q(b)
                keys_values(b)
                for t in range(5):
                    if t < 4:
                        cross_score(b, p, t)
                    if t > 0:
                        turn_xprob(b, t - 1)
                cross_pv(b, p)
                cross_m(b)
                turn_x2(b)

            def logits(half):
                pe.wait_ge(x2T_lo_ready, HB * (half + 1))
                pe.wait_ge(ctx_copied, 2 * HB * (half + 1))
                if half == 0:
                    pe.wait_ge(gate_lo_ready, 1)
                for c in range(KC):
                    last = split_product(qkv_ps[0:NE, 0:HB * 128], gate_hi[:, c], gate_lo[:, c],
                                         x2T_hi[:, c].rearrange("f b s -> f (b s)"), x2T_lo[:, c].rearrange("f b s -> f (b s)"), c == 0, c == KC - 1)
                last.then_inc(logits_done, 1)

            def turn_logits(half):
                pe.wait_ge(logitT_ready, half + 1)
                for k in range(HB):
                    m = pe.transpose(qkv_ps[:, NE * k:NE * (k + 1)], logitT[:, 128 * k:128 * (k + 1)], ident[0:NE, 0:NE])
                m.then_inc(logits_turned, 1)

            def ranks(half):
                pe.wait_ge(chosen_ready, half + 1)
                pe.wait_ge(tri_ready, 2)
                b0 = HB * half
                dst = qkv_ps[:, 0:HB * NE]
                pe.matmul(dst, tri_bf[:], chosen_bf[:].rearrange("t b e -> t (b e)"), start=True, stop=False)
                m = pe.matmul(dst, ones_bf[:], before_bf[:, b0:b0 + HB].rearrange("t b e -> t (b e)"), start=False, stop=True)
                if half == 1:
                    m = pe.matmul(qkv_ps[:, 512:512 + NE], ones_bf[:], before_bf[:, B], start=True, stop=True)
                m.then_inc(ranks_done, 1)

            def shared_gate_up(half, f):
                for j, (bank_, first_) in enumerate(((score[f], sh_gate_done), (turn[f], sh_up_done))):
                    for c in range(KC):
                        w = slice(FF * j + 128 * f, FF * j + 128 * (f + 1))
                        last = split_product(bank_[:], w_hi[:, 1, c, w], w_lo[:, 1, c, w],
                                             x2T_hi[:, c].rearrange("f b s -> f (b s)"), x2T_lo[:, c].rearrange("f b s -> f (b s)"), c == 0, c == KC - 1)
                    last.then_inc(first_, 1)

            def shared_down(half, k):
                n = HB * half + k
                if n == 0:
                    pe.wait_ge(y2_ready, HB)
                    pe.wait_ge(xo_lo_ready, HB)
                elif k < 2:
                    pe.wait_ge(y2_ready, HB * (half + 1))
                    pe.wait_ge(xo_lo_ready, HB * (half + 1))
                else:
                    pe.wait_ge(base_ready, n - 1)
                for f in range(FC):
                    t_ = slice(128 * k, 128 * (k + 1))
                    last = split_product((out_a, out_b)[k % 2][:], shT_hi[:, f, t_], shT_lo[:, f, t_], w_hi[:, 1, KC + f], w_lo[:, 1, KC + f], f == 0, f == FC - 1)
                last.then_inc(sh_down_done, 1)

            for half in (0, 1):
                cross_step(4 * half, 0)
                cross_step(4 * half + 1, 1)
                cross_step(4 * half + 2, 0)
                cross_step(4 * half + 3, 1)
                logits(half)
                pe.wait_ge(sh_lo_ready, WCH)
                pe.wait_ge(xsub_done, 4 * HB * (half + 1))
                shared_gate_up(half, 0)
                turn_logits(half)
                shared_gate_up(half, 1)
                ranks(half)
                pe.wait_ge(shT_lo_ready, FC * (half + 1))
                for k in range(HB):
                    shared_down(half, k)

            def turn_slot(t, q):
                pe.wait_ge(xs_loaded[q], 8 * (t - q) + 16)
                if isinstance(t, int) and t == 0:
                    pe.wait_ge(sh_z_ready, 2 * FC)
                else:
                    pe.wait_ge(xs_lo_ready, t)
                for c in range(KC):
                    m = pe.transpose(turn[0][:, 128 * c:128 * (c + 1)], xs_in[q][:, 128 * c:128 * (c + 1)], ident[:])
                m.then_inc(xs_turned, 1)

            def slot_gate_up(t, q):
                e = pe.value_load(tab[0:1, 0, bass.ds(t, 1)], min_val=0, max_val=NE - 1)
                buf = pe.value_load(tab[0:1, 1, bass.ds(t, 1)], min_val=0, max_val=1)
                pe.wait_ge(w_lo_ready, e * WCH + WCH)
                pe.wait_ge(xs_lo_ready, t + 1)
                if not isinstance(t, int) or t > 1:
                    pe.wait_ge(z_ready, t - 1)
                for c in range(KC):
                    last = split_product(score[q][:], xsT_hi[q][:, c], xsT_lo[q][:, c],
                                         w_hi[:, bass.ds(buf, 1), c].rearrange("k o n -> k (o n)"),
                                         w_lo[:, bass.ds(buf, 1), c].rearrange("k o n -> k (o n)"), c == 0, c == KC - 1)
                last.then_inc(gate_up_done, 1)

            def turn_z(t):
                pe.wait_ge(z_ready, t + 1)
                if not isinstance(t, int) or t > 0:
                    pe.wait_ge(zT_lo_ready, t)
                for f in range(FC):
                    m = pe.transpose(turn[1][:, 128 * f:128 * (f + 1)], z[:, 128 * f:128 * (f + 1)], ident[:])
                m.then_inc(z_turned, 1)

            def slot_down(t, q):
                buf = pe.value_load(tab[0:1, 1, bass.ds(t, 1)], min_val=0, max_val=1)
                pe.wait_ge(zT_lo_ready, t + 1)
                if isinstance(t, int) and t < 2:
                    pe.wait_ge(base_ready, B)
                else:
                    pe.wait_ge(y_copied, t - 1)
                for f in range(FC):
                    last = split_product((out_a, out_b)[q][:], zT_hi[:, f], zT_lo[:, f],
                                         w_hi[:, bass.ds(buf, 1), KC + f].rearrange("k o n -> k (o n)"),
                                         w_lo[:, bass.ds(buf, 1), KC + f].rearrange("k o n -> k (o n)"), f == 0, f == FC - 1)
                last.then_inc(slot_done, 1)

            pe.wait_ge(tables_ready, 1)
            turn_slot(0, 0)

            def step(t, q):
                slot_gate_up(t, q)
                if not isinstance(t, int) or t < SLOTS - 1:
                    turn_slot(t + 1, 1 - q)
                if not isinstance(t, int) or t > 0:
                    slot_down(t - 1, 1 - q)
                turn_z(t)

            step(0, 0)
            step(1, 1)
            step(2, 0)
            with pe.Fori(1, (SLOTS - 3) // 2) as i:
                step(i * 2 + 1, 1)
                step(i * 2 + 2, 0)
            step(SLOTS - 2, 1)
            step(SLOTS - 1, 0)
            slot_down(SLOTS - 1, 0)

        @block.vector
        def _(dve):
            dve.memset(stack[:].bitcast(F32)[:, 0:NQ, 3, :], 0.0)
            dve.memset(stack[:].bitcast(F32)[:, NQ:, 3, 2:], 0.0)
            dve.memset(neg_max_parts[:].bitcast(F32)[:, 2:4], 0.0)
            dve.memset(stack[:].bitcast(F32)[:, NQ:, 3, 0:2], 1.0).then_inc(consts_ready, 1)
            for p in (0, 1):
                dve.memset(v_ones[p][:, :, HD:HD + 1], 1.0)
                dve.memset(v_ones[p][:, :, HD + 1:], 0.0)
            dve.memset(eps[:], EPS)
            dve.memset(neg_half[:], -0.5).then_inc(consts_ready, 1)
            dve.wait_ge(consts_in, 48)
            dve.tensor_copy(ident_bf[:], ident[:]).then_inc(consts_ready, 1)
            dve.tensor_copy(causal_bf[:], causal[:].rearrange("s (o t) -> s o t", o=1).to_broadcast([128, REP, 128])).then_inc(consts_ready, 1)

            def x_lo(b, p):
                dve.wait_ge(xT_hi_ready, b + 1)
                if not isinstance(b, int) or b > 1:
                    dve.wait_ge(qkv_done, b - 1)
                dve.tensor_tensor(xT_lo[p][:], xT[:, p], xT_hi[p][:].bitcast(F32), ALU.subtract).then_inc(xT_lo_ready, 1)

            def rope_products(b, p):
                dve.wait_ge(qkv_done, b + 1)
                if not isinstance(b, int) or b > 0:
                    dve.wait_ge(rot_ready, 2 * b)
                qk = qkv_ps[:, 0:QK_HEADS * HD].rearrange("s (h e) -> s h e", e=HD)
                for j, dst in ((0, rope_cos), (1, rope_sin)):
                    f = rope[:, j:j + 1].to_broadcast([128, QK_HEADS, HD])
                    m = dve.tensor_tensor(dst[:].rearrange("s h a e -> s h (a e)"), qk, f, ALU.mult)
                m.then_inc(rope_read, 1)

            def low_parts(b):
                dve.wait_ge(stack_hi, 2 * b + 2)
                dve.tensor_tensor(stack[:, 0:NQ, 2], rotated[:, 0:NQ], stack[:, 0:NQ, 0].bitcast(F32), ALU.subtract).then_inc(stack_lo, 1)
                dve.tensor_tensor(stack[:, NQ:, 1], rotated[:, NQ:], stack[:, NQ:, 0].bitcast(F32), ALU.subtract).then_inc(stack_lo, 1)

            def qkT_copies(b, p):
                for r in (1, 3):
                    dve.wait_ge(qkT_turned, 5 * b + r + 1)
                    dve.tensor_copy(qT[p][:, 4 * r:4 * r + 4].rearrange("k r s -> k (r s)"), turn[1][:]).then_inc(qkT_by_dve, 1)
                dve.wait_ge(qkT_by_act, 3 * b + 3)
                dve.wait_ge(qkT_by_dve, 2 * b + 2)
                dve.tensor_copy(qT_half[:], qT[p][:].bitcast(F32)).then_inc(halves_ready, 1)
                dve.tensor_copy(kT_half[:], kT[p][:].bitcast(F32)).then_inc(halves_ready, 1)

            def maxima(b):
                for g in range(NKV):
                    dve.wait_ge(pass1_done, 8 * b + g + 1)
                    dve.tensor_reduce(neg_max[:, g], score[g % 2][:].rearrange("s (r t) -> s r t", r=REP), AX.X, ALU.max,
                                      negate=True).then_inc(max_done, 1)
                dve.wait_ge(max_done, 8 * b + 8)
                nm = neg_max[:].rearrange("s (u a) r -> s a u r", a=2)
                dve.tensor_copy(neg_max_parts[:, 0:2, 0], nm).then_inc(max_hi, 1)
                dve.wait_ge(max_hi, b + 1)
                dve.tensor_tensor(neg_max_parts[:, 0:2, 1], nm, neg_max_parts[:, 0:2, 0].bitcast(F32), ALU.subtract).then_inc(max_parts, 1)

            def normalise(b, half):
                src = (out_a, out_b)[half][:].rearrange("s (r j e) -> s r j e", r=REP, e=32)
                rs = attn_rsum[:, half]
                dve.wait_ge(pv_turned, 2 * b + half + 1)
                dve.reciprocal(rs, src[:, :, :, HD]).then_inc(rsum_ready, 1)
                dve.wait_ge(rsum_ready, 2 * b + half + 1)
                if not isinstance(b, int) or b > 0:
                    dve.wait_ge(oT_turned, b)
                dst = attn_out[:, half].rearrange("s (j r) e -> s r j e", r=REP)
                dve.tensor_tensor(dst, src[:, :, :, 0:HD], rs.rearrange("s r (j o) -> s r j o", o=1).to_broadcast([128, REP, 4, HD]),
                                  ALU.mult).then_inc(attn_normed, 1)

            def o_lo(b):
                dve.wait_ge(oT_hi_ready, b + 1)
                if not isinstance(b, int) or b > 0:
                    dve.wait_ge(wo_done, b)
                dve.tensor_tensor(oT_lo[:].rearrange("k c s -> k (c s)"), turn[1][:], oT_hi[:].rearrange("k c s -> k (c s)").bitcast(F32),
                                  ALU.subtract).then_inc(oT_lo_ready, 1)

            def residual1(b, p):
                dve.wait_ge(wo_done, b + 1)
                dve.wait_ge(x_loaded[p], 8 * (b - p) + 16)
                dve.tensor_tensor(y1[:], out_a[:], x_in[:, p], ALU.add).then_inc(y1_ready, 1)
                dve.wait_ge(y1_ready, b + 1)
                dve.bn_stats(bn6[:], y1[:]).then_inc(stats1, 1)
                dve.wait_ge(stats1, b + 1)
                dve.sem_inc(passed)
                dve.bn_aggr(mean_var[:], bn6[:]).then_inc(mv1, 1)

            def x1_write(b):
                dve.wait_ge(rstd1, b + 1)
                dve.wait_ge(mv1, b + 1)
                dve.tensor_scalar(x1[:, bass.ds(b, 1)].rearrange("s o d -> s (o d)"), y1[:], mean_var[:, 0:1], rstd[:, 0:1],
                                  ALU.subtract, ALU.mult).then_inc(x1_ready, 1)

            x_lo(0, 0)
            for c in range(KC):
                dve.wait_ge(wqkv_hi_ready, c + 1)
                dve.tensor_tensor(wqkv_lo[:, c], wst[:, c], wqkv_hi[:, c].bitcast(F32), ALU.subtract).then_inc(wqkv_lo_ready, 1)
            x_lo(1, 1)
            dve.wait_ge(wo_hi_ready, 1)
            dve.tensor_tensor(wo_lo[:], wo_in[:], wo_hi[:].bitcast(F32), ALU.subtract).then_inc(wo_lo_ready, 1)
            rope_products(0, 0)
            low_parts(0)
            qkT_copies(0, 0)

            def step(b, p):
                first, final = isinstance(b, int) and b == 0, isinstance(b, int) and b == B - 1
                maxima(b)
                if not first:
                    residual1(b - 1, 1 - p)
                if not final:
                    rope_products(b + 1, 1 - p)
                if not first:
                    x1_write(b - 1)
                if not final:
                    low_parts(b + 1)
                normalise(b, 0)
                normalise(b, 1)
                if not final:
                    qkT_copies(b + 1, 1 - p)
                o_lo(b)
                if not (isinstance(b, int) and b >= B - 2):
                    x_lo(b + 2, p)

            step(0, 0)
            with dve.Fori(0, (B - 4) // 2) as i:
                step(i * 2 + 1, 1)
                step(i * 2 + 2, 0)
            step(B - 3, 1)
            step(B - 2, 0)
            step(B - 1, 1)
            residual1(B - 1, 1)
            x1_write(B - 1)

            dve.wait_ge(wo_done, B)
            dve.wait_ge(max_rows, 64 * B)
            dve.memset(ones_col[:], 1.0).then_inc(cross_masks, 1)
            for j, (w, hi, lo) in enumerate(((wq_in, wq_hi, wq_lo), (wm_in, wm_hi, wm_lo))):
                dve.wait_ge(cross_hi, j + 1)
                dve.tensor_tensor(lo[:], w[:], hi[:].bitcast(F32), ALU.subtract).then_inc(cross_lo, 1)

            def head_keys(b, p):
                dve.wait_ge(kv_done, b + 1)
                if not isinstance(b, int) or b > 0:
                    dve.wait_ge(keys_lo_ready, b)
                    dve.wait_ge(keys_hi_ready, b)
                k = qkv_ps[:, 512:512 + XK].rearrange("c (o k) -> c o k", o=1).to_broadcast([128, XH, XK])
                dve.tensor_tensor(keys[:], k, head_mask[:].rearrange("c (h o) -> c h o", o=1).to_broadcast([128, XH, XK]), ALU.mult).then_inc(keys_ready, 1)
                if not isinstance(b, int) or b > 1:
                    dve.wait_ge(xpv_done, b - 1)
                v = qkv_ps[:, 640:768].rearrange("k (j h d) -> k j h d", j=XH // HPT, h=HPT)
                vm = value_mask[:].rearrange("k (a h d) -> k a h d", a=1, d=1).to_broadcast([128, XH // HPT, HPT, XD])
                dve.tensor_tensor(values[p][:], v, vm, ALU.mult).then_inc(values_ready, 1)
                dve.wait_ge(keys_hi_ready, b + 1)
                dve.tensor_tensor(keys_lo[p][:], keys[:].rearrange("c h k -> c (h k)"), keys_hi[p][:].bitcast(F32), ALU.subtract).then_inc(keys_lo_ready, 1)

            def x1_low(b):
                dve.wait_ge(x1_hi_ready, b + 1)
                dve.tensor_tensor(x1_lo[:], x1[:, bass.ds(b, 1)].rearrange("s o d -> s (o d)"), x1_hi[:].bitcast(F32), ALU.subtract).then_inc(x1_lo_ready, 1)

            def xq_low(b):
                dve.wait_ge(xq_hi_ready, b + 1)
                dve.scalar_tensor_tensor(out=xq_lo[:], in0=out_a[:], scalar=bias_q[:, 0:1], in1=xq_hi[:].bitcast(F32), op0=ALU.add, op1=ALU.subtract).then_inc(xq_lo_ready, 1)

            def xmax_sub(b, t):
                dve.wait_ge(xscore_done, 4 * b + t + 1)
                sc = score[t % 2][:].rearrange("n (h k) -> n h k", k=XK)
                dve.tensor_reduce(xmax[:, t % 2], sc, AX.X, ALU.max).then_inc(xmax_ready, 1)
                dve.wait_ge(xmax_ready, 4 * b + t + 1)
                if not (isinstance(b, int) and b == 0 and t < 2):
                    dve.wait_ge(xprob_turned, 4 * b + t - 1)
                dve.tensor_tensor(xprob[t % 2][:], sc, xmax[:, t % 2].rearrange("n (h o) -> n h o", o=1).to_broadcast([128, XH, XK]), ALU.subtract).then_inc(xsub_done, 1)

            def xsum_rec(b, t):
                dve.wait_ge(xexp_done, 4 * b + t + 1)
                if not (isinstance(b, int) and b == 0 and t < 2):
                    dve.wait_ge(xprob_ready, 4 * b + t - 1)
                dve.tensor_reduce(xsum[:, t % 2], xprob[t % 2][:], AX.X, ALU.add).then_inc(xsum_ready, 1)
                dve.wait_ge(xsum_ready, 4 * b + t + 1)
                dve.reciprocal(xrec[:, t % 2], xsum[:, t % 2]).then_inc(xrec_ready, 1)

            def xo_low(b):
                dve.wait_ge(xo_hi_ready, b + 1)
                dve.tensor_tensor(xo_lo[:], out_b[:], xo_hi[:].bitcast(F32), ALU.subtract).then_inc(xo_lo_ready, 1)

            def residual2(b):
                dve.wait_ge(wm_done, b + 1)
                if not isinstance(b, int) or b > 0:
                    dve.wait_ge(x2s_ready, b)
                dve.scalar_tensor_tensor(out=y2[:], in0=out_a[:], scalar=bias_m[:, 0:1], in1=x1[:, bass.ds(b, 1)].rearrange("s o d -> s (o d)"),
                                         op0=ALU.add, op1=ALU.add).then_inc(y2_ready, 1)
                dve.wait_ge(y2_ready, b + 1)
                dve.bn_stats(bn6b[:], y2[:]).then_inc(stats2, 1)
                dve.wait_ge(stats2, b + 1)
                dve.sem_inc(passed)
                dve.bn_aggr(mean_var2[:], bn6b[:]).then_inc(mv2, 1)
                dve.wait_ge(rstd2_ready, b + 1)
                dve.wait_ge(mv2, b + 1)
                if not isinstance(b, int) or b > 0:
                    dve.wait_ge(x2_turned, b)
                    dve.wait_ge(x2_ready, b)
                dve.tensor_scalar(x2s[:], y2[:], mean_var2[:, 0:1], rstd2[:, 0:1], ALU.subtract, ALU.mult).then_inc(x2s_ready, 1)

            def x2T_low(b):
                dve.wait_ge(x2T_hi_ready, b + 1)
                q = b % (B // 2) if isinstance(b, int) else b
                dve.tensor_tensor(x2T_lo[:, :, q], turn[0][:].rearrange("f (c s) -> f c s", c=KC), x2T_hi[:, :, q].bitcast(F32), ALU.subtract).then_inc(x2T_lo_ready, 1)

            dve.wait_ge(cross_in, 16 * 11)

            def cross_step(b, p):
                x1_low(b)
                xq_low(b)
                head_keys(b, p)
                for t in range(5):
                    if t < 4:
                        xmax_sub(b, t)
                    if t > 0:
                        xsum_rec(b, t - 1)
                xo_low(b)
                residual2(b)
                x2T_low(b)

            routed = [0]

            def link(ins):
                routed[0] += 1
                ins.then_inc(route, 1)
                dve.wait_ge(route, routed[0])

            def wide(ap, n):
                return ap.rearrange("t (b o) -> t b o", o=1).to_broadcast([128, HB, n])

            def choose(half):
                bs = slice(HB * half, HB * (half + 1))
                dve.wait_ge(logit_exp, half + 1)
                link(dve.tensor_scalar(e_score[:], e_score[:], 1.0, None, ALU.add))
                link(dve.reciprocal(e_score[:], e_score[:]))
                link(dve.tensor_tensor(e_score[:], e_score[:], bias_e[:].rearrange("t (o e) -> t o e", o=1).to_broadcast([128, HB, NE]), ALU.add))
                for j in range(TOPK):
                    best, one = weight[:, j, bs], picked[:, j, bs]
                    link(dve.tensor_reduce(best, e_score[:], AX.X, ALU.max))
                    link(dve.tensor_tensor(e_eq[:], e_score[:], wide(best, NE), ALU.is_equal))
                    io = iota16[:].rearrange("t (o e) -> t o e", o=1).to_broadcast([128, HB, NE])
                    link(dve.tensor_tensor(e_eq[:], e_eq[:], io, ALU.mult))
                    link(dve.tensor_reduce(e_low[:], e_eq[:], AX.X, ALU.min))
                    link(dve.tensor_tensor(one, io, wide(e_low[:], NE), ALU.is_equal))
                    link(dve.scalar_tensor_tensor(out=e_score[:], in0=one, scalar=MASKED, in1=e_score[:], op0=ALU.mult, op1=ALU.add))
                link(dve.tensor_scalar(chosen[:], e_score[:], MASKED / 10, None, ALU.is_lt))
                link(dve.tensor_copy(chosen_bf[:], chosen[:]))
                for k in range(HB):
                    b = HB * half + k
                    link(dve.tensor_tensor(before[:, b + 1], before[:, b], chosen[:, k], ALU.add))
                m = dve.tensor_copy(before_bf[:, HB * half:HB * (half + 1) + 1], before[:, HB * half:HB * (half + 1) + 1])
                m.then_inc(chosen_ready, 1)
                link(dve.tensor_reduce(w_sum[:], weight[:, :, bs].rearrange("t j b -> t b j"), AX.X, ALU.add))
                link(dve.tensor_scalar(w_sum[:], w_sum[:], 1e-20, None, ALU.add))
                link(dve.reciprocal(w_rec[:], w_sum[:]))
                link(dve.tensor_tensor(weight[:, :, bs], weight[:, :, bs], w_rec[:].rearrange("t (o b) -> t o b", o=1).to_broadcast([128, TOPK, HB]), ALU.mult))

            def place_rows(half):
                bs = slice(HB * half, HB * (half + 1))
                dve.wait_ge(ranks_done, half + 1)
                m = dve.tensor_copy(rank[:, bs], qkv_ps[:, 0:HB * NE].rearrange("t (b e) -> t b e", e=NE))
                link(m)
                if half == 1:
                    link(dve.tensor_copy(count[:], qkv_ps[:, 512:512 + NE]))
                link(dve.tensor_tensor(place[:, bs], rank[:, bs], region[:].rearrange("t (o e) -> t o e", o=1).to_broadcast([128, HB, NE]), ALU.add))
                for j in range(TOPK):
                    link(dve.tensor_tensor(picked_place[:, j, bs], picked[:, j, bs], place[:, bs], ALU.mult))
                link(dve.tensor_reduce(row_f[:, :, bs], picked_place[:, :, bs], AX.X, ALU.add))
                dve.tensor_copy(row_of[:, :, bs], row_f[:, :, bs]).then_inc(rows_ready, 1)

            def slot_tables():
                cb = count[:].rearrange("t (e o) -> t e o", o=1).to_broadcast([128, NE, 8])
                link(dve.tensor_tensor(over[:], cb, thresholds[:].rearrange("t (o k) -> t o k", o=1).to_broadcast([128, NE, 8]), ALU.is_gt))
                link(dve.tensor_reduce(n_slots[:], over[:], AX.X, ALU.add))
                nb = n_slots[:].rearrange("t (o e) -> t o e", o=1)
                link(dve.tensor_tensor(prod[:], nb.to_broadcast([128, NE, NE]), upto_mask[:], ALU.mult))
                link(dve.tensor_reduce(slots_to[:], prod[:], AX.X, ALU.add))
                link(dve.tensor_tensor(slot_base[:], slots_to[:], n_slots[:], ALU.subtract))
                sn = slot_no[:].rearrange("t (s o) -> t s o", o=1).to_broadcast([1, SLOTS, NE])
                link(dve.tensor_tensor(passed_e[:], slots_to[0:1].rearrange("t (o e) -> t o e", o=1).to_broadcast([1, SLOTS, NE]), sn, ALU.is_le))
                f = tab_f
                link(dve.memset(f[:], -1.0))
                link(dve.tensor_reduce(f[:, 0, 1:], passed_e[:, :, 0:NE - 1], AX.X, ALU.add))
                link(dve.tensor_reduce(f[:, 1, 1:], passed_e[:], AX.X, ALU.add))
                link(dve.tensor_reduce(f[:, 2, 1:], passed_e[:, :, 0:NE - 2], AX.X, ALU.add))
                link(dve.tensor_tensor(passed_w[:], passed_e[:], alternate[:].rearrange("t (o e) -> t o e", o=1).to_broadcast([1, SLOTS, NE]), ALU.mult))
                link(dve.tensor_reduce(f[:, 3, 1:], passed_w[:], AX.X, ALU.add))
                link(dve.tensor_tensor(passed_w[:], passed_e[:], nb[0:1].to_broadcast([1, SLOTS, NE]), ALU.mult))
                link(dve.tensor_reduce(f[:, 4, 1:], passed_w[:], AX.X, ALU.add))
                link(dve.tensor_tensor(f[:, 4, 1:], slot_no[:], f[:, 4, 1:], ALU.subtract))
                link(dve.tensor_scalar(f[:, 4, 1:], f[:, 4, 1:], float(SLOT), None, ALU.mult))
                link(dve.scalar_tensor_tensor(out=f[:, 5, 1:], in0=f[:, 1, 1:], scalar=float(REGION), in1=f[:, 4, 1:], op0=ALU.mult, op1=ALU.add))
                link(dve.tensor_tensor(f[:, 4, 1:], f[:, 2, 1:], f[:, 2, 0:SLOTS], ALU.subtract))
                link(dve.tensor_tensor(pad_f[:], count[0:1], region[0:1], ALU.add))
                dve.tensor_copy(tab[:, 0], f[:, 0, 1:])
                dve.tensor_copy(tab[:, 1], f[:, 3, 1:])
                dve.tensor_scalar(tab[:, 2], f[:, 5, 1:], float(IDLE_ROW), None, ALU.min)
                dve.tensor_copy(tab[:, 3], f[:, 4, 1:])
                dve.tensor_copy(pad_row[:], pad_f[:]).then_inc(tables_ready, 1)

            def result_rows():
                link(dve.tensor_scalar(slot_base[:], slot_base[:], float(SLOT), None, ALU.mult))
                link(dve.tensor_tensor(place[:], rank[:], slot_base[:].rearrange("t (o e) -> t o e", o=1).to_broadcast([128, B, NE]), ALU.add))
                for j in range(TOPK):
                    link(dve.tensor_tensor(picked_place[:, j], picked[:, j], place[:], ALU.mult))
                link(dve.tensor_reduce(row_f[:], picked_place[:], AX.X, ALU.add))
                dve.tensor_copy(yrow_of[:], row_f[:]).then_inc(yrows_ready, 1)

            def split_low(buf, hi_sem, lo_sem, have, chunks=range(WCH)):
                for c in chunks:
                    dve.wait_ge(hi_sem, have + c + 1)
                    dve.sem_inc(passed)
                    raw, hi, lo = (w[:, bass.ds(buf, 1), c].rearrange("k o n -> k (o n)") for w in (w_raw, w_hi, w_lo))
                    dve.tensor_tensor(lo, raw, hi.bitcast(F32), ALU.subtract).then_inc(lo_sem, 1)

            def shared_z(half, f):
                n = FC * half + f
                dve.wait_ge(sh_silu_done, n + 1)
                dve.wait_ge(sh_up_done, n + 1)
                if n > 0:
                    dve.wait_ge(shT_lo_ready, n)
                    dve.wait_ge(shT_hi_ready, n)
                dve.tensor_tensor(sh_z[:], turn[f][:], sh_silu[:], ALU.mult).then_inc(sh_z_ready, 1)
                dve.wait_ge(shT_hi_ready, n + 1)
                dve.tensor_tensor(shT_lo[:, f], sh_z[:], shT_hi[:, f].bitcast(F32), ALU.subtract).then_inc(shT_lo_ready, 1)

            def shared_base(half, k):
                b = HB * half + k
                dve.wait_ge(sh_down_done, b + 1)
                dve.wait_ge(x2_ready, b + 1)
                dve.tensor_tensor(base[:, b], (out_a, out_b)[k % 2][:], x2[:, b], ALU.add).then_inc(base_ready, 1)

            dve.memset(before[:, 0], 0.0)
            dve.memset(ones_bf[:], 1.0).then_inc(tri_ready, 1)
            dve.memset(zeros[:], 0.0).then_inc(zeros_ready, 1)
            dve.wait_ge(moe_in, 16 * 9)
            dve.tensor_copy(tri_bf[:], tri[:]).then_inc(tri_ready, 1)
            dve.wait_ge(gate_hi_ready, 1)
            dve.tensor_tensor(gate_lo[:], gate_in[:], gate_hi[:].bitcast(F32), ALU.subtract).then_inc(gate_lo_ready, 1)

            for half in (0, 1):
                for k in range(HB):
                    cross_step(HB * half + k, k % 2)
                    if k < WCH // 2:
                        split_low(1 - half, (sh_hi_ready, w_hi_ready)[half], (sh_lo_ready, w_lo_ready)[half], 0, range(2 * k, 2 * k + 2))
                dve.wait_ge(logits_done, half + 1)
                if half == 1:
                    dve.wait_ge(logits_turned, 1)
                dve.tensor_copy(logitT[:], qkv_ps[0:NE, 0:HB * 128]).then_inc(logitT_ready, 1)
                shared_z(half, 0)
                choose(half)
                shared_z(half, 1)
                place_rows(half)
                if half == 1:
                    slot_tables()
                for k in range(HB):
                    shared_base(half, k)
            result_rows()

            def slot_x_low(t, q):
                dve.wait_ge(xs_hi_ready, t + 1)
                if not isinstance(t, int) or t > 1:
                    dve.wait_ge(gate_up_done, t - 1)
                dve.tensor_tensor(xsT_lo[q][:].rearrange("f c s -> f (c s)"), turn[0][:], xsT_hi[q][:].rearrange("f c s -> f (c s)").bitcast(F32),
                                  ALU.subtract).then_inc(xs_lo_ready, 1)

            def slot_z(t, q):
                dve.wait_ge(silu_done, t + 1)
                if not isinstance(t, int) or t > 0:
                    dve.wait_ge(z_turned, t)
                dve.tensor_tensor(z[:], silu_g[:], score[q][:, FF:2 * FF], ALU.mult).then_inc(z_ready, 1)

            def slot_z_low(t):
                dve.wait_ge(zT_hi_ready, t + 1)
                if not isinstance(t, int) or t > 0:
                    dve.wait_ge(slot_done, t)
                dve.tensor_tensor(zT_lo[:].rearrange("f c s -> f (c s)"), turn[1][:, 0:FF], zT_hi[:].rearrange("f c s -> f (c s)").bitcast(F32),
                                  ALU.subtract).then_inc(zT_lo_ready, 1)

            def next_expert_low(t):
                first = dve.value_load(tab[0:1, 3, bass.ds(t, 1)], min_val=0, max_val=1)
                with dve.If(first > 0):
                    e = dve.value_load(tab[0:1, 0, bass.ds(t, 1)], min_val=0, max_val=NE - 2)
                    buf = dve.value_load(tab[0:1, 1, bass.ds(t, 1)], min_val=0, max_val=1)
                    split_low(1 - buf, w_hi_ready, w_lo_ready, (e + 1) * WCH)

            slot_x_low(0, 0)

            def step(t, q):
                slot_z(t, q)
                if not isinstance(t, int) or t < SLOTS - 1:
                    slot_x_low(t + 1, 1 - q)
                slot_z_low(t)
                next_expert_low(t)

            step(0, 0)
            with dve.Fori(0, (SLOTS - 3) // 2) as i:
                step(i * 2 + 1, 1)
                step(i * 2 + 2, 0)
            step(SLOTS - 2, 1)
            step(SLOTS - 1, 0)

            def combine(b, p):
                dve.wait_ge(gathered_in[p], 32 * (b - p) + 64)
                if not isinstance(b, int) or b > 0:
                    dve.wait_ge(out_ready, b)
                for j in range(TOPK):
                    src = base[:, bass.ds(b, 1)].rearrange("s o d -> s (o d)") if j == 0 else y3
                    dve.scalar_tensor_tensor(out=y3, in0=gathered[p][:, j], scalar=weight[:, j, bass.ds(b, 1)], in1=src,
                                             op0=ALU.mult, op1=ALU.add).then_inc(combined, 1)
                    dve.wait_ge(combined, b * TOPK + j + 1)
                dve.bn_stats(bn6c[:], y3).then_inc(stats3, 1)
                dve.wait_ge(stats3, b + 1)
                dve.sem_inc(passed)
                dve.bn_aggr(mean_var3[:], bn6c[:]).then_inc(mv3, 1)
                dve.wait_ge(rstd3_ready, b + 1)
                dve.wait_ge(mv3, b + 1)
                if not isinstance(b, int) or b > 1:
                    dve.wait_ge(out_in[p], 8 * (b - p))
                dve.tensor_scalar(out_sb[p], y3, mean_var3[:, 0:1], rstd3[:, 0:1], ALU.subtract, ALU.mult).then_inc(out_ready, 1)

            combine(0, 0)
            with dve.Fori(0, (B - 2) // 2) as i:
                combine(i * 2 + 1, 1)
                combine(i * 2 + 2, 0)
            combine(B - 1, 1)

        @block.scalar
        def _(act):
            def x_hi(b, p):
                act.wait_ge(xT_in[p], 8 * (b - p) + 16)
                if not isinstance(b, int) or b > 1:
                    act.wait_ge(qkv_done, b - 1)
                act.copy(xT_hi[p][:], xT[:, p]).then_inc(xT_hi_ready, 1)

            def v_copy(b, p):
                act.wait_ge(rope_read, b + 1)
                if not isinstance(b, int) or b > 1:
                    act.wait_ge(pv_done, 8 * b - 8)
                act.copy(v_ones[p][:, :, 0:HD], qkv_ps[:, QK_HEADS * HD:QKV].rearrange("s (g e) -> s g e", e=HD)).then_inc(v_ready, 1)

            def high_parts(b):
                act.wait_ge(rot_ready, 2 * b + 2)
                if not isinstance(b, int) or b > 0:
                    act.wait_ge(qkT_turned, 5 * b)
                r = rotated[:].rearrange("s h (o e) -> s h o e", o=1)
                act.copy(stack[:, 0:NQ, 0:2], r[:, 0:NQ].to_broadcast([128, NQ, 2, HD])).then_inc(stack_hi, 1)
                act.copy(stack[:, NQ:, 0:3:2], r[:, NQ:].to_broadcast([128, NKV, 2, HD])).then_inc(stack_hi, 1)

            def qkT_copies(b, p):
                for r in (0, 2, 4):
                    act.wait_ge(qkT_turned, 5 * b + r + 1)
                    dst = qT[p][:, 4 * r:4 * r + 4] if r < 4 else kT[p][:]
                    act.copy(dst.rearrange("k r s -> k (r s)"), turn[0][:]).then_inc(qkT_by_act, 1)

            def maxT_copy(b):
                act.wait_ge(max_turned, b + 1)
                if not isinstance(b, int) or b > 0:
                    act.wait_ge(max_rows, 64 * b)
                act.copy(maxT[:], out_b[0:64, 0:128]).then_inc(maxT_ready, 1)

            def exps(b):
                for g in range(NKV):
                    act.wait_ge(pass2_done, 8 * b + g + 1)
                    if g >= 4 or not isinstance(b, int) or b > 0:
                        act.wait_ge(pv_done, 8 * b + g - 3)
                    act.activation(probs[g % 4][:].rearrange("t r s -> t (r s)"), score[g % 2][:], ACT.Exp,
                                   scale=float(HD) ** -0.5).then_inc(exp_done, 1)

            def pv_copy(b, half):
                act.wait_ge(pv_done, 8 * b + 4 * half + 4)
                if not isinstance(b, int) or b > 0:
                    act.wait_ge(pv_turned, 2 * b - 1 + half)
                act.copy(pv_sb[half][:].rearrange("k r s -> k (r s)"), (out_a, out_b)[half][:]).then_inc(pv_copied, 1)

            def o_hi(b):
                act.wait_ge(oT_turned, b + 1)
                if not isinstance(b, int) or b > 0:
                    act.wait_ge(wo_done, b)
                act.copy(oT_hi[:].rearrange("k c s -> k (c s)"), turn[1][:]).then_inc(oT_hi_ready, 1)

            x_hi(0, 0)
            for c in range(KC):
                act.wait_ge(wqkv_in[c], 16)
                act.copy(wqkv_hi[:, c], wst[:, c]).then_inc(wqkv_hi_ready, 1)
            x_hi(1, 1)
            act.wait_ge(wo_loaded, 16)
            act.copy(wo_hi[:], wo_in[:]).then_inc(wo_hi_ready, 1)
            v_copy(0, 0)
            high_parts(0)
            qkT_copies(0, 0)

            def step(b, p):
                final = isinstance(b, int) and b == B - 1
                maxT_copy(b)
                if not final:
                    v_copy(b + 1, 1 - p)
                    high_parts(b + 1)
                exps(b)
                pv_copy(b, 0)
                pv_copy(b, 1)
                if not final:
                    qkT_copies(b + 1, 1 - p)
                o_hi(b)
                if not (isinstance(b, int) and b >= B - 2):
                    x_hi(b + 2, p)

            step(0, 0)
            with act.Fori(0, (B - 4) // 2) as i:
                step(i * 2 + 1, 1)
                step(i * 2 + 2, 0)
            step(B - 3, 1)
            step(B - 2, 0)
            step(B - 1, 1)

            act.wait_ge(cross_in, 16 * 11)
            act.wait_ge(wo_done, B)
            act.copy(wq_hi[:], wq_in[:]).then_inc(cross_hi, 1)
            act.copy(wm_hi[:], wm_in[:]).then_inc(cross_hi, 1)
            act.wait_ge(proj_summed, 1)
            act.copy(proj_sum_k[:], qkv_ps[0:1, 0:XK]).then_inc(proj_sums, 1)
            act.copy(proj_sum_v[:], qkv_ps[0:1, XK:2 * XK].rearrange("o (a k) -> o a k", a=1).to_broadcast([1, HPT, XK])).then_inc(proj_sums, 1)

            def ctx_copy(b):
                act.wait_ge(ctx_done, b + 1)
                if not isinstance(b, int) or b > 0:
                    act.wait_ge(kv_done, b)
                act.copy(ctx_k[:], qkv_ps[:, 0:XK]).then_inc(ctx_copied, 1)
                act.copy(ctx_v[:], qkv_ps[:, XK:2 * XK].rearrange("d (a k) -> d a k", a=1).to_broadcast([128, HPT, XK])).then_inc(ctx_copied, 1)

            def x1_high(b):
                if not isinstance(b, int) or b > 0:
                    act.wait_ge(xq_done, b)
                act.copy(x1_hi[:], x1[:, bass.ds(b, 1)].rearrange("s o d -> s (o d)")).then_inc(x1_hi_ready, 1)

            def xq_high(b):
                act.wait_ge(xq_done, b + 1)
                if not isinstance(b, int) or b > 0:
                    act.wait_ge(xscore_done, 4 * b)
                act.activation(xq_hi[:], out_a[:], ACT.Identity, bias=bias_q[:, 0:1]).then_inc(xq_hi_ready, 1)

            def keys_high(b, p):
                act.wait_ge(keys_ready, b + 1)
                if not isinstance(b, int) or b > 1:
                    act.wait_ge(xscore_done, 4 * b - 4)
                act.copy(keys_hi[p][:], keys[:].rearrange("c h k -> c (h k)")).then_inc(keys_hi_ready, 1)

            def xexp(b, t):
                act.wait_ge(xsub_done, 4 * b + t + 1)
                act.activation(xprob[t % 2][:], xprob[t % 2][:], ACT.Exp, scale=float(XD) ** -0.5).then_inc(xexp_done, 1)

            def xprobT_copy(b, t):
                act.wait_ge(xprob_turned, 4 * b + t + 1)
                if t == 0 and (not isinstance(b, int) or b > 0):
                    act.wait_ge(xpv_done, b)
                act.copy(xprobT[:, :, 128 * t:128 * t + 128], turn[t % 2][:].rearrange("k (j n) -> k j n", n=128)).then_inc(xprobT_ready, 1)

            def xo_high(b):
                act.wait_ge(xpv_done, b + 1)
                if not isinstance(b, int) or b > 0:
                    act.wait_ge(wm_done, b)
                act.copy(xo_hi[:], out_b[:]).then_inc(xo_hi_ready, 1)

            def x2T_high(b):
                act.wait_ge(x2_turned, b + 1)
                q = b % (B // 2) if isinstance(b, int) else b
                act.copy(x2T_hi[:, :, q], turn[0][:].rearrange("f (c s) -> f c s", c=KC)).then_inc(x2T_hi_ready, 1)

            act.wait_ge(x1_ready, B)

            def cross_step(b, p):
                x1_high(b)
                ctx_copy(b)
                xq_high(b)
                keys_high(b, p)
                for t in range(6):
                    if t < 4:
                        xexp(b, t)
                    if t > 1:
                        xprobT_copy(b, t - 2)
                xo_high(b)
                x2T_high(b)

            def split_high(buf, hi_sem, chunks=range(WCH)):
                for c in chunks:
                    raw, hi = (w[:, bass.ds(buf, 1), c].rearrange("k o n -> k (o n)") for w in (w_raw, w_hi))
                    act.copy(hi, raw).then_inc(hi_sem, 1)

            def shared_high(half, f):
                n = FC * half + f
                act.wait_ge(sh_gate_done, n + 1)
                if n > 0:
                    act.wait_ge(sh_z_ready, n)
                act.activation(sh_silu[:], score[f][:], ACT.Silu).then_inc(sh_silu_done, 1)
                act.wait_ge(sh_z_ready, n + 1)
                if half == 1 and f == 0:
                    act.wait_ge(sh_down_done, HB)
                act.copy(shT_hi[:, f], sh_z[:]).then_inc(shT_hi_ready, 1)

            act.wait_ge(moe_in, 16 * 9)
            act.copy(gate_hi[:], gate_in[:]).then_inc(gate_hi_ready, 1)

            for half in (0, 1):
                for k in range(HB):
                    cross_step(HB * half + k, k % 2)
                    if k < WCH // 2:
                        act.wait_ge(w_in, 16 * half + 16)
                        split_high(1 - half, (sh_hi_ready, w_hi_ready)[half], range(2 * k, 2 * k + 2))
                shared_high(half, 0)
                act.wait_ge(logits_turned, half + 1)
                if half == 1:
                    act.wait_ge(rows_ready, 1)
                act.activation(e_score[:], qkv_ps[:, 0:HB * NE].rearrange("t (b e) -> t b e", e=NE), ACT.Exp, scale=-1.0).then_inc(logit_exp, 1)
                shared_high(half, 1)

            act.wait_ge(tables_ready, 1)

            def slot_x_high(t, q):
                act.wait_ge(xs_turned, t + 1)
                if not isinstance(t, int) or t > 1:
                    act.wait_ge(gate_up_done, t - 1)
                act.copy(xsT_hi[q][:].rearrange("f c s -> f (c s)"), turn[0][:]).then_inc(xs_hi_ready, 1)

            def slot_silu(t, q):
                act.wait_ge(gate_up_done, t + 1)
                if not isinstance(t, int) or t > 0:
                    act.wait_ge(z_ready, t)
                act.activation(silu_g[:], score[q][:, 0:FF], ACT.Silu).then_inc(silu_done, 1)

            def slot_z_high(t):
                act.wait_ge(z_turned, t + 1)
                if not isinstance(t, int) or t > 0:
                    act.wait_ge(slot_done, t)
                act.copy(zT_hi[:].rearrange("f c s -> f (c s)"), turn[1][:, 0:FF]).then_inc(zT_hi_ready, 1)

            def y_copy(t, q):
                act.wait_ge(slot_done, t + 1)
                if not isinstance(t, int) or t > 1:
                    act.wait_ge(y_stored[q], 8 * (t - q))
                act.copy(y_sb[q][:], (out_a, out_b)[q][:]).then_inc(y_copied, 1)

            def next_expert_high(t):
                first = act.value_load(tab[0:1, 3, bass.ds(t, 1)], min_val=0, max_val=1)
                with act.If(first > 0):
                    e = act.value_load(tab[0:1, 0, bass.ds(t, 1)], min_val=0, max_val=NE - 2)
                    buf = act.value_load(tab[0:1, 1, bass.ds(t, 1)], min_val=0, max_val=1)
                    act.wait_ge(w_in, e * 16 + 48)
                    act.wait_ge(slot_done, t)
                    split_high(1 - buf, w_hi_ready)

            slot_x_high(0, 0)

            def step(t, q):
                slot_silu(t, q)
                if not isinstance(t, int) or t < SLOTS - 1:
                    slot_x_high(t + 1, 1 - q)
                if not isinstance(t, int) or t > 0:
                    y_copy(t - 1, 1 - q)
                slot_z_high(t)
                next_expert_high(t)

            step(0, 0)
            with act.Fori(0, (SLOTS - 3) // 2) as i:
                step(i * 2 + 1, 1)
                step(i * 2 + 2, 0)
            step(SLOTS - 2, 1)
            step(SLOTS - 1, 0)
            y_copy(SLOTS - 1, 0)

        @block.gpsimd
        def _(pool):
            pool.wait_ge(consts_ready, 4)

            def rotate(b):
                pool.wait_ge(rope_read, b + 1)
                if not isinstance(b, int) or b > 0:
                    pool.wait_ge(stack_lo, 2 * b)
                r = rotated[:].rearrange("s h (a e) -> s h a e", a=2)
                pool.tensor_tensor(r[:, :, 0], rope_cos[:, :, 0], rope_sin[:, :, 1], ALU.subtract).then_inc(rot_ready, 1)
                pool.tensor_tensor(r[:, :, 1], rope_cos[:, :, 1], rope_sin[:, :, 0], ALU.add).then_inc(rot_ready, 1)

            def mask_probs(b):
                for g in range(NKV):
                    pool.wait_ge(exp_done, 8 * b + g + 1)
                    pool.sem_inc(passed)
                    pr = probs[g % 4][:]
                    pool.affine_select(out=pr, in_=pr, pattern=[[0, REP], [1, 128]], compare_op=ALU.is_ge, fill=0.0,
                                       base=0, channel_multiplier=-1).then_inc(causal_done, 1)

            def rstd_1(b):
                pool.wait_ge(mv1, b + 1)
                pool.tensor_tensor(rstd[:], mean_var[:, 1:2], eps[:], ALU.add).then_inc(ve1, 1)
                pool.wait_ge(ve1, b + 1)
                pool.tensor_tensor(rstd[:], rstd[:], neg_half[:], ALU.pow).then_inc(rstd1, 1)

            rotate(0)

            def step(b, p):
                first, final = isinstance(b, int) and b == 0, isinstance(b, int) and b == B - 1
                if not first:
                    rstd_1(b - 1)
                if not final:
                    rotate(b + 1)
                mask_probs(b)

            over_batches(pool, step, None, None)
            rstd_1(B - 1)

            def xnormalise(b, t):
                pool.wait_ge(xrec_ready, 4 * b + t + 1)
                pr = xprob[t % 2][:]
                pool.tensor_tensor(pr, pr, xrec[:, t % 2].rearrange("n (h o) -> n h o", o=1).to_broadcast([128, XH, XK]), ALU.mult).then_inc(xprob_ready, 1)

            def rstd_2(b):
                pool.wait_ge(mv2, b + 1)
                pool.tensor_tensor(rstd2[:], mean_var2[:, 1:2], eps[:], ALU.add).then_inc(ve2, 1)
                pool.wait_ge(ve2, b + 1)
                pool.tensor_tensor(rstd2[:], rstd2[:], neg_half[:], ALU.pow).then_inc(rstd2_ready, 1)

            def x2_keep(b):
                pool.wait_ge(x2s_ready, b + 1)
                pool.tensor_copy(x2[:, bass.ds(b, 1)].rearrange("s o d -> s (o d)"), x2s[:]).then_inc(x2_ready, 1)

            def cross_step(b, p):
                for t in range(4):
                    xnormalise(b, t)
                rstd_2(b)
                x2_keep(b)

            def load_weights(src, buf):
                pool.dma_start(w_raw[:, buf], src).then_inc(w_in, 16)

            pool.wait_ge(x1_ready, B)
            pool.wait_ge(wo_done, B)
            load_weights(T["shared"], 1)
            pool.wait_ge(w_in, 16)
            load_weights(T["experts"][0], 0)

            def scatter(b, j):
                if j == 0:
                    pool.wait_ge(x2_ready, b + 1)
                pool.indirect_dma_start(xs_dram, bass.IndirectOffsetOnAxis(ap=row_of[:, j, b:b + 1], axis=0), x2[:, b], None).then_inc(scattered, 16)

            for half in (0, 1):
                for b in range(HB * half, HB * (half + 1)):
                    cross_step(b, b % 2)
                    if half == 1:
                        if b == HB:
                            pool.wait_ge(rows_ready, 1)
                        for j in range(TOPK):
                            scatter(b - HB, j)
            pool.wait_ge(rows_ready, 2)
            for b in range(HB, B):
                for j in range(TOPK):
                    scatter(b, j)

            pool.wait_ge(w_in, 32)
            pool.wait_ge(sh_lo_ready, WCH)
            load_weights(T["experts"][1], 1)

            def load_expert(e, buf):
                pool.wait_ge(w_in, e * 16 + 16)
                pool.wait_ge(w_lo_ready, (e - 1) * WCH)
                load_weights(T["experts"][bass.ds(e, 1)].rearrange("o p c n -> (o p) c n"), buf)

            with pool.Fori(1, NE // 2) as i:
                load_expert(i * 2, 0)
                load_expert(i * 2 + 1, 1)

            pool.wait_ge(yrows_ready, 1)
            pool.wait_ge(y_stored[0], 16 * ((SLOTS + 1) // 2))
            pool.wait_ge(y_stored[1], 16 * (SLOTS // 2))

            def gather(b, p):
                if not isinstance(b, int) or b > 1:
                    pool.wait_ge(combined, b * TOPK - TOPK)
                for j in range(TOPK):
                    pool.indirect_dma_start(gathered[p][:, j], None, ys_dram, bass.IndirectOffsetOnAxis(ap=yrow_of[:, j, bass.ds(b, 1)], axis=0)).then_inc(gathered_in[p], 16)

            def rstd_3(b):
                pool.wait_ge(mv3, b + 1)
                pool.tensor_tensor(rstd3[:], mean_var3[:, 1:2], eps[:], ALU.add).then_inc(ve3, 1)
                pool.wait_ge(ve3, b + 1)
                pool.tensor_tensor(rstd3[:], rstd3[:], neg_half[:], ALU.pow).then_inc(rstd3_ready, 1)

            gather(0, 0)
            gather(1, 1)
            for b in range(B):
                rstd_3(b)
                if b < B - 2:
                    gather(b + 2, b % 2)


def lay_out(inputs):
    f = {k: np.asarray(v) for k, v in inputs.items()}
    x = f["x"]
    w = f["L0_attn_w_qkv"]
    half = np.concatenate([np.arange(0, HD, 2), np.arange(1, HD, 2)])
    heads = np.arange(NQ).reshape(NKV // 2, 2, REP).transpose(0, 2, 1).ravel()
    heads = np.concatenate([heads, np.arange(NQ, QK_HEADS)])
    cols = np.concatenate([(heads[:, None] * HD + half[None, :]).ravel(), np.arange(QK_HEADS * HD, QKV)])
    rows = lambda m: m.reshape(m.shape[0] // 128, 128, -1).transpose(1, 0, 2)
    arrays = {
        "x": x,
        "xT": x.transpose(0, 2, 1).reshape(B, KC, 128, S).transpose(0, 2, 1, 3),
        "w_qkv": rows(w[:, cols]),
        "w_o": rows(f["L0_attn_w_o"]),
    }
    ch = np.arange(D // KC).reshape(XD, XH).T.ravel()
    arrays.update({
        "wq": f["L0_xattn_Wq"][ch].T, "wk": f["L0_xattn_Wk"][ch].T, "wv": f["L0_xattn_Wv"][ch].T,
        "wm": f["L0_xattn_Wm"][:, ch].T,
        "bq": f["L0_xattn_bq"][ch][:, None], "bk": f["L0_xattn_bk"][ch][None], "bv": f["L0_xattn_bv"][ch][None],
        "bm": f["L0_xattn_bm"][:, None],
        "proj": rows(np.concatenate([f["L0_xattn_proj_k"], f["L0_xattn_proj_v"]], 1)),
        "ctxT": f["ctx_4096"].transpose(0, 2, 1).reshape(B, KC, 128, S).transpose(0, 2, 1, 3),
    })
    wt = lambda w: rows(w.T)
    ffn = lambda g, u, d: np.concatenate([np.concatenate([wt(g), wt(u)], 2), wt(d)], 1)
    arrays.update({
        "gate": rows(f["L0_ffn_gate_w"].T),
        "bias_e": np.broadcast_to(f["L0_ffn_bias"][None], (128, NE)),
        "experts": np.stack([ffn(f["L0_ffn_Wg"][e], f["L0_ffn_Wu"][e], f["L0_ffn_Wd"][e]) for e in range(NE)]),
        "shared": ffn(f["L0_ffn_Sg"], f["L0_ffn_Su"], f["L0_ffn_Sd"]),
    })
    arrays.update(tables())
    return {k: np.ascontiguousarray(v) for k, v in arrays.items()}


def kernel(**inputs):
    import concourse.bacc as bacc
    from concourse.bass_utils import run_bass_kernel_spmd

    arrays = lay_out(inputs)
    nc = bacc.Bacc("TRN2", target_bir_lowering=False, num_devices=1)
    T = {n: nc.dram_tensor(f"in_{n}", a.shape, mybir.dt.from_np(a.dtype), kind="ExternalInput").ap() for n, a in arrays.items()}
    T["out"] = nc.dram_tensor("out_0", (B, S, D), F32, kind="ExternalOutput").ap()
    program(nc, T)
    r = run_bass_kernel_spmd(nc, [{f"in_{n}": a for n, a in arrays.items()}], core_ids=[0])
    return r.results[0]["out_0"]
```

```python
from contextlib import ExitStack

import numpy as np

import concourse.bass as bass
from concourse import mybir

F32 = mybir.dt.float32
F32R = mybir.dt.float32r
BF16 = mybir.dt.bfloat16
F16 = mybir.dt.float16
I32 = mybir.dt.int32
ALU = mybir.AluOpType
ACT = mybir.ActivationFunctionType
AX = mybir.AxisListType

B, S, D = 8, 128, 512
KC = D // 128
HD, NQ, NKV = 16, 32, 8
REP = NQ // NKV
QKV = HD * (NQ + 2 * NKV)
QK_HEADS = NQ + NKV
STACK = 4 * HD
XH, XD, XK = 16, 8, 32
HPT = 128 // XK
NE, TOPK, FF = 16, 4, 256
FC = FF // 128
TOKENS = B * S
SLOT = 128
REGION = TOKENS + SLOT
IDLE_ROW = NE * REGION
SLOTS = (TOKENS * TOPK + NE * (SLOT - 1)) // SLOT
HB = B // 2
WCH = KC + FC
EPS = 1e-5
MASKED = -1e30


def tables():
    inv_freq = (1.0 / np.float32(10000.0) ** (np.arange(0, HD, 2, dtype=np.float32) / np.float32(HD))).astype(np.float32)
    angles = np.arange(S, dtype=np.float32)[:, None] * inv_freq[None, :]
    cos, sin = np.cos(angles).astype(np.float32), np.sin(angles).astype(np.float32)
    rope = np.stack([np.concatenate([cos, cos], 1), np.concatenate([sin, sin], 1)], 1)
    return {
        "rope": np.ascontiguousarray(rope),
        "head_mask": (np.arange(128)[:, None] // XD == np.arange(XH)[None]).astype(np.float32),
        "value_mask": (np.arange(128)[:, None] // XK == np.arange(HPT)[None]).astype(np.float32),
        "region": np.broadcast_to(np.arange(NE, dtype=np.float32) * REGION, (128, NE)),
        "iota16": np.broadcast_to(np.arange(NE, dtype=np.float32) - NE, (128, NE)),
        "tri": (np.arange(128)[:, None] < np.arange(128)[None]).astype(np.float32),
        "thresholds": np.broadcast_to(np.array([-1] + [128 * k for k in range(1, 8)], np.float32), (128, 8)),
        "upto_mask": np.broadcast_to((np.arange(NE)[None] <= np.arange(NE)[:, None]).astype(np.float32), (128, NE, NE)),
        "slot_no": np.arange(SLOTS, dtype=np.float32)[None],
        "alternate": np.array([[(-1.0) ** e for e in range(NE - 1)] + [0.0]], np.float32),
        "ident": np.eye(128, dtype=np.float32),
        "causal": np.where(np.arange(S)[None, :] > np.arange(S)[:, None], np.float32(MASKED), np.float32(0)).astype(np.float32),
    }


def program(nc, T):
    T["xs"] = nc.dram_tensor("dispatched", (NE * REGION + SLOT, D), F32).ap()
    T["ys"] = nc.dram_tensor("slot_results", (SLOTS * SLOT, D), F32).ap()
    with ExitStack() as ctx:
        def sb(name, shape, dt=F32):
            return ctx.enter_context(nc.sbuf_tensor(name, shape, dt))

        def sem(name):
            return ctx.enter_context(nc.semaphore(name))

        ident = sb("ident", [128, 128])
        neg_half = sb("neg_half", [128, 1])
        eps = sb("eps", [128, 1])
        x1 = sb("x1", [128, B, D])
        base = x1
        x2 = sb("x2", [128, B, D])
        bias_e = sb("bias_e", [128, NE]); region = sb("region", [128, NE])
        iota16 = sb("iota16", [128, NE]); tri = sb("tri", [128, 128]); tri_bf = sb("tri_bf", [128, 128], BF16)
        e_score = sb("e_score", [128, HB, NE]); e_eq = sb("e_eq", [128, HB, NE]); e_low = sb("e_low", [128, HB])
        picked = sb("picked", [128, TOPK, B, NE])
        weight = sb("weight", [128, TOPK, B]); w_sum = sb("w_sum", [128, HB]); w_rec = sb("w_rec", [128, HB])
        chosen = sb("chosen", [128, HB, NE]); chosen_bf = sb("chosen_bf", [128, HB, NE], BF16)
        before = sb("before", [128, B + 1, NE]); before_bf = sb("before_bf", [128, B + 1, NE], BF16)
        rank = sb("rank", [128, B, NE]); place = sb("place", [128, B, NE])
        picked_place = sb("picked_place", [128, TOPK, B, NE]); row_f = sb("row_f", [128, TOPK, B])
        row_of = sb("row_of", [128, TOPK, B], I32); yrow_of = sb("yrow_of", [128, TOPK, B], I32)
        x2T_hi = sb("x2T_hi", [128, KC, B // 2, 128], F32R)
        x2T_lo = sb("x2T_lo", [128, KC, B // 2, 128], F32R)
        ones_bf = sb("ones_bf", [128, 128], BF16)

        self_scope = ExitStack()
        outer_sb = sb

        def sb(name, shape, dt=F32):
            return self_scope.enter_context(nc.sbuf_tensor(name, shape, dt))

        ident_bf = sb("ident_bf", [128, 128], BF16)
        causal = sb("causal", [128, 128])
        causal_bf = sb("causal_bf", [128, REP, 128], BF16)
        rope = sb("rope", [128, 2, HD])
        wst = sb("wst", [128, KC, QKV])
        wqkv_hi = sb("wqkv_hi", [128, KC, QKV], F32R)
        wqkv_lo = sb("wqkv_lo", [128, KC, QKV], F32R)
        wo_in = sb("wo_in", [128, KC, D])
        wo_hi = sb("wo_hi", [128, KC, D], F32R)
        wo_lo = sb("wo_lo", [128, KC, D], F32R)
        xT = sb("xT", [128, 2, KC, 128])
        xT_hi = [sb(f"xT_hi{p}", [128, KC, 128], F32R) for p in (0, 1)]
        xT_lo = [sb(f"xT_lo{p}", [128, KC, 128], F32R) for p in (0, 1)]
        x_in = sb("x_in", [128, 2, D])
        rope_cos = sb("rope_cos", [128, QK_HEADS, 2, HD // 2])
        rope_sin = sb("rope_sin", [128, QK_HEADS, 2, HD // 2])
        rotated = sb("rotated", [128, QK_HEADS, HD])
        stack = sb("stack", [128, QK_HEADS, 4, HD], F32R)
        v_ones = [sb(f"v_ones{p}", [128, NKV, 32]) for p in (0, 1)]
        qT = [sb(f"qT{p}", [128, NQ // 2, 128], F32R) for p in (0, 1)]
        kT = [sb(f"kT{p}", [128, NKV // 2, 128], F32R) for p in (0, 1)]
        qT_half = sb("qT_half", [128, NQ // 2, 128], F16)
        kT_half = sb("kT_half", [128, NKV // 2, 128], F16)
        pv_sb = [sb(f"pv_sb{h}", [128, REP, 128]) for h in (0, 1)]
        neg_max = sb("neg_max", [128, NKV, REP])
        neg_max_parts = sb("neg_max_parts", [128, 4, 2, NKV // 2, REP], F32R)
        maxT = sb("maxT", [64, 128], F32R)
        probs = [sb(f"probs{r}", [128, REP, 128]) for r in range(4)]
        attn_rsum = sb("attn_rsum", [128, 2, REP, 4])
        attn_out = sb("attn_out", [128, 2, NQ // 2, HD])
        oT_hi = sb("oT_hi", [128, KC, 128], F32R)
        oT_lo = sb("oT_lo", [128, KC, 128], F32R)
        y1 = sb("y1", [128, D])
        bn6 = sb("bn6", [128, 6])
        mean_var = sb("mean_var", [128, 2])
        rstd = sb("rstd", [128, 1])
        self_scope.close()
        sb = outer_sb

        gate_in = sb("gate_in", [128, KC, NE]); gate_hi = sb("gate_hi", [128, KC, NE], F32R); gate_lo = sb("gate_lo", [128, KC, NE], F32R)
        logitT = sb("logitT", [NE, HB * 128])
        w_raw = sb("w_raw", [128, 2, WCH, D])
        w_hi = sb("w_hi", [128, 2, WCH, D], F32R); w_lo = sb("w_lo", [128, 2, WCH, D], F32R)
        count = sb("count", [128, NE]); thresholds = sb("thresholds", [128, 8]); over = sb("over", [128, NE, 8])
        n_slots = sb("n_slots", [128, NE]); slots_to = sb("slots_to", [128, NE]); slot_base = sb("slot_base", [128, NE])
        upto_mask = sb("upto_mask", [128, NE, NE]); prod = sb("prod", [128, NE, NE])
        slot_no = sb("slot_no", [1, SLOTS]); passed_e = sb("passed_e", [1, SLOTS, NE]); passed_w = sb("passed_w", [1, SLOTS, NE]); alternate = sb("alternate", [1, NE])
        tab_f = sb("tab_f", [1, 6, SLOTS + 1]); tab = sb("tab", [1, 4, SLOTS], I32); pad_f = sb("pad_f", [1, NE]); pad_row = sb("pad_row", [1, NE], I32)
        zeros = sb("zeros", [128, D])
        sh_z = sb("sh_z", [128, D])
        shT_hi = sb("shT_hi", [128, FC, D], F32R); shT_lo = sb("shT_lo", [128, FC, D], F32R)
        gathered = [w_raw[:, q, 0:TOPK] for q in (0, 1)]
        out_sb = [w_raw[:, q, TOPK] for q in (0, 1)]
        y3 = w_raw[:, 0, TOPK + 1]
        bn6c = sb("bn6c", [128, 6]); mean_var3 = sb("mean_var3", [128, 2]); rstd3 = sb("rstd3", [128, 1])
        xs_dram, ys_dram = T["xs"], T["ys"]
        cross_scope = ExitStack()

        def sb(name, shape, dt=F32):
            return cross_scope.enter_context(nc.sbuf_tensor(name, shape, dt))

        wq_in = sb("wq_in", [128, 128]); wq_hi = sb("wq_hi", [128, 128], F32R); wq_lo = sb("wq_lo", [128, 128], F32R)
        wm_in = sb("wm_in", [128, 128]); wm_hi = sb("wm_hi", [128, 128], F32R); wm_lo = sb("wm_lo", [128, 128], F32R)
        wk = sb("wk", [128, 128]); wv = sb("wv", [128, 128])
        bias_q = sb("bias_q", [128, 1]); bias_m = sb("bias_m", [128, 1])
        bias_k_row = sb("bias_k_row", [1, 128]); bias_v_row = sb("bias_v_row", [1, 128])
        proj = sb("proj", [128, KC, 2 * XK])
        head_mask = sb("head_mask", [128, XH]); value_mask = sb("value_mask", [128, HPT])
        ones_col = sb("ones_col", [128, 1])
        proj_sum_k = sb("proj_sum_k", [1, XK]); proj_sum_v = sb("proj_sum_v", [1, HPT, XK])
        ctxT = [sb(f"ctxT{p}", [128, KC, 128]) for p in (0, 1)]
        ctx_k = sb("ctx_k", [128, XK]); ctx_v = sb("ctx_v", [128, HPT, XK])
        keys = sb("keys", [128, XH, XK])
        keys_hi = [sb(f"keys_hi{p}", [128, XH * XK], F32R) for p in (0, 1)]
        keys_lo = [sb(f"keys_lo{p}", [128, XH * XK], F32R) for p in (0, 1)]
        values = [sb(f"values{p}", [128, XH // HPT, HPT, XD]) for p in (0, 1)]
        x1_hi = sb("x1_hi", [128, D], F32R); x1_lo = sb("x1_lo", [128, D], F32R)
        xq_hi = sb("xq_hi", [128, D], F32R); xq_lo = sb("xq_lo", [128, D], F32R)
        xmax = sb("xmax", [128, 4, XH]); xsum = sb("xsum", [128, 4, XH]); xrec = sb("xrec", [128, 4, XH])
        xprob = [sb(f"xprob{t}", [128, XH, XK]) for t in range(4)]
        xprobT = [sb(f"xprobT{t}", [128, XH // HPT, 128]) for t in (0, 1)]
        xo_hi = sb("xo_hi", [128, D], F32R); xo_lo = sb("xo_lo", [128, D], F32R)
        y2 = sb("y2", [128, D]); x2s = sb("x2s", [128, D])
        bn6b = sb("bn6b", [128, 6]); mean_var2 = sb("mean_var2", [128, 2]); rstd2 = sb("rstd2", [128, 1])
        cross_scope.close()
        sb = outer_sb
        xs_in = [sb(f"xs_in{q}", [128, D]) for q in (0, 1)]
        xsT_hi = [sb(f"xsT_hi{q}", [128, KC, 128], F32R) for q in (0, 1)]
        xsT_lo = [sb(f"xsT_lo{q}", [128, KC, 128], F32R) for q in (0, 1)]
        silu_g = sb("silu_g", [128, FF]); z = sb("z", [128, FF])
        zT_hi = sb("zT_hi", [128, FC, 128], F32R); zT_lo = sb("zT_lo", [128, FC, 128], F32R)
        y_sb = [sb(f"y_sb{q}", [128, D]) for q in (0, 1)]

        bank = [ctx.enter_context(nc.psum_tensor(f"bank{i}", [128, 512], F32)) for i in range(2, 8)]
        qkv_ps = ctx.enter_context(nc.psum_tensor("qkv_ps", [128, 1024], F32))
        turn = [bank[0], bank[1]]
        score = [bank[2], bank[3]]
        out_a, out_b = bank[4], bank[5]
        ctx_ps, k_ps, v_ps = qkv_ps[:, 512:512 + 2 * XK], qkv_ps[:, 576:576 + XK], qkv_ps[:, 640:768]

        consts_in = sem("consts_in"); wqkv_in = [sem(f"wqkv_in{c}") for c in range(KC)]; wo_loaded = sem("wo_loaded")
        xT_in = [sem(f"xT_in{p}") for p in (0, 1)]; x_loaded = [sem(f"x_loaded{p}") for p in (0, 1)]
        consts_ready = sem("consts_ready")
        wqkv_hi_ready = sem("wqkv_hi_ready"); wqkv_lo_ready = sem("wqkv_lo_ready")
        wo_hi_ready = sem("wo_hi_ready"); wo_lo_ready = sem("wo_lo_ready")
        xT_hi_ready = sem("xT_hi_ready"); xT_lo_ready = sem("xT_lo_ready")
        qkv_done = sem("qkv_done"); rope_read = sem("rope_read"); v_ready = sem("v_ready")
        rot_ready = sem("rot_ready"); stack_hi = sem("stack_hi"); stack_lo = sem("stack_lo")
        qkT_turned = sem("qkT_turned"); qkT_by_act = sem("qkT_by_act"); qkT_by_dve = sem("qkT_by_dve")
        pass1_done = sem("pass1_done"); max_done = sem("max_done")
        max_hi = sem("max_hi"); max_parts = sem("max_parts"); max_turned = sem("max_turned")
        maxT_ready = sem("maxT_ready"); max_rows = sem("max_rows")
        pass2_done = sem("pass2_done"); exp_done = sem("exp_done"); causal_done = sem("causal_done")
        pv_done = sem("pv_done"); halves_ready = sem("halves_ready"); pv_copied = sem("pv_copied"); pv_turned = sem("pv_turned"); rsum_ready = sem("rsum_ready"); attn_normed = sem("attn_normed")
        oT_turned = sem("oT_turned"); oT_hi_ready = sem("oT_hi_ready"); oT_lo_ready = sem("oT_lo_ready")
        wo_done = sem("wo_done"); y1_ready = sem("y1_ready"); stats1 = sem("stats1"); mv1 = sem("mv1")
        ve1 = sem("ve1"); rstd1 = sem("rstd1"); x1_ready = sem("x1_ready")
        cross_in = sem("cross_in"); cross_hi = sem("cross_hi"); cross_lo = sem("cross_lo"); cross_masks = sem("cross_masks")
        proj_summed = sem("proj_summed"); proj_sums = sem("proj_sums")
        ctxT_in = [sem(f"ctxT_in{p}") for p in (0, 1)]
        ctx_done = sem("ctx_done"); ctx_copied = sem("ctx_copied"); kv_done = sem("kv_done")
        keys_ready = sem("keys_ready"); values_ready = sem("values_ready"); keys_hi_ready = sem("keys_hi_ready"); keys_lo_ready = sem("keys_lo_ready")
        x1_hi_ready = sem("x1_hi_ready"); x1_lo_ready = sem("x1_lo_ready"); xq_done = sem("xq_done")
        xq_hi_ready = sem("xq_hi_ready"); xq_lo_ready = sem("xq_lo_ready")
        xscore_done = sem("xscore_done"); xmax_ready = sem("xmax_ready"); xsub_done = sem("xsub_done"); xexp_done = sem("xexp_done")
        xsum_ready = sem("xsum_ready"); xrec_ready = sem("xrec_ready"); xprob_ready = sem("xprob_ready")
        xprob_turned = sem("xprob_turned"); xprobT_ready = sem("xprobT_ready"); xpv_done = sem("xpv_done")
        xo_hi_ready = sem("xo_hi_ready"); xo_lo_ready = sem("xo_lo_ready"); wm_done = sem("wm_done")
        y2_ready = sem("y2_ready"); stats2 = sem("stats2"); mv2 = sem("mv2"); ve2 = sem("ve2"); rstd2_ready = sem("rstd2_ready")
        x2s_ready = sem("x2s_ready"); x2_ready = sem("x2_ready"); x2_turned = sem("x2_turned")
        x2T_hi_ready = sem("x2T_hi_ready"); x2T_lo_ready = sem("x2T_lo_ready")
        moe_in = sem("moe_in"); gate_hi_ready = sem("gate_hi_ready"); gate_lo_ready = sem("gate_lo_ready"); tri_ready = sem("tri_ready")
        logits_done = sem("logits_done"); logitT_ready = sem("logitT_ready"); logits_turned = sem("logits_turned"); logit_exp = sem("logit_exp")
        route = sem("route"); chosen_ready = sem("chosen_ready"); ranks_done = sem("ranks_done"); ranks_read = sem("ranks_read"); rows_ready = sem("rows_ready")
        scattered = sem("scattered"); counts_done = sem("counts_done"); tables_ready = sem("tables_ready"); yrows_ready = sem("yrows_ready"); padded = sem("padded")
        zeros_ready = sem("zeros_ready")
        w_in = sem("w_in"); w_hi_ready = sem("w_hi_ready"); w_lo_ready = sem("w_lo_ready")
        sh_hi_ready = sem("sh_hi_ready"); sh_lo_ready = sem("sh_lo_ready")
        sh_gate_done = sem("sh_gate_done"); sh_up_done = sem("sh_up_done"); sh_silu_done = sem("sh_silu_done"); sh_z_ready = sem("sh_z_ready")
        shT_hi_ready = sem("shT_hi_ready"); shT_lo_ready = sem("shT_lo_ready"); sh_down_done = sem("sh_down_done"); base_ready = sem("base_ready")
        xs_loaded = [sem(f"xs_loaded{q}") for q in (0, 1)]; xs_turned = sem("xs_turned"); xs_hi_ready = sem("xs_hi_ready"); xs_lo_ready = sem("xs_lo_ready")
        gate_up_done = sem("gate_up_done"); silu_done = sem("silu_done"); z_ready = sem("z_ready"); z_turned = sem("z_turned")
        zT_hi_ready = sem("zT_hi_ready"); zT_lo_ready = sem("zT_lo_ready"); slot_done = sem("slot_done"); y_copied = sem("y_copied")
        y_stored = [sem(f"y_stored{q}") for q in (0, 1)]
        gathered_in = [sem(f"gathered_in{q}") for q in (0, 1)]; combined = sem("combined"); stats3 = sem("stats3"); mv3 = sem("mv3"); ve3 = sem("ve3"); rstd3_ready = sem("rstd3_ready")
        out_ready = sem("out_ready"); out_in = [sem(f"out_in{q}") for q in (0, 1)]
        passed = sem("passed")

        block = ctx.enter_context(nc.Block())

        def over_batches(eng, step, first, last_):
            step(0, 0)
            with eng.Fori(0, (B - 2) // 2) as i:
                step(i * 2 + 1, 1)
                step(i * 2 + 2, 0)
            step(B - 1, 1)

        def half_place(t, b):
            return t[:, :, b % HB] if isinstance(b, int) else t[:, :, bass.ds(b, 1)].rearrange("f c o s -> f c (o s)")

        @block.sync
        def _(sp):
            def load_xT(b, p):
                sp.dma_start(xT[:, p], T["xT"][bass.ds(b, 1)].rearrange("o p c s -> (o p) c s")).then_inc(xT_in[p], 16)

            def load_x(b, p):
                sp.dma_start(x_in[:, p], T["x"][bass.ds(b, 1)].rearrange("o s d -> (o s) d")).then_inc(x_loaded[p], 16)

            load_xT(0, 0)
            for c in range(KC):
                sp.dma_start(wst[:, c], T["w_qkv"][:, c]).then_inc(wqkv_in[c], 16)
            sp.dma_start(rope[:], T["rope"]).then_inc(consts_in, 16)
            sp.dma_start(ident[:], T["ident"]).then_inc(consts_in, 16)
            sp.dma_start(causal[:], T["causal"]).then_inc(consts_in, 16)
            load_xT(1, 1)
            load_x(0, 0)
            sp.dma_start(wo_in[:], T["w_o"]).then_inc(wo_loaded, 16)

            def step(b, p):
                sp.wait_ge(maxT_ready, b + 1)
                for a in (0, 1):
                    row = 64 * a + 3 * HD
                    sp.dma_start(qT[p][row:row + 2, :, :].bitcast(F32),
                                 maxT[32 * a:32 * a + 32, :].bitcast(F32)).then_inc(max_rows, 16)
                if not (isinstance(b, int) and b >= B - 2):
                    sp.wait_ge(xT_hi_ready, b + 1)
                    sp.wait_ge(xT_lo_ready, b + 1)
                    load_xT(b + 2, p)
                if not (isinstance(b, int) and b == B - 1):
                    if not isinstance(b, int) or b > 0:
                        sp.wait_ge(y1_ready, b)
                    load_x(b + 1, 1 - p)

            step(0, 0)
            with sp.Fori(0, (B - 4) // 2) as i:
                step(i * 2 + 1, 1)
                step(i * 2 + 2, 0)
            step(B - 3, 1)
            step(B - 2, 0)
            step(B - 1, 1)
            sp.wait_ge(x1_ready, B)
            sp.wait_ge(wo_done, B)
            for tile, name in ((wq_in, "wq"), (wm_in, "wm"), (wk, "wk"), (wv, "wv"), (bias_q, "bq"), (bias_m, "bm"),
                               (bias_k_row, "bk"), (bias_v_row, "bv"), (proj, "proj"), (head_mask, "head_mask"),
                               (value_mask, "value_mask")):
                sp.dma_start(tile[:], T[name]).then_inc(cross_in, 16)

            def load_ctx(b, p):
                if not isinstance(b, int) or b > 1:
                    sp.wait_ge(ctx_done, b - 1)
                sp.dma_start(ctxT[p][:], T["ctxT"][bass.ds(b, 1)].rearrange("o p c s -> (o p) c s")).then_inc(ctxT_in[p], 16)

            load_ctx(0, 0)
            load_ctx(1, 1)
            MOE_CONSTS = ((gate_in, "gate"), (bias_e, "bias_e"), (region, "region"), (iota16, "iota16"), (tri, "tri"),
                          (thresholds, "thresholds"), (upto_mask, "upto_mask"), (slot_no, "slot_no"), (alternate, "alternate"))
            for tile, name in MOE_CONSTS:
                sp.dma_start(tile[:], T[name]).then_inc(moe_in, 16)
            with sp.Fori(1, B // 2) as i:
                load_ctx(i * 2, 0)
                load_ctx(i * 2 + 1, 1)
            sp.wait_ge(zeros_ready, 1)
            sp.dma_start(xs_dram[IDLE_ROW:IDLE_ROW + SLOT, :], zeros[:]).then_inc(padded, 16)
            sp.wait_ge(tables_ready, 1)
            with sp.Fori(0, NE) as e:
                row = sp.value_load(pad_row[0:1, bass.ds(e, 1)], min_val=0, max_val=IDLE_ROW - SLOT)
                sp.dma_start(xs_dram[bass.ds(row, SLOT), :], zeros[:]).then_inc(padded, 16)
            sp.wait_ge(padded, 16 * (NE + 1))
            sp.wait_ge(scattered, 16 * TOPK * B)

            def load_slot(t, q):
                row = sp.value_load(tab[0:1, 2, bass.ds(t, 1)], min_val=0, max_val=IDLE_ROW)
                sp.dma_start(xs_in[q][:], xs_dram[bass.ds(row, SLOT), :]).then_inc(xs_loaded[q], 16)

            def store_slot(t, q):
                sp.wait_ge(y_copied, t + 1)
                sp.dma_start(ys_dram[bass.ds(t * SLOT, SLOT), :], y_sb[q][:]).then_inc(y_stored[q], 16)

            load_slot(0, 0)
            load_slot(1, 1)

            def step(t, q):
                if not isinstance(t, int) or t < SLOTS - 2:
                    sp.wait_ge(xs_turned, t + 1)
                    load_slot(t + 2, q)
                if not isinstance(t, int) or t > 0:
                    store_slot(t - 1, 1 - q)

            step(0, 0)
            with sp.Fori(0, (SLOTS - 3) // 2) as i:
                step(i * 2 + 1, 1)
                step(i * 2 + 2, 0)
            step(SLOTS - 2, 1)
            step(SLOTS - 1, 0)
            store_slot(SLOTS - 1, 0)
            def store_out(b, p):
                sp.wait_ge(out_ready, b + 1)
                sp.dma_start(T["out"][bass.ds(b, 1)].rearrange("o s d -> (o s) d"), out_sb[p]).then_inc(out_in[p], 16)

            with sp.Fori(0, B // 2) as i:
                store_out(i * 2, 0)
                store_out(i * 2 + 1, 1)
            sp.wait_ge(out_in[0], 16 * (B // 2))
            sp.wait_ge(out_in[1], 16 * (B // 2))

        @block.tensor
        def _(pe):
            def split_product(out, stat_hi, stat_lo, mov_hi, mov_lo, start, stop):
                pe.matmul(out, stat_hi, mov_lo, start=start, stop=False)
                pe.matmul(out, stat_lo, mov_hi, start=False, stop=False)
                return pe.matmul(out, stat_hi, mov_hi, start=False, stop=stop)

            def qkv_chunk(b, p, c):
                if c == 0:
                    pe.wait_ge(xT_hi_ready, b + 1)
                    pe.wait_ge(xT_lo_ready, b + 1)
                    if not isinstance(b, int) or b > 0:
                        pe.wait_ge(rope_read, b)
                        pe.wait_ge(v_ready, b)
                if isinstance(b, int) and b == 0:
                    pe.wait_ge(wqkv_hi_ready, c + 1)
                    pe.wait_ge(wqkv_lo_ready, c + 1)
                for lo, hi in ((0, 512), (512, QKV)):
                    last = split_product(qkv_ps[:, lo:hi], xT_hi[p][:, c], xT_lo[p][:, c],
                                         wqkv_hi[:, c, lo:hi], wqkv_lo[:, c, lo:hi], c == 0, c == KC - 1)
                if c == KC - 1:
                    last.then_inc(qkv_done, 1)

            def turn_qk(b, r):
                if r == 0:
                    pe.wait_ge(stack_hi, 2 * b + 2)
                    pe.wait_ge(stack_lo, 2 * b + 2)
                pairs = stack[:].rearrange("s (j two) a e -> s j (two a e)", two=2).bitcast(F32)
                if r == 1:
                    if not isinstance(b, int) or b > 1:
                        pe.wait_ge(oT_lo_ready, b - 1)
                elif r == 3:
                    pe.wait_ge(qkT_by_dve, 2 * b + 1)
                elif r > 0 or not isinstance(b, int) or b > 0:
                    pe.wait_ge(qkT_by_act, 3 * b + r // 2)
                j0 = NQ // 2 if r == 0 else 4 * (r - 1)
                for j in range(4):
                    t = pe.transpose(turn[r % 2][:, 128 * j:128 * j + 128], pairs[:, j0 + j], ident[:])
                t.then_inc(qkT_turned, 1)

            def pass1(b, p, g):
                u, a = g // 2, g % 2
                rows = slice(64 * a, 64 * a + HD)
                pe.wait_ge(halves_ready, 5 * b + u + 2)
                if g < 2:
                    if not isinstance(b, int) or b > 0:
                        pe.wait_ge(exp_done, 8 * b - 1 + g)
                else:
                    pe.wait_ge(max_done, 8 * b + g - 1)
                pe.matmul(score[g % 2][:], ident_bf[:], causal_bf[:].rearrange("s r t -> s (r t)"), start=True, stop=False)
                for r in range(REP):
                    m = pe.matmul(score[g % 2][:, 128 * r:128 * r + 128], qT_half[rows, 4 * u + r], kT_half[rows, u],
                                  start=False, stop=(r == REP - 1))
                m.then_inc(pass1_done, 1)

            def turn_max(b):
                pe.wait_ge(max_parts, b + 1)
                if not isinstance(b, int) or b > 0:
                    pe.wait_ge(attn_normed, 2 * b)
                pe.transpose(out_b[:, 0:128], neg_max_parts[:].rearrange("s a q u r -> s (a q u r)").bitcast(F32),
                             ident[:]).then_inc(max_turned, 1)

            def pass2(b, p, g):
                u, a = g // 2, g % 2
                rows = slice(64 * a, 64 * a + 3 * HD + 2)
                if g == 0:
                    pe.wait_ge(max_rows, 32 * b + 32)
                if g < 2:
                    pe.wait_ge(max_done, 8 * b + 7 + g)
                else:
                    pe.wait_ge(exp_done, 8 * b + g - 1)
                pe.matmul(score[g % 2][:], kT[p][rows, u], qT[p][rows, 4 * u:4 * u + 4].rearrange("k r s -> k (r s)"),
                          start=True, stop=True).then_inc(pass2_done, 1)

            def pv(b, p, g):
                pe.wait_ge(causal_done, 8 * b + g + 1)
                if g == 0:
                    pe.wait_ge(v_ready, b + 1)
                    if not isinstance(b, int) or b > 0:
                        pe.wait_ge(y1_ready, b)
                if g == 4:
                    pe.wait_ge(maxT_ready, b + 1)
                dst = out_a if g < 4 else out_b
                j = 32 * (g % 4)
                pe.matmul(dst[j:j + 32, :], v_ones[p][:, g], probs[g % 4][:].rearrange("t r s -> t (r s)"),
                          start=True, stop=True).then_inc(pv_done, 1)

            def turn_pv(b, half):
                pe.wait_ge(pv_copied, 2 * b + half + 1)
                for r in range(REP):
                    t = pe.transpose((out_a, out_b)[half][:, 128 * r:128 * r + 128], pv_sb[half][:, r], ident[:])
                t.then_inc(pv_turned, 1)

            def turn_o(b):
                pe.wait_ge(attn_normed, 2 * b + 2)
                pe.wait_ge(qkT_by_dve, 2 * b + 4 if not (isinstance(b, int) and b == B - 1) else 2 * B)
                if isinstance(b, int) and b == B - 1:
                    pe.wait_ge(oT_lo_ready, B - 1)
                o = attn_out[:].rearrange("s a h e -> s (a h e)")
                for c in range(KC):
                    t = pe.transpose(turn[1][:, 128 * c:128 * c + 128], o[:, 128 * c:128 * c + 128], ident[:])
                t.then_inc(oT_turned, 1)

            def w_o(b):
                pe.wait_ge(oT_hi_ready, b + 1)
                pe.wait_ge(oT_lo_ready, b + 1)
                if isinstance(b, int) and b == 0:
                    pe.wait_ge(wo_hi_ready, 1)
                    pe.wait_ge(wo_lo_ready, 1)
                for c in range(KC):
                    last = split_product(out_a[:], oT_hi[:, c], oT_lo[:, c], wo_hi[:, c], wo_lo[:, c], c == 0, c == KC - 1)
                last.then_inc(wo_done, 1)

            pe.wait_ge(consts_ready, 4)
            for c in range(KC):
                qkv_chunk(0, 0, c)
            for r in range(5):
                turn_qk(0, r)

            def step(b, p):
                first, final = isinstance(b, int) and b == 0, isinstance(b, int) and b == B - 1
                for g in range(NKV):
                    pass1(b, p, g)
                    if g == 2 and not first:
                        turn_pv(b - 1, 0)
                        turn_pv(b - 1, 1)
                    if g == 6 and not first:
                        turn_o(b - 1)
                    if g % 2 and not final:
                        qkv_chunk(b + 1, 1 - p, g // 2)
                turn_max(b)
                if not first:
                    w_o(b - 1)
                pass2(b, p, 0)
                pass2(b, p, 1)
                for g in range(NKV):
                    if g < NKV - 2:
                        pass2(b, p, g + 2)
                    pv(b, p, g)
                    if g >= NKV - 5 and not final:
                        turn_qk(b + 1, g - (NKV - 5))

            over_batches(pe, step, None, None)
            turn_pv(B - 1, 0)
            turn_pv(B - 1, 1)
            turn_o(B - 1)
            w_o(B - 1)

            def context(b, p):
                pe.wait_ge(ctxT_in[p], 8 * (b - p) + 16)
                if not isinstance(b, int) or b > 0:
                    pe.wait_ge(ctx_copied, 2 * b)
                    pe.wait_ge(values_ready, b)
                for c in range(KC):
                    m = pe.matmul(ctx_ps, ctxT[p][:, c], proj[:, c], start=(c == 0), stop=(c == KC - 1))
                m.then_inc(ctx_done, 1)

            def keys_values(b):
                pe.wait_ge(ctx_copied, 2 * b + 2)
                pe.matmul(k_ps, wk[:], ctx_k[:], start=True, stop=False)
                pe.matmul(k_ps, bias_k_row[:], proj_sum_k[:], start=False, stop=True)
                pe.matmul(v_ps, ctx_v[:].rearrange("d h k -> d (h k)"), wv[:], start=True, stop=False)
                pe.matmul(v_ps, proj_sum_v[:].rearrange("o h k -> o (h k)"), bias_v_row[:], start=False, stop=True).then_inc(kv_done, 1)

            def cross_q(b):
                pe.wait_ge(x1_hi_ready, b + 1)
                pe.wait_ge(x1_lo_ready, b + 1)
                if isinstance(b, int) and b == 0:
                    pe.wait_ge(y1_ready, B)
                elif not isinstance(b, int) or b > 1:
                    pe.wait_ge(y2_ready, b - 1)
                split_product(out_a[:], wq_hi[:], wq_lo[:], x1_hi[:], x1_lo[:], True, True).then_inc(xq_done, 1)

            def cross_score(b, p, t):
                if t == 0:
                    pe.wait_ge(xq_lo_ready, b + 1)
                    pe.wait_ge(keys_lo_ready, b + 1)
                if isinstance(b, int) and b == 0 and t < 2:
                    pe.wait_ge(exp_done, 8 * B)
                else:
                    pe.wait_ge(xsub_done, 4 * b + t - 1)
                n = slice(128 * t, 128 * t + 128)
                split_product(score[t % 2][:], xq_hi[:, n], xq_lo[:, n], keys_hi[p][:], keys_lo[p][:], True, True).then_inc(xscore_done, 1)

            def turn_xprob(b, t):
                pe.wait_ge(xprob_ready, 4 * b + t + 1)
                if t > 1 or not isinstance(b, int) or b > 0:
                    pe.wait_ge(xprobT_ready, 4 * b + t - 1)
                for j in range(XH // HPT):
                    m = pe.transpose(turn[t % 2][:, 128 * j:128 * j + 128], xprob[t][:, HPT * j:HPT * (j + 1)].rearrange("n h k -> n (h k)"), ident[:])
                m.then_inc(xprob_turned, 1)

            def cross_pv(b, p, t):
                pe.wait_ge(xprobT_ready, 4 * b + t + 1)
                if t == 0:
                    pe.wait_ge(values_ready, b + 1)
                    if isinstance(b, int) and b == 0:
                        pe.wait_ge(attn_normed, 2 * B)
                    else:
                        pe.wait_ge(xo_lo_ready, b)
                n = slice(128 * t, 128 * t + 128)
                for j in range(XH // HPT):
                    m = pe.matmul(out_b[32 * j:32 * j + 32, n], values[p][:, j].rearrange("k h d -> k (h d)"), xprobT[t % 2][:, j], start=True, stop=True)
                m.then_inc(xpv_done, 1)

            def cross_m(b):
                pe.wait_ge(xo_lo_ready, b + 1)
                split_product(out_a[:], wm_hi[:], wm_lo[:], xo_hi[:], xo_lo[:], True, True).then_inc(wm_done, 1)

            def turn_x2(b):
                pe.wait_ge(x2s_ready, b + 1)
                if not isinstance(b, int) or b > 0:
                    pe.wait_ge(x2T_lo_ready, b)
                for c in range(KC):
                    m = pe.transpose(qkv_ps[:, 128 * c:128 * c + 128], x2s[:, 128 * c:128 * c + 128], ident[:])
                m.then_inc(x2_turned, 1)

            pe.wait_ge(cross_in, 16 * 11)
            pe.wait_ge(cross_lo, 2)
            pe.wait_ge(cross_masks, 1)
            pe.wait_ge(oT_lo_ready, B)
            pe.wait_ge(rope_read, B)
            pe.wait_ge(v_ready, B)
            for c in range(KC):
                m = pe.matmul(qkv_ps[0:1, 0:2 * XK], ones_col[:], proj[:, c], start=(c == 0), stop=(c == KC - 1))
            m.then_inc(proj_summed, 1)
            pe.wait_ge(proj_sums, 2)

            def cross_step(b, p):
                first, final = isinstance(b, int) and b == 0, isinstance(b, int) and b == B - 1
                if not final:
                    context(b + 1, 1 - p)
                cross_score(b, p, 2)
                if not first:
                    cross_m(b - 1)
                if not final:
                    keys_values(b + 1)
                cross_score(b, p, 3)
                if not final:
                    cross_q(b + 1)
                turn_xprob(b, 0)
                turn_xprob(b, 1)
                cross_pv(b, p, 0)
                turn_xprob(b, 2)
                cross_pv(b, p, 1)
                if not first:
                    turn_x2(b - 1)
                turn_xprob(b, 3)
                cross_pv(b, p, 2)
                if not final:
                    cross_score(b + 1, 1 - p, 0)
                cross_pv(b, p, 3)
                if not final:
                    cross_score(b + 1, 1 - p, 1)

            context(0, 0)
            keys_values(0)
            cross_q(0)
            cross_score(0, 0, 0)
            cross_score(0, 0, 1)

            def logits(half):
                pe.wait_ge(x2T_lo_ready, HB * (half + 1))
                if half == 0:
                    pe.wait_ge(gate_lo_ready, 1)
                for c in range(KC):
                    last = split_product(qkv_ps[0:NE, 0:HB * 128], gate_hi[:, c], gate_lo[:, c],
                                         x2T_hi[:, c].rearrange("f b s -> f (b s)"), x2T_lo[:, c].rearrange("f b s -> f (b s)"), c == 0, c == KC - 1)
                last.then_inc(logits_done, 1)

            def turn_logits(half):
                pe.wait_ge(logitT_ready, half + 1)
                for k in range(HB):
                    m = pe.transpose(qkv_ps[:, NE * k:NE * (k + 1)], logitT[:, 128 * k:128 * (k + 1)], ident[0:NE, 0:NE])
                m.then_inc(logits_turned, 1)

            def ranks(half):
                pe.wait_ge(chosen_ready, half + 1)
                pe.wait_ge(tri_ready, 2)
                b0 = HB * half
                dst = qkv_ps[:, 0:HB * NE]
                pe.matmul(dst, tri_bf[:], chosen_bf[:].rearrange("t b e -> t (b e)"), start=True, stop=False)
                m = pe.matmul(dst, ones_bf[:], before_bf[:, b0:b0 + HB].rearrange("t b e -> t (b e)"), start=False, stop=True)
                if half == 1:
                    m = pe.matmul(qkv_ps[:, 512:512 + NE], ones_bf[:], before_bf[:, B], start=True, stop=True)
                m.then_inc(ranks_done, 1)

            def shared_gate_up(half, f):
                for j, (bank_, first_) in enumerate(((score[f], sh_gate_done), (turn[f], sh_up_done))):
                    for c in range(KC):
                        w = slice(FF * j + 128 * f, FF * j + 128 * (f + 1))
                        last = split_product(bank_[:], w_hi[:, 1, c, w], w_lo[:, 1, c, w],
                                             x2T_hi[:, c].rearrange("f b s -> f (b s)"), x2T_lo[:, c].rearrange("f b s -> f (b s)"), c == 0, c == KC - 1)
                    last.then_inc(first_, 1)

            def shared_down(half, k):
                if k > 1:
                    pe.wait_ge(base_ready, HB * half + k - 1)
                for f in range(FC):
                    t_ = slice(128 * k, 128 * (k + 1))
                    last = split_product((out_a, out_b)[k % 2][:], shT_hi[:, f, t_], shT_lo[:, f, t_], w_hi[:, 1, KC + f], w_lo[:, 1, KC + f], f == 0, f == FC - 1)
                last.then_inc(sh_down_done, 1)

            def route_half(half):
                pe.wait_ge(xo_lo_ready, (HB + 1, B)[half])
                if half == 0:
                    pe.wait_ge(xq_lo_ready, HB + 2)
                    pe.wait_ge(xsub_done, 4 * (HB + 1) + 2)
                else:
                    pe.wait_ge(y2_ready, B)
                logits(half)
                pe.wait_ge(sh_lo_ready, WCH)
                shared_gate_up(half, 0)
                turn_logits(half)
                shared_gate_up(half, 1)
                ranks(half)
                pe.wait_ge(shT_lo_ready, FC * (half + 1))
                for k in range(HB):
                    shared_down(half, k)
                pe.wait_ge(base_ready, HB * (half + 1))

            cross_step(0, 0)
            with pe.Fori(0, HB // 2) as i:
                cross_step(i * 2 + 1, 1)
                cross_step(i * 2 + 2, 0)
            route_half(0)
            for b in range(HB + 1, B):
                cross_step(b, b % 2)
            cross_m(B - 1)
            turn_x2(B - 1)
            route_half(1)

            def turn_slot(t, q):
                pe.wait_ge(xs_loaded[q], 8 * (t - q) + 16)
                if isinstance(t, int) and t == 0:
                    pe.wait_ge(sh_z_ready, 2 * FC)
                else:
                    pe.wait_ge(xs_lo_ready, t)
                for c in range(KC):
                    m = pe.transpose(turn[0][:, 128 * c:128 * (c + 1)], xs_in[q][:, 128 * c:128 * (c + 1)], ident[:])
                m.then_inc(xs_turned, 1)

            def slot_gate_up(t, q):
                e = pe.value_load(tab[0:1, 0, bass.ds(t, 1)], min_val=0, max_val=NE - 1)
                buf = pe.value_load(tab[0:1, 1, bass.ds(t, 1)], min_val=0, max_val=1)
                pe.wait_ge(w_lo_ready, e * WCH + WCH)
                pe.wait_ge(xs_lo_ready, t + 1)
                if not isinstance(t, int) or t > 1:
                    pe.wait_ge(z_ready, t - 1)
                for c in range(KC):
                    last = split_product(score[q][:], xsT_hi[q][:, c], xsT_lo[q][:, c],
                                         w_hi[:, bass.ds(buf, 1), c].rearrange("k o n -> k (o n)"),
                                         w_lo[:, bass.ds(buf, 1), c].rearrange("k o n -> k (o n)"), c == 0, c == KC - 1)
                last.then_inc(gate_up_done, 1)

            def turn_z(t):
                pe.wait_ge(z_ready, t + 1)
                if not isinstance(t, int) or t > 0:
                    pe.wait_ge(zT_lo_ready, t)
                for f in range(FC):
                    m = pe.transpose(turn[1][:, 128 * f:128 * (f + 1)], z[:, 128 * f:128 * (f + 1)], ident[:])
                m.then_inc(z_turned, 1)

            def slot_down(t, q):
                buf = pe.value_load(tab[0:1, 1, bass.ds(t, 1)], min_val=0, max_val=1)
                pe.wait_ge(zT_lo_ready, t + 1)
                if isinstance(t, int) and t < 2:
                    pe.wait_ge(base_ready, B)
                else:
                    pe.wait_ge(y_copied, t - 1)
                for f in range(FC):
                    last = split_product((out_a, out_b)[q][:], zT_hi[:, f], zT_lo[:, f],
                                         w_hi[:, bass.ds(buf, 1), KC + f].rearrange("k o n -> k (o n)"),
                                         w_lo[:, bass.ds(buf, 1), KC + f].rearrange("k o n -> k (o n)"), f == 0, f == FC - 1)
                last.then_inc(slot_done, 1)

            pe.wait_ge(tables_ready, 1)
            turn_slot(0, 0)

            def step(t, q):
                slot_gate_up(t, q)
                if not isinstance(t, int) or t < SLOTS - 1:
                    turn_slot(t + 1, 1 - q)
                if not isinstance(t, int) or t > 0:
                    slot_down(t - 1, 1 - q)
                turn_z(t)

            step(0, 0)
            step(1, 1)
            step(2, 0)
            with pe.Fori(1, (SLOTS - 3) // 2) as i:
                step(i * 2 + 1, 1)
                step(i * 2 + 2, 0)
            step(SLOTS - 2, 1)
            step(SLOTS - 1, 0)
            slot_down(SLOTS - 1, 0)

        @block.vector
        def _(dve):
            dve.memset(stack[:].bitcast(F32)[:, 0:NQ, 3, :], 0.0)
            dve.memset(stack[:].bitcast(F32)[:, NQ:, 3, 2:], 0.0)
            dve.memset(neg_max_parts[:].bitcast(F32)[:, 2:4], 0.0)
            dve.memset(stack[:].bitcast(F32)[:, NQ:, 3, 0:2], 1.0).then_inc(consts_ready, 1)
            for p in (0, 1):
                dve.memset(v_ones[p][:, :, HD:HD + 1], 1.0)
                dve.memset(v_ones[p][:, :, HD + 1:], 0.0)
            dve.memset(eps[:], EPS)
            dve.memset(neg_half[:], -0.5).then_inc(consts_ready, 1)
            dve.wait_ge(consts_in, 48)
            dve.tensor_copy(ident_bf[:], ident[:]).then_inc(consts_ready, 1)
            dve.tensor_copy(causal_bf[:], causal[:].rearrange("s (o t) -> s o t", o=1).to_broadcast([128, REP, 128])).then_inc(consts_ready, 1)

            def x_lo(b, p):
                dve.wait_ge(xT_hi_ready, b + 1)
                if not isinstance(b, int) or b > 1:
                    dve.wait_ge(qkv_done, b - 1)
                dve.tensor_tensor(xT_lo[p][:], xT[:, p], xT_hi[p][:].bitcast(F32), ALU.subtract).then_inc(xT_lo_ready, 1)

            def rope_products(b, p):
                dve.wait_ge(qkv_done, b + 1)
                if not isinstance(b, int) or b > 0:
                    dve.wait_ge(rot_ready, 2 * b)
                qk = qkv_ps[:, 0:QK_HEADS * HD].rearrange("s (h e) -> s h e", e=HD)
                for j, dst in ((0, rope_cos), (1, rope_sin)):
                    f = rope[:, j:j + 1].to_broadcast([128, QK_HEADS, HD])
                    m = dve.tensor_tensor(dst[:].rearrange("s h a e -> s h (a e)"), qk, f, ALU.mult)
                m.then_inc(rope_read, 1)

            def low_parts(b):
                dve.wait_ge(stack_hi, 2 * b + 2)
                dve.tensor_tensor(stack[:, 0:NQ, 2], rotated[:, 0:NQ], stack[:, 0:NQ, 0].bitcast(F32), ALU.subtract).then_inc(stack_lo, 1)
                dve.tensor_tensor(stack[:, NQ:, 1], rotated[:, NQ:], stack[:, NQ:, 0].bitcast(F32), ALU.subtract).then_inc(stack_lo, 1)

            def qkT_copies(b, p):
                for r in range(5):
                    dst = kT[p][:] if r == 0 else qT[p][:, 4 * r - 4:4 * r]
                    if r % 2:
                        dve.wait_ge(qkT_turned, 5 * b + r + 1)
                        dve.tensor_copy(dst.rearrange("k r s -> k (r s)"), turn[1][:]).then_inc(qkT_by_dve, 1)
                        dve.wait_ge(qkT_by_dve, 2 * b + r // 2 + 1)
                    else:
                        dve.wait_ge(qkT_by_act, 3 * b + r // 2 + 1)
                    if r == 0:
                        dve.tensor_copy(kT_half[:], dst.bitcast(F32)).then_inc(halves_ready, 1)
                    else:
                        dve.tensor_copy(qT_half[:, 4 * r - 4:4 * r], dst.bitcast(F32)).then_inc(halves_ready, 1)

            def maxima(b):
                for g in range(NKV):
                    dve.wait_ge(pass1_done, 8 * b + g + 1)
                    dve.tensor_reduce(neg_max[:, g], score[g % 2][:].rearrange("s (r t) -> s r t", r=REP), AX.X, ALU.max,
                                      negate=True).then_inc(max_done, 1)
                    if not isinstance(b, int) or b > 0:
                        if g == 3:
                            normalise(b - 1, 0)
                            normalise(b - 1, 1)
                        if g == 6:
                            o_lo(b - 1)
                dve.wait_ge(max_done, 8 * b + 8)
                nm = neg_max[:].rearrange("s (u a) r -> s a u r", a=2)
                dve.tensor_copy(neg_max_parts[:, 0:2, 0], nm).then_inc(max_hi, 1)
                dve.wait_ge(max_hi, b + 1)
                dve.tensor_tensor(neg_max_parts[:, 0:2, 1], nm, neg_max_parts[:, 0:2, 0].bitcast(F32), ALU.subtract).then_inc(max_parts, 1)

            def normalise(b, half):
                src = (out_a, out_b)[half][:].rearrange("s (r j e) -> s r j e", r=REP, e=32)
                rs = attn_rsum[:, half]
                dve.wait_ge(pv_turned, 2 * b + half + 1)
                dve.reciprocal(rs, src[:, :, :, HD]).then_inc(rsum_ready, 1)
                dve.wait_ge(rsum_ready, 2 * b + half + 1)
                if not isinstance(b, int) or b > 0:
                    dve.wait_ge(oT_turned, b)
                dst = attn_out[:, half].rearrange("s (j r) e -> s r j e", r=REP)
                dve.tensor_tensor(dst, src[:, :, :, 0:HD], rs.rearrange("s r (j o) -> s r j o", o=1).to_broadcast([128, REP, 4, HD]),
                                  ALU.mult).then_inc(attn_normed, 1)

            def o_lo(b):
                dve.wait_ge(oT_hi_ready, b + 1)
                if not isinstance(b, int) or b > 0:
                    dve.wait_ge(wo_done, b)
                dve.tensor_tensor(oT_lo[:].rearrange("k c s -> k (c s)"), turn[1][:], oT_hi[:].rearrange("k c s -> k (c s)").bitcast(F32),
                                  ALU.subtract).then_inc(oT_lo_ready, 1)

            def residual1(b, p):
                dve.wait_ge(wo_done, b + 1)
                dve.wait_ge(x_loaded[p], 8 * (b - p) + 16)
                dve.tensor_tensor(y1[:], out_a[:], x_in[:, p], ALU.add).then_inc(y1_ready, 1)
                dve.wait_ge(y1_ready, b + 1)
                dve.bn_stats(bn6[:], y1[:]).then_inc(stats1, 1)
                dve.wait_ge(stats1, b + 1)
                dve.sem_inc(passed)
                dve.bn_aggr(mean_var[:], bn6[:]).then_inc(mv1, 1)

            def x1_write(b):
                dve.wait_ge(rstd1, b + 1)
                dve.wait_ge(mv1, b + 1)
                dve.tensor_scalar(x1[:, bass.ds(b, 1)].rearrange("s o d -> s (o d)"), y1[:], mean_var[:, 0:1], rstd[:, 0:1],
                                  ALU.subtract, ALU.mult).then_inc(x1_ready, 1)

            x_lo(0, 0)
            for c in range(KC):
                dve.wait_ge(wqkv_hi_ready, c + 1)
                dve.tensor_tensor(wqkv_lo[:, c], wst[:, c], wqkv_hi[:, c].bitcast(F32), ALU.subtract).then_inc(wqkv_lo_ready, 1)
            x_lo(1, 1)
            dve.wait_ge(wo_hi_ready, 1)
            dve.tensor_tensor(wo_lo[:], wo_in[:], wo_hi[:].bitcast(F32), ALU.subtract).then_inc(wo_lo_ready, 1)
            rope_products(0, 0)
            low_parts(0)
            qkT_copies(0, 0)

            def step(b, p):
                first, final = isinstance(b, int) and b == 0, isinstance(b, int) and b == B - 1
                maxima(b)
                if not final:
                    rope_products(b + 1, 1 - p)
                if not first:
                    residual1(b - 1, 1 - p)
                if not final:
                    low_parts(b + 1)
                if not first:
                    x1_write(b - 1)
                if not final:
                    qkT_copies(b + 1, 1 - p)
                if not (isinstance(b, int) and b >= B - 2):
                    x_lo(b + 2, p)

            step(0, 0)
            with dve.Fori(0, (B - 4) // 2) as i:
                step(i * 2 + 1, 1)
                step(i * 2 + 2, 0)
            step(B - 3, 1)
            step(B - 2, 0)
            step(B - 1, 1)
            normalise(B - 1, 0)
            normalise(B - 1, 1)
            o_lo(B - 1)
            residual1(B - 1, 1)
            x1_write(B - 1)

            dve.wait_ge(wo_done, B)
            dve.wait_ge(max_rows, 32 * B)
            dve.memset(ones_col[:], 1.0).then_inc(cross_masks, 1)
            for j, (w, hi, lo) in enumerate(((wq_in, wq_hi, wq_lo), (wm_in, wm_hi, wm_lo))):
                dve.wait_ge(cross_hi, j + 1)
                dve.tensor_tensor(lo[:], w[:], hi[:].bitcast(F32), ALU.subtract).then_inc(cross_lo, 1)

            def head_keys(b, p):
                dve.wait_ge(kv_done, b + 1)
                if not isinstance(b, int) or b > 0:
                    dve.wait_ge(keys_lo_ready, b)
                    dve.wait_ge(keys_hi_ready, b)
                k = k_ps.rearrange("c (o k) -> c o k", o=1).to_broadcast([128, XH, XK])
                dve.tensor_tensor(keys[:], k, head_mask[:].rearrange("c (h o) -> c h o", o=1).to_broadcast([128, XH, XK]), ALU.mult).then_inc(keys_ready, 1)
                if not isinstance(b, int) or b > 1:
                    dve.wait_ge(xpv_done, 4 * b - 4)
                v = v_ps.rearrange("k (j h d) -> k j h d", j=XH // HPT, h=HPT)
                vm = value_mask[:].rearrange("k (a h d) -> k a h d", a=1, d=1).to_broadcast([128, XH // HPT, HPT, XD])
                dve.tensor_tensor(values[p][:], v, vm, ALU.mult).then_inc(values_ready, 1)

            def keys_low(b, p):
                dve.wait_ge(keys_hi_ready, b + 1)
                dve.tensor_tensor(keys_lo[p][:], keys[:].rearrange("c h k -> c (h k)"), keys_hi[p][:].bitcast(F32), ALU.subtract).then_inc(keys_lo_ready, 1)

            def x1_low(b):
                dve.wait_ge(x1_hi_ready, b + 1)
                dve.tensor_tensor(x1_lo[:], x1[:, bass.ds(b, 1)].rearrange("s o d -> s (o d)"), x1_hi[:].bitcast(F32), ALU.subtract).then_inc(x1_lo_ready, 1)

            def xq_low(b):
                dve.wait_ge(xq_hi_ready, b + 1)
                dve.scalar_tensor_tensor(out=xq_lo[:], in0=out_a[:], scalar=bias_q[:, 0:1], in1=xq_hi[:].bitcast(F32), op0=ALU.add, op1=ALU.subtract).then_inc(xq_lo_ready, 1)

            def xmax_sub(b, t):
                dve.wait_ge(xscore_done, 4 * b + t + 1)
                sc = score[t % 2][:].rearrange("n (h k) -> n h k", k=XK)
                dve.tensor_reduce(xmax[:, t], sc, AX.X, ALU.max).then_inc(xmax_ready, 1)
                dve.wait_ge(xmax_ready, 4 * b + t + 1)
                if not isinstance(b, int) or b > 0:
                    dve.wait_ge(xprob_turned, 4 * b + t - 3)
                dve.tensor_tensor(xprob[t][:], sc, xmax[:, t].rearrange("n (h o) -> n h o", o=1).to_broadcast([128, XH, XK]), ALU.subtract).then_inc(xsub_done, 1)

            def xsum_rec(b, t):
                dve.wait_ge(xexp_done, 4 * b + t + 1)
                if not isinstance(b, int) or b > 0:
                    dve.wait_ge(xprob_ready, 4 * b + t - 3)
                dve.tensor_reduce(xsum[:, t], xprob[t][:], AX.X, ALU.add).then_inc(xsum_ready, 1)
                dve.wait_ge(xsum_ready, 4 * b + t + 1)
                dve.reciprocal(xrec[:, t], xsum[:, t]).then_inc(xrec_ready, 1)

            def xo_low(b):
                dve.wait_ge(xo_hi_ready, b + 1)
                dve.tensor_tensor(xo_lo[:], out_b[:], xo_hi[:].bitcast(F32), ALU.subtract).then_inc(xo_lo_ready, 1)

            def residual2(b):
                dve.wait_ge(wm_done, b + 1)
                if not isinstance(b, int) or b > 0:
                    dve.wait_ge(x2s_ready, b)
                dve.scalar_tensor_tensor(out=y2[:], in0=out_a[:], scalar=bias_m[:, 0:1], in1=x1[:, bass.ds(b, 1)].rearrange("s o d -> s (o d)"),
                                         op0=ALU.add, op1=ALU.add).then_inc(y2_ready, 1)
                dve.wait_ge(y2_ready, b + 1)
                dve.bn_stats(bn6b[:], y2[:]).then_inc(stats2, 1)
                dve.wait_ge(stats2, b + 1)
                dve.sem_inc(passed)
                dve.bn_aggr(mean_var2[:], bn6b[:]).then_inc(mv2, 1)

            def x2_write(b):
                dve.wait_ge(rstd2_ready, b + 1)
                dve.wait_ge(mv2, b + 1)
                if not isinstance(b, int) or b > 0:
                    dve.wait_ge(x2_turned, b)
                    dve.wait_ge(x2_ready, b)
                dve.tensor_scalar(x2s[:], y2[:], mean_var2[:, 0:1], rstd2[:, 0:1], ALU.subtract, ALU.mult).then_inc(x2s_ready, 1)

            def x2T_low(b):
                dve.wait_ge(x2T_hi_ready, b + 1)
                lo, hi = (half_place(t, b) for t in (x2T_lo, x2T_hi))
                dve.tensor_tensor(lo, qkv_ps[:, 0:D].rearrange("f (c s) -> f c s", c=KC), hi.bitcast(F32), ALU.subtract).then_inc(x2T_lo_ready, 1)

            def cross_step(b, p):
                first, final = isinstance(b, int) and b == 0, isinstance(b, int) and b == B - 1
                if not final:
                    x1_low(b + 1)
                xsum_rec(b, 0)
                xmax_sub(b, 2)
                xsum_rec(b, 1)
                if not first:
                    residual2(b - 1)
                xmax_sub(b, 3)
                xsum_rec(b, 2)
                if not final:
                    head_keys(b + 1, 1 - p)
                xsum_rec(b, 3)
                if not first:
                    x2_write(b - 1)
                if not final:
                    xq_low(b + 1)
                    keys_low(b + 1, 1 - p)
                if not first:
                    x2T_low(b - 1)
                if not final:
                    xmax_sub(b + 1, 0)
                xo_low(b)
                if not final:
                    xmax_sub(b + 1, 1)

            dve.wait_ge(cross_in, 16 * 11)
            x1_low(0)
            head_keys(0, 0)
            keys_low(0, 0)
            xq_low(0)
            xmax_sub(0, 0)
            xmax_sub(0, 1)

            routed = [0]

            def link(ins):
                routed[0] += 1
                ins.then_inc(route, 1)
                dve.wait_ge(route, routed[0])

            def wide(ap, n):
                return ap.rearrange("t (b o) -> t b o", o=1).to_broadcast([128, HB, n])

            def choose(half):
                bs = slice(HB * half, HB * (half + 1))
                dve.wait_ge(logit_exp, half + 1)
                link(dve.tensor_scalar(e_score[:], e_score[:], 1.0, None, ALU.add))
                link(dve.reciprocal(e_score[:], e_score[:]))
                link(dve.tensor_tensor(e_score[:], e_score[:], bias_e[:].rearrange("t (o e) -> t o e", o=1).to_broadcast([128, HB, NE]), ALU.add))
                for j in range(TOPK):
                    best, one = weight[:, j, bs], picked[:, j, bs]
                    link(dve.tensor_reduce(best, e_score[:], AX.X, ALU.max))
                    link(dve.tensor_tensor(e_eq[:], e_score[:], wide(best, NE), ALU.is_equal))
                    io = iota16[:].rearrange("t (o e) -> t o e", o=1).to_broadcast([128, HB, NE])
                    link(dve.tensor_tensor(e_eq[:], e_eq[:], io, ALU.mult))
                    link(dve.tensor_reduce(e_low[:], e_eq[:], AX.X, ALU.min))
                    link(dve.tensor_tensor(one, io, wide(e_low[:], NE), ALU.is_equal))
                    link(dve.scalar_tensor_tensor(out=e_score[:], in0=one, scalar=MASKED, in1=e_score[:], op0=ALU.mult, op1=ALU.add))
                link(dve.tensor_scalar(chosen[:], e_score[:], MASKED / 10, None, ALU.is_lt))
                link(dve.tensor_copy(chosen_bf[:], chosen[:]))
                for k in range(HB):
                    b = HB * half + k
                    link(dve.tensor_tensor(before[:, b + 1], before[:, b], chosen[:, k], ALU.add))
                m = dve.tensor_copy(before_bf[:, HB * half:HB * (half + 1) + 1], before[:, HB * half:HB * (half + 1) + 1])
                m.then_inc(chosen_ready, 1)
                link(dve.tensor_reduce(w_sum[:], weight[:, :, bs].rearrange("t j b -> t b j"), AX.X, ALU.add))
                link(dve.tensor_scalar(w_sum[:], w_sum[:], 1e-20, None, ALU.add))
                link(dve.reciprocal(w_rec[:], w_sum[:]))
                link(dve.tensor_tensor(weight[:, :, bs], weight[:, :, bs], w_rec[:].rearrange("t (o b) -> t o b", o=1).to_broadcast([128, TOPK, HB]), ALU.mult))

            def place_rows(half):
                bs = slice(HB * half, HB * (half + 1))
                dve.wait_ge(ranks_done, half + 1)
                m = dve.tensor_copy(rank[:, bs], qkv_ps[:, 0:HB * NE].rearrange("t (b e) -> t b e", e=NE))
                link(m)
                if half == 1:
                    link(dve.tensor_copy(count[:], qkv_ps[:, 512:512 + NE]))
                link(dve.tensor_tensor(place[:, bs], rank[:, bs], region[:].rearrange("t (o e) -> t o e", o=1).to_broadcast([128, HB, NE]), ALU.add))
                for j in range(TOPK):
                    link(dve.tensor_tensor(picked_place[:, j, bs], picked[:, j, bs], place[:, bs], ALU.mult))
                link(dve.tensor_reduce(row_f[:, :, bs], picked_place[:, :, bs], AX.X, ALU.add))
                dve.tensor_copy(row_of[:, :, bs], row_f[:, :, bs]).then_inc(rows_ready, 1)

            def slot_tables():
                cb = count[:].rearrange("t (e o) -> t e o", o=1).to_broadcast([128, NE, 8])
                link(dve.tensor_tensor(over[:], cb, thresholds[:].rearrange("t (o k) -> t o k", o=1).to_broadcast([128, NE, 8]), ALU.is_gt))
                link(dve.tensor_reduce(n_slots[:], over[:], AX.X, ALU.add))
                nb = n_slots[:].rearrange("t (o e) -> t o e", o=1)
                link(dve.tensor_tensor(prod[:], nb.to_broadcast([128, NE, NE]), upto_mask[:], ALU.mult))
                link(dve.tensor_reduce(slots_to[:], prod[:], AX.X, ALU.add))
                link(dve.tensor_tensor(slot_base[:], slots_to[:], n_slots[:], ALU.subtract))
                sn = slot_no[:].rearrange("t (s o) -> t s o", o=1).to_broadcast([1, SLOTS, NE])
                link(dve.tensor_tensor(passed_e[:], slots_to[0:1].rearrange("t (o e) -> t o e", o=1).to_broadcast([1, SLOTS, NE]), sn, ALU.is_le))
                f = tab_f
                link(dve.memset(f[:], -1.0))
                link(dve.tensor_reduce(f[:, 0, 1:], passed_e[:, :, 0:NE - 1], AX.X, ALU.add))
                link(dve.tensor_reduce(f[:, 1, 1:], passed_e[:], AX.X, ALU.add))
                link(dve.tensor_reduce(f[:, 2, 1:], passed_e[:, :, 0:NE - 2], AX.X, ALU.add))
                link(dve.tensor_tensor(passed_w[:], passed_e[:], alternate[:].rearrange("t (o e) -> t o e", o=1).to_broadcast([1, SLOTS, NE]), ALU.mult))
                link(dve.tensor_reduce(f[:, 3, 1:], passed_w[:], AX.X, ALU.add))
                link(dve.tensor_tensor(passed_w[:], passed_e[:], nb[0:1].to_broadcast([1, SLOTS, NE]), ALU.mult))
                link(dve.tensor_reduce(f[:, 4, 1:], passed_w[:], AX.X, ALU.add))
                link(dve.tensor_tensor(f[:, 4, 1:], slot_no[:], f[:, 4, 1:], ALU.subtract))
                link(dve.tensor_scalar(f[:, 4, 1:], f[:, 4, 1:], float(SLOT), None, ALU.mult))
                link(dve.scalar_tensor_tensor(out=f[:, 5, 1:], in0=f[:, 1, 1:], scalar=float(REGION), in1=f[:, 4, 1:], op0=ALU.mult, op1=ALU.add))
                link(dve.tensor_tensor(f[:, 4, 1:], f[:, 2, 1:], f[:, 2, 0:SLOTS], ALU.subtract))
                link(dve.tensor_tensor(pad_f[:], count[0:1], region[0:1], ALU.add))
                dve.tensor_copy(tab[:, 0], f[:, 0, 1:])
                dve.tensor_copy(tab[:, 1], f[:, 3, 1:])
                dve.tensor_scalar(tab[:, 2], f[:, 5, 1:], float(IDLE_ROW), None, ALU.min)
                dve.tensor_copy(tab[:, 3], f[:, 4, 1:])
                dve.tensor_copy(pad_row[:], pad_f[:]).then_inc(tables_ready, 1)

            def result_rows():
                link(dve.tensor_scalar(slot_base[:], slot_base[:], float(SLOT), None, ALU.mult))
                link(dve.tensor_tensor(place[:], rank[:], slot_base[:].rearrange("t (o e) -> t o e", o=1).to_broadcast([128, B, NE]), ALU.add))
                for j in range(TOPK):
                    link(dve.tensor_tensor(picked_place[:, j], picked[:, j], place[:], ALU.mult))
                link(dve.tensor_reduce(row_f[:], picked_place[:], AX.X, ALU.add))
                dve.tensor_copy(yrow_of[:], row_f[:]).then_inc(yrows_ready, 1)

            def split_low(buf, hi_sem, lo_sem, have, chunks=range(WCH)):
                for c in chunks:
                    dve.wait_ge(hi_sem, have + c + 1)
                    dve.sem_inc(passed)
                    raw, hi, lo = (w[:, bass.ds(buf, 1), bass.ds(c, 1)].rearrange("k o c n -> k (o c n)") for w in (w_raw, w_hi, w_lo))
                    dve.tensor_tensor(lo, raw, hi.bitcast(F32), ALU.subtract).then_inc(lo_sem, 1)

            def shared_z(half, f):
                n = FC * half + f
                dve.wait_ge(sh_silu_done, n + 1)
                dve.wait_ge(sh_up_done, n + 1)
                dve.tensor_tensor(sh_z[:], turn[f][:], sh_z[:], ALU.mult).then_inc(sh_z_ready, 1)
                dve.wait_ge(shT_hi_ready, n + 1)
                dve.tensor_tensor(shT_lo[:, f], sh_z[:], shT_hi[:, f].bitcast(F32), ALU.subtract).then_inc(shT_lo_ready, 1)

            def shared_base(half, k):
                b = HB * half + k
                dve.wait_ge(sh_down_done, b + 1)
                dve.wait_ge(x2_ready, b + 1)
                dve.tensor_tensor(base[:, b], (out_a, out_b)[k % 2][:], x2[:, b], ALU.add).then_inc(base_ready, 1)

            dve.memset(before[:, 0], 0.0)
            dve.memset(ones_bf[:], 1.0).then_inc(tri_ready, 1)
            dve.memset(zeros[:], 0.0).then_inc(zeros_ready, 1)
            dve.wait_ge(moe_in, 16 * 9)
            dve.tensor_copy(tri_bf[:], tri[:]).then_inc(tri_ready, 1)
            dve.wait_ge(gate_hi_ready, 1)
            dve.tensor_tensor(gate_lo[:], gate_in[:], gate_hi[:].bitcast(F32), ALU.subtract).then_inc(gate_lo_ready, 1)

            def route_half(half):
                dve.wait_ge(logits_done, half + 1)
                if half == 1:
                    dve.wait_ge(logits_turned, 1)
                dve.tensor_copy(logitT[:], qkv_ps[0:NE, 0:HB * 128]).then_inc(logitT_ready, 1)
                shared_z(half, 0)
                choose(half)
                shared_z(half, 1)
                place_rows(half)
                if half == 1:
                    slot_tables()
                for k in range(HB):
                    shared_base(half, k)

            cross_step(0, 0)
            with dve.Fori(0, HB // 2) as i:
                cross_step(i * 2 + 1, 1)
                split_low(1, sh_hi_ready, sh_lo_ready, 0, [i * 3 + c for c in range(WCH // 2)])
                cross_step(i * 2 + 2, 0)
            route_half(0)
            for b in range(HB + 1, B):
                cross_step(b, b % 2)
                k = 2 * (b - HB - 1)
                split_low(0, w_hi_ready, w_lo_ready, 0, range(k, k + 2))
            residual2(B - 1)
            x2_write(B - 1)
            x2T_low(B - 1)
            route_half(1)
            result_rows()

            def slot_x_low(t, q):
                dve.wait_ge(xs_hi_ready, t + 1)
                if not isinstance(t, int) or t > 1:
                    dve.wait_ge(gate_up_done, t - 1)
                dve.tensor_tensor(xsT_lo[q][:].rearrange("f c s -> f (c s)"), turn[0][:], xsT_hi[q][:].rearrange("f c s -> f (c s)").bitcast(F32),
                                  ALU.subtract).then_inc(xs_lo_ready, 1)

            def slot_z(t, q):
                dve.wait_ge(silu_done, t + 1)
                if not isinstance(t, int) or t > 0:
                    dve.wait_ge(z_turned, t)
                dve.tensor_tensor(z[:], silu_g[:], score[q][:, FF:2 * FF], ALU.mult).then_inc(z_ready, 1)

            def slot_z_low(t):
                dve.wait_ge(zT_hi_ready, t + 1)
                if not isinstance(t, int) or t > 0:
                    dve.wait_ge(slot_done, t)
                dve.tensor_tensor(zT_lo[:].rearrange("f c s -> f (c s)"), turn[1][:, 0:FF], zT_hi[:].rearrange("f c s -> f (c s)").bitcast(F32),
                                  ALU.subtract).then_inc(zT_lo_ready, 1)

            def next_expert_low(t):
                first = dve.value_load(tab[0:1, 3, bass.ds(t, 1)], min_val=0, max_val=1)
                with dve.If(first > 0):
                    e = dve.value_load(tab[0:1, 0, bass.ds(t, 1)], min_val=0, max_val=NE - 2)
                    buf = dve.value_load(tab[0:1, 1, bass.ds(t, 1)], min_val=0, max_val=1)
                    split_low(1 - buf, w_hi_ready, w_lo_ready, (e + 1) * WCH)

            slot_x_low(0, 0)

            def step(t, q):
                slot_z(t, q)
                if not isinstance(t, int) or t < SLOTS - 1:
                    slot_x_low(t + 1, 1 - q)
                slot_z_low(t)
                next_expert_low(t)

            step(0, 0)
            with dve.Fori(0, (SLOTS - 3) // 2) as i:
                step(i * 2 + 1, 1)
                step(i * 2 + 2, 0)
            step(SLOTS - 2, 1)
            step(SLOTS - 1, 0)

            def combine(b, p):
                dve.wait_ge(gathered_in[p], 32 * (b - p) + 64)
                if not isinstance(b, int) or b > 0:
                    dve.wait_ge(out_ready, b)
                for j in range(TOPK):
                    src = base[:, bass.ds(b, 1)].rearrange("s o d -> s (o d)") if j == 0 else y3
                    dve.scalar_tensor_tensor(out=y3, in0=gathered[p][:, j], scalar=weight[:, j, bass.ds(b, 1)], in1=src,
                                             op0=ALU.mult, op1=ALU.add).then_inc(combined, 1)
                    dve.wait_ge(combined, b * TOPK + j + 1)
                dve.bn_stats(bn6c[:], y3).then_inc(stats3, 1)
                dve.wait_ge(stats3, b + 1)
                dve.sem_inc(passed)
                dve.bn_aggr(mean_var3[:], bn6c[:]).then_inc(mv3, 1)
                dve.wait_ge(rstd3_ready, b + 1)
                dve.wait_ge(mv3, b + 1)
                if not isinstance(b, int) or b > 1:
                    dve.wait_ge(out_in[p], 8 * (b - p))
                dve.tensor_scalar(out_sb[p], y3, mean_var3[:, 0:1], rstd3[:, 0:1], ALU.subtract, ALU.mult).then_inc(out_ready, 1)

            combine(0, 0)
            with dve.Fori(0, (B - 2) // 2) as i:
                combine(i * 2 + 1, 1)
                combine(i * 2 + 2, 0)
            combine(B - 1, 1)

        @block.scalar
        def _(act):
            def x_hi(b, p):
                act.wait_ge(xT_in[p], 8 * (b - p) + 16)
                if not isinstance(b, int) or b > 1:
                    act.wait_ge(qkv_done, b - 1)
                act.copy(xT_hi[p][:], xT[:, p]).then_inc(xT_hi_ready, 1)

            def v_copy(b, p):
                act.wait_ge(rope_read, b + 1)
                if not isinstance(b, int) or b > 1:
                    act.wait_ge(pv_done, 8 * b - 8)
                act.copy(v_ones[p][:, :, 0:HD], qkv_ps[:, QK_HEADS * HD:QKV].rearrange("s (g e) -> s g e", e=HD)).then_inc(v_ready, 1)

            def high_parts(b):
                act.wait_ge(rot_ready, 2 * b + 2)
                if not isinstance(b, int) or b > 0:
                    act.wait_ge(qkT_turned, 5 * b)
                r = rotated[:].rearrange("s h (o e) -> s h o e", o=1)
                act.copy(stack[:, 0:NQ, 0:2], r[:, 0:NQ].to_broadcast([128, NQ, 2, HD])).then_inc(stack_hi, 1)
                act.copy(stack[:, NQ:, 0:3:2], r[:, NQ:].to_broadcast([128, NKV, 2, HD])).then_inc(stack_hi, 1)

            def qkT_copies(b, p, rounds=(0, 2, 4)):
                for r in rounds:
                    act.wait_ge(qkT_turned, 5 * b + r + 1)
                    dst = kT[p][:] if r == 0 else qT[p][:, 4 * r - 4:4 * r]
                    act.copy(dst.rearrange("k r s -> k (r s)"), turn[0][:]).then_inc(qkT_by_act, 1)

            def maxT_copy(b):
                act.wait_ge(max_turned, b + 1)
                if not isinstance(b, int) or b > 0:
                    act.wait_ge(max_rows, 32 * b)
                act.copy(maxT[:], out_b[0:64, 0:128]).then_inc(maxT_ready, 1)

            def exps(b, groups):
                for g in groups:
                    act.wait_ge(pass2_done, 8 * b + g + 1)
                    if g >= 4 or not isinstance(b, int) or b > 0:
                        act.wait_ge(pv_done, 8 * b + g - 3)
                    act.activation(probs[g % 4][:].rearrange("t r s -> t (r s)"), score[g % 2][:], ACT.Exp,
                                   scale=float(HD) ** -0.5).then_inc(exp_done, 1)

            def pv_copy(b, half):
                act.wait_ge(pv_done, 8 * b + 4 * half + 4)
                if not isinstance(b, int) or b > 0:
                    act.wait_ge(pv_turned, 2 * b)
                act.copy(pv_sb[half][:].rearrange("k r s -> k (r s)"), (out_a, out_b)[half][:]).then_inc(pv_copied, 1)

            def o_hi(b):
                act.wait_ge(oT_turned, b + 1)
                if not isinstance(b, int) or b > 0:
                    act.wait_ge(wo_done, b)
                act.copy(oT_hi[:].rearrange("k c s -> k (c s)"), turn[1][:]).then_inc(oT_hi_ready, 1)

            x_hi(0, 0)
            for c in range(KC):
                act.wait_ge(wqkv_in[c], 16)
                act.copy(wqkv_hi[:, c], wst[:, c]).then_inc(wqkv_hi_ready, 1)
            x_hi(1, 1)
            act.wait_ge(wo_loaded, 16)
            act.copy(wo_hi[:], wo_in[:]).then_inc(wo_hi_ready, 1)
            v_copy(0, 0)
            high_parts(0)
            qkT_copies(0, 0)

            def step(b, p):
                final = isinstance(b, int) and b == B - 1
                if not isinstance(b, int) or b > 0:
                    pv_copy(b - 1, 0)
                    pv_copy(b - 1, 1)
                    o_hi(b - 1)
                maxT_copy(b)
                if not final:
                    v_copy(b + 1, 1 - p)
                    high_parts(b + 1)
                if not (isinstance(b, int) and b >= B - 2):
                    x_hi(b + 2, p)
                exps(b, range(NKV - 2))
                if not final:
                    qkT_copies(b + 1, 1 - p, (0,))
                exps(b, (NKV - 2,))
                exps(b, (NKV - 1,))
                if not final:
                    qkT_copies(b + 1, 1 - p, (2, 4))

            step(0, 0)
            with act.Fori(0, (B - 4) // 2) as i:
                step(i * 2 + 1, 1)
                step(i * 2 + 2, 0)
            step(B - 3, 1)
            step(B - 2, 0)
            step(B - 1, 1)

            pv_copy(B - 1, 0)
            pv_copy(B - 1, 1)
            o_hi(B - 1)

            act.wait_ge(cross_in, 16 * 11)
            act.wait_ge(wo_done, B)
            act.copy(wq_hi[:], wq_in[:]).then_inc(cross_hi, 1)
            act.copy(wm_hi[:], wm_in[:]).then_inc(cross_hi, 1)
            act.wait_ge(proj_summed, 1)
            act.copy(proj_sum_k[:], qkv_ps[0:1, 0:XK]).then_inc(proj_sums, 1)
            act.copy(proj_sum_v[:], qkv_ps[0:1, XK:2 * XK].rearrange("o (a k) -> o a k", a=1).to_broadcast([1, HPT, XK])).then_inc(proj_sums, 1)

            def ctx_copy(b):
                act.wait_ge(ctx_done, b + 1)
                if not isinstance(b, int) or b > 0:
                    act.wait_ge(kv_done, b)
                act.copy(ctx_k[:], ctx_ps[:, 0:XK]).then_inc(ctx_copied, 1)
                act.copy(ctx_v[:], ctx_ps[:, XK:2 * XK].rearrange("d (a k) -> d a k", a=1).to_broadcast([128, HPT, XK])).then_inc(ctx_copied, 1)

            def x1_high(b):
                if not isinstance(b, int) or b > 0:
                    act.wait_ge(xq_done, b)
                act.copy(x1_hi[:], x1[:, bass.ds(b, 1)].rearrange("s o d -> s (o d)")).then_inc(x1_hi_ready, 1)

            def xq_high(b):
                act.wait_ge(xq_done, b + 1)
                if not isinstance(b, int) or b > 0:
                    act.wait_ge(xscore_done, 4 * b)
                act.activation(xq_hi[:], out_a[:], ACT.Identity, bias=bias_q[:, 0:1]).then_inc(xq_hi_ready, 1)

            def keys_high(b, p):
                act.wait_ge(keys_ready, b + 1)
                if not isinstance(b, int) or b > 1:
                    act.wait_ge(xscore_done, 4 * b - 4)
                act.copy(keys_hi[p][:], keys[:].rearrange("c h k -> c (h k)")).then_inc(keys_hi_ready, 1)

            def xexp(b, t):
                act.wait_ge(xsub_done, 4 * b + t + 1)
                act.activation(xprob[t][:], xprob[t][:], ACT.Exp, scale=float(XD) ** -0.5).then_inc(xexp_done, 1)

            def xprobT_copy(b, t):
                act.wait_ge(xprob_turned, 4 * b + t + 1)
                if not (isinstance(b, int) and b == 0 and t < 2):
                    act.wait_ge(xpv_done, 4 * b + t - 1)
                act.copy(xprobT[t % 2][:], turn[t % 2][:].rearrange("k (j n) -> k j n", n=128)).then_inc(xprobT_ready, 1)

            def xo_high(b):
                act.wait_ge(xpv_done, 4 * b + 4)
                if not isinstance(b, int) or b > 0:
                    act.wait_ge(wm_done, b)
                act.copy(xo_hi[:], out_b[:]).then_inc(xo_hi_ready, 1)

            def x2T_high(b):
                act.wait_ge(x2_turned, b + 1)
                act.copy(half_place(x2T_hi, b), qkv_ps[:, 0:D].rearrange("f (c s) -> f c s", c=KC)).then_inc(x2T_hi_ready, 1)

            act.wait_ge(x1_ready, B)

            def cross_step(b, p):
                first, final = isinstance(b, int) and b == 0, isinstance(b, int) and b == B - 1
                xexp(b, 0)
                if not final:
                    x1_high(b + 1)
                    ctx_copy(b + 1)
                xexp(b, 1)
                xexp(b, 2)
                xprobT_copy(b, 0)
                xexp(b, 3)
                xprobT_copy(b, 1)
                if not final:
                    xq_high(b + 1)
                    keys_high(b + 1, 1 - p)
                xprobT_copy(b, 2)
                if not first:
                    x2T_high(b - 1)
                xprobT_copy(b, 3)
                xo_high(b)

            x1_high(0)
            ctx_copy(0)
            keys_high(0, 0)
            xq_high(0)

            def split_high(buf, hi_sem, chunks=range(WCH)):
                for c in chunks:
                    raw, hi = (w[:, bass.ds(buf, 1), bass.ds(c, 1)].rearrange("k o c n -> k (o c n)") for w in (w_raw, w_hi))
                    act.copy(hi, raw).then_inc(hi_sem, 1)

            def shared_high(half, f):
                n = FC * half + f
                act.wait_ge(sh_gate_done, n + 1)
                if n > 0:
                    act.wait_ge(shT_lo_ready, n)
                act.activation(sh_z[:], score[f][:], ACT.Silu).then_inc(sh_silu_done, 1)
                act.wait_ge(sh_z_ready, n + 1)
                if half == 1 and f == 0:
                    act.wait_ge(sh_down_done, HB)
                act.copy(shT_hi[:, f], sh_z[:]).then_inc(shT_hi_ready, 1)

            act.wait_ge(moe_in, 16 * 9)
            act.copy(gate_hi[:], gate_in[:]).then_inc(gate_hi_ready, 1)

            def route_half(half):
                shared_high(half, 0)
                act.wait_ge(logits_turned, half + 1)
                if half == 1:
                    act.wait_ge(rows_ready, 1)
                act.activation(e_score[:], qkv_ps[:, 0:HB * NE].rearrange("t (b e) -> t b e", e=NE), ACT.Exp, scale=-1.0).then_inc(logit_exp, 1)
                shared_high(half, 1)

            cross_step(0, 0)
            act.wait_ge(w_in, 16)
            with act.Fori(0, HB // 2) as i:
                cross_step(i * 2 + 1, 1)
                split_high(1, sh_hi_ready, [i * 3 + c for c in range(WCH // 2)])
                cross_step(i * 2 + 2, 0)
            route_half(0)
            act.wait_ge(w_in, 32)
            for b in range(HB + 1, B):
                cross_step(b, b % 2)
                k = 2 * (b - HB - 1)
                split_high(0, w_hi_ready, range(k, k + 2))
            x2T_high(B - 1)
            route_half(1)

            act.wait_ge(tables_ready, 1)

            def slot_x_high(t, q):
                act.wait_ge(xs_turned, t + 1)
                if not isinstance(t, int) or t > 1:
                    act.wait_ge(gate_up_done, t - 1)
                act.copy(xsT_hi[q][:].rearrange("f c s -> f (c s)"), turn[0][:]).then_inc(xs_hi_ready, 1)

            def slot_silu(t, q):
                act.wait_ge(gate_up_done, t + 1)
                if not isinstance(t, int) or t > 0:
                    act.wait_ge(z_ready, t)
                act.activation(silu_g[:], score[q][:, 0:FF], ACT.Silu).then_inc(silu_done, 1)

            def slot_z_high(t):
                act.wait_ge(z_turned, t + 1)
                if not isinstance(t, int) or t > 0:
                    act.wait_ge(slot_done, t)
                act.copy(zT_hi[:].rearrange("f c s -> f (c s)"), turn[1][:, 0:FF]).then_inc(zT_hi_ready, 1)

            def y_copy(t, q):
                act.wait_ge(slot_done, t + 1)
                if not isinstance(t, int) or t > 1:
                    act.wait_ge(y_stored[q], 8 * (t - q))
                act.copy(y_sb[q][:], (out_a, out_b)[q][:]).then_inc(y_copied, 1)

            def next_expert_high(t):
                first = act.value_load(tab[0:1, 3, bass.ds(t, 1)], min_val=0, max_val=1)
                with act.If(first > 0):
                    e = act.value_load(tab[0:1, 0, bass.ds(t, 1)], min_val=0, max_val=NE - 2)
                    buf = act.value_load(tab[0:1, 1, bass.ds(t, 1)], min_val=0, max_val=1)
                    act.wait_ge(w_in, e * 16 + 48)
                    act.wait_ge(slot_done, t)
                    split_high(1 - buf, w_hi_ready)

            slot_x_high(0, 0)

            def step(t, q):
                slot_silu(t, q)
                if not isinstance(t, int) or t < SLOTS - 1:
                    slot_x_high(t + 1, 1 - q)
                if not isinstance(t, int) or t > 0:
                    y_copy(t - 1, 1 - q)
                slot_z_high(t)
                next_expert_high(t)

            step(0, 0)
            with act.Fori(0, (SLOTS - 3) // 2) as i:
                step(i * 2 + 1, 1)
                step(i * 2 + 2, 0)
            step(SLOTS - 2, 1)
            step(SLOTS - 1, 0)
            y_copy(SLOTS - 1, 0)

        @block.gpsimd
        def _(pool):
            pool.wait_ge(consts_ready, 4)

            def rotate(b):
                pool.wait_ge(rope_read, b + 1)
                if not isinstance(b, int) or b > 0:
                    pool.wait_ge(stack_lo, 2 * b)
                r = rotated[:].rearrange("s h (a e) -> s h a e", a=2)
                pool.tensor_tensor(r[:, :, 0], rope_cos[:, :, 0], rope_sin[:, :, 1], ALU.subtract).then_inc(rot_ready, 1)
                pool.tensor_tensor(r[:, :, 1], rope_cos[:, :, 1], rope_sin[:, :, 0], ALU.add).then_inc(rot_ready, 1)

            def mask_probs(b):
                for g in range(NKV):
                    pool.wait_ge(exp_done, 8 * b + g + 1)
                    pool.sem_inc(passed)
                    pr = probs[g % 4][:]
                    pool.affine_select(out=pr, in_=pr, pattern=[[0, REP], [1, 128]], compare_op=ALU.is_ge, fill=0.0,
                                       base=0, channel_multiplier=-1).then_inc(causal_done, 1)

            def rstd_1(b):
                pool.wait_ge(mv1, b + 1)
                pool.tensor_tensor(rstd[:], mean_var[:, 1:2], eps[:], ALU.add).then_inc(ve1, 1)
                pool.wait_ge(ve1, b + 1)
                pool.tensor_tensor(rstd[:], rstd[:], neg_half[:], ALU.pow).then_inc(rstd1, 1)

            rotate(0)

            def step(b, p):
                first, final = isinstance(b, int) and b == 0, isinstance(b, int) and b == B - 1
                if not final:
                    rotate(b + 1)
                if not first:
                    rstd_1(b - 1)
                mask_probs(b)

            over_batches(pool, step, None, None)
            rstd_1(B - 1)

            def xnormalise(b, t):
                pool.wait_ge(xrec_ready, 4 * b + t + 1)
                pr = xprob[t][:]
                pool.tensor_tensor(pr, pr, xrec[:, t].rearrange("n (h o) -> n h o", o=1).to_broadcast([128, XH, XK]), ALU.mult).then_inc(xprob_ready, 1)

            def rstd_2(b):
                pool.wait_ge(mv2, b + 1)
                pool.tensor_tensor(rstd2[:], mean_var2[:, 1:2], eps[:], ALU.add).then_inc(ve2, 1)
                pool.wait_ge(ve2, b + 1)
                pool.tensor_tensor(rstd2[:], rstd2[:], neg_half[:], ALU.pow).then_inc(rstd2_ready, 1)

            def x2_keep(b):
                pool.wait_ge(x2s_ready, b + 1)
                pool.tensor_copy(x2[:, bass.ds(b, 1)].rearrange("s o d -> s (o d)"), x2s[:]).then_inc(x2_ready, 1)

            def cross_step(b):
                first = isinstance(b, int) and b == 0
                xnormalise(b, 0)
                xnormalise(b, 1)
                if not first:
                    rstd_2(b - 1)
                xnormalise(b, 2)
                xnormalise(b, 3)
                if not first:
                    x2_keep(b - 1)

            def load_weights(src, buf):
                pool.dma_start(w_raw[:, buf], src).then_inc(w_in, 16)

            pool.wait_ge(x1_ready, B)
            pool.wait_ge(wo_done, B)
            load_weights(T["shared"], 1)
            pool.wait_ge(w_in, 16)
            load_weights(T["experts"][0], 0)

            def scatter(b, j):
                if j == 0:
                    pool.wait_ge(x2_ready, b + 1)
                pool.indirect_dma_start(xs_dram, bass.IndirectOffsetOnAxis(ap=row_of[:, j, b:b + 1], axis=0), x2[:, b], None).then_inc(scattered, 16)

            cross_step(0)
            with pool.Fori(1, HB + 1) as b:
                cross_step(b)
            for b in range(HB + 1, B):
                cross_step(b)
                if b == HB + 1:
                    pool.wait_ge(rows_ready, 1)
                for j in range(TOPK):
                    scatter(b - HB - 1, j)
            rstd_2(B - 1)
            x2_keep(B - 1)
            for j in range(TOPK):
                scatter(HB - 1, j)
            pool.wait_ge(rows_ready, 2)
            for b in range(HB, B):
                for j in range(TOPK):
                    scatter(b, j)

            pool.wait_ge(w_in, 32)
            pool.wait_ge(sh_lo_ready, WCH)
            load_weights(T["experts"][1], 1)

            def load_expert(e, buf):
                pool.wait_ge(w_in, e * 16 + 16)
                pool.wait_ge(w_lo_ready, (e - 1) * WCH)
                load_weights(T["experts"][bass.ds(e, 1)].rearrange("o p c n -> (o p) c n"), buf)

            with pool.Fori(1, NE // 2) as i:
                load_expert(i * 2, 0)
                load_expert(i * 2 + 1, 1)

            pool.wait_ge(yrows_ready, 1)
            pool.wait_ge(y_stored[0], 16 * ((SLOTS + 1) // 2))
            pool.wait_ge(y_stored[1], 16 * (SLOTS // 2))

            def gather(b, p):
                if not isinstance(b, int) or b > 1:
                    pool.wait_ge(combined, b * TOPK - TOPK)
                for j in range(TOPK):
                    pool.indirect_dma_start(gathered[p][:, j], None, ys_dram, bass.IndirectOffsetOnAxis(ap=yrow_of[:, j, bass.ds(b, 1)], axis=0)).then_inc(gathered_in[p], 16)

            def rstd_3(b):
                pool.wait_ge(mv3, b + 1)
                pool.tensor_tensor(rstd3[:], mean_var3[:, 1:2], eps[:], ALU.add).then_inc(ve3, 1)
                pool.wait_ge(ve3, b + 1)
                pool.tensor_tensor(rstd3[:], rstd3[:], neg_half[:], ALU.pow).then_inc(rstd3_ready, 1)

            gather(0, 0)
            gather(1, 1)
            for b in range(B):
                rstd_3(b)
                if b < B - 2:
                    gather(b + 2, b % 2)


def lay_out(inputs):
    f = {k: np.asarray(v) for k, v in inputs.items()}
    x = f["x"]
    w = f["L0_attn_w_qkv"]
    half = np.concatenate([np.arange(0, HD, 2), np.arange(1, HD, 2)])
    heads = np.arange(NQ).reshape(NKV // 2, 2, REP).transpose(0, 2, 1).ravel()
    heads = np.concatenate([heads, np.arange(NQ, QK_HEADS)])
    cols = np.concatenate([(heads[:, None] * HD + half[None, :]).ravel(), np.arange(QK_HEADS * HD, QKV)])
    rows = lambda m: m.reshape(m.shape[0] // 128, 128, -1).transpose(1, 0, 2)
    arrays = {
        "x": x,
        "xT": x.transpose(0, 2, 1).reshape(B, KC, 128, S).transpose(0, 2, 1, 3),
        "w_qkv": rows(w[:, cols]),
        "w_o": rows(f["L0_attn_w_o"]),
    }
    ch = np.arange(D // KC).reshape(XD, XH).T.ravel()
    arrays.update({
        "wq": f["L0_xattn_Wq"][ch].T, "wk": f["L0_xattn_Wk"][ch].T, "wv": f["L0_xattn_Wv"][ch].T,
        "wm": f["L0_xattn_Wm"][:, ch].T,
        "bq": f["L0_xattn_bq"][ch][:, None], "bk": f["L0_xattn_bk"][ch][None], "bv": f["L0_xattn_bv"][ch][None],
        "bm": f["L0_xattn_bm"][:, None],
        "proj": rows(np.concatenate([f["L0_xattn_proj_k"], f["L0_xattn_proj_v"]], 1)),
        "ctxT": f["ctx_4096"].transpose(0, 2, 1).reshape(B, KC, 128, S).transpose(0, 2, 1, 3),
    })
    wt = lambda w: rows(w.T)
    ffn = lambda g, u, d: np.concatenate([np.concatenate([wt(g), wt(u)], 2), wt(d)], 1)
    arrays.update({
        "gate": rows(f["L0_ffn_gate_w"].T),
        "bias_e": np.broadcast_to(f["L0_ffn_bias"][None], (128, NE)),
        "experts": np.stack([ffn(f["L0_ffn_Wg"][e], f["L0_ffn_Wu"][e], f["L0_ffn_Wd"][e]) for e in range(NE)]),
        "shared": ffn(f["L0_ffn_Sg"], f["L0_ffn_Su"], f["L0_ffn_Sd"]),
    })
    arrays.update(tables())
    return {k: np.ascontiguousarray(v) for k, v in arrays.items()}


def kernel(**inputs):
    import concourse.bacc as bacc
    from concourse.bass_utils import run_bass_kernel_spmd

    arrays = lay_out(inputs)
    nc = bacc.Bacc("TRN2", target_bir_lowering=False, num_devices=1)
    T = {n: nc.dram_tensor(f"in_{n}", a.shape, mybir.dt.from_np(a.dtype), kind="ExternalInput").ap() for n, a in arrays.items()}
    T["out"] = nc.dram_tensor("out_0", (B, S, D), F32, kind="ExternalOutput").ap()
    program(nc, T)
    r = run_bass_kernel_spmd(nc, [{f"in_{n}": a for n, a in arrays.items()}], core_ids=[0])
    return r.results[0]["out_0"]
```

```python
from contextlib import ExitStack

import numpy as np

import concourse.bass as bass
from concourse import mybir

F32 = mybir.dt.float32
F32R = mybir.dt.float32r
BF16 = mybir.dt.bfloat16
F16 = mybir.dt.float16
I32 = mybir.dt.int32
ALU = mybir.AluOpType
ACT = mybir.ActivationFunctionType
AX = mybir.AxisListType

B, S, D = 8, 128, 512
KC = D // 128
HD, NQ, NKV = 16, 32, 8
REP = NQ // NKV
QKV = HD * (NQ + 2 * NKV)
QK_HEADS = NQ + NKV
STACK = 4 * HD
XH, XD, XK = 16, 8, 32
HPT = 128 // XK
NE, TOPK, FF = 16, 4, 256
FC = FF // 128
TOKENS = B * S
SLOT = 128
REGION = TOKENS + SLOT
IDLE_ROW = NE * REGION
SLOTS = (TOKENS * TOPK + NE * (SLOT - 1)) // SLOT
SURE_STEPS = TOKENS * TOPK // SLOT + 1
NT = 64
SETS = 3
COLS = 10
HB = B // 2
WCH = KC + FC
EARLY, LATE = range(WCH - 4), range(WCH - 4, WCH)
EPS = 1e-5
MASKED = -1e30


def tables():
    inv_freq = (1.0 / np.float32(10000.0) ** (np.arange(0, HD, 2, dtype=np.float32) / np.float32(HD))).astype(np.float32)
    angles = np.arange(S, dtype=np.float32)[:, None] * inv_freq[None, :]
    cos, sin = np.cos(angles).astype(np.float32), np.sin(angles).astype(np.float32)
    rope = np.stack([np.concatenate([cos, cos], 1), np.concatenate([sin, sin], 1)], 1)
    return {
        "rope": np.ascontiguousarray(rope),
        "head_mask": (np.arange(128)[:, None] // XD == np.arange(XH)[None]).astype(np.float32),
        "value_mask": (np.arange(128)[:, None] // XK == np.arange(HPT)[None]).astype(np.float32),
        "region": np.broadcast_to(np.arange(NE, dtype=np.float32) * REGION, (128, NE)),
        "iota16": np.broadcast_to(np.arange(NE, dtype=np.float32) - NE, (128, NE)),
        "tri": (np.arange(128)[:, None] < np.arange(128)[None]).astype(np.float32),
        "thresholds": np.broadcast_to(np.arange(0, TOKENS, SLOT, dtype=np.float32), (128, 8)),
        "upto_mask": np.broadcast_to((np.arange(NE)[None] <= np.arange(NE)[:, None]).astype(np.float32), (128, NE, NE)),
        "slot_no": np.arange(128, dtype=np.float32)[:, None],
        "rounds": np.broadcast_to(np.arange(SETS, NE, SETS, dtype=np.float32), (128, len(range(SETS, NE, SETS)))),
        "ident": np.eye(128, dtype=np.float32),
        "causal": np.where(np.arange(S)[None, :] > np.arange(S)[:, None], np.float32(MASKED), np.float32(0)).astype(np.float32),
    }


def program(nc, T):
    T["xs"] = nc.dram_tensor("dispatched", (NE * REGION + SLOT, D), F32).ap()
    T["ys"] = nc.dram_tensor("slot_results", ((SLOTS + 1) * SLOT, D), F32).ap()
    with ExitStack() as ctx:
        def sb(name, shape, dt=F32):
            return ctx.enter_context(nc.sbuf_tensor(name, shape, dt))

        def sem(name):
            return ctx.enter_context(nc.semaphore(name))

        def under(name, shape, dt=F32):
            with ExitStack() as scope:
                return scope.enter_context(nc.sbuf_tensor(name, shape, dt))

        ident = sb("ident", [128, 128])
        neg_half = sb("neg_half", [128, 1])
        eps = sb("eps", [128, 1])
        x1 = sb("x1", [128, B, D])
        base = x1
        x2 = sb("x2", [128, B, D])
        bias_e = sb("bias_e", [128, NE]); region = sb("region", [128, NE])
        iota16 = sb("iota16", [128, NE]); tri = sb("tri", [128, 128]); tri_bf = sb("tri_bf", [128, 128], BF16)
        e_score = sb("e_score", [128, HB, NE]); e_eq = sb("e_eq", [128, HB, NE]); e_low = sb("e_low", [128, HB])
        picked = sb("picked", [128, TOPK, B, NE])
        weight = sb("weight", [128, TOPK, B]); w_sum = sb("w_sum", [128, HB]); w_rec = sb("w_rec", [128, HB])
        chosen = sb("chosen", [128, HB, NE]); chosen_bf = sb("chosen_bf", [128, HB, NE], BF16)
        before = sb("before", [128, B + 1, NE]); before_bf = sb("before_bf", [128, B + 1, NE], BF16)
        rank = sb("rank", [128, B, NE]); place = sb("place", [128, B, NE])
        picked_place = sb("picked_place", [128, TOPK, B, NE]); row_f = sb("row_f", [128, TOPK, B])
        row_of = sb("row_of", [128, TOPK, B], I32); yrow_of = sb("yrow_of", [128, TOPK, B], I32)
        gathered0 = under("gathered0", [128, TOPK, D])
        x2T_hi = sb("x2T_hi", [128, KC, B // 2, 128], F32R)
        gathered1 = under("gathered1", [128, TOPK, D])
        x2T_lo = sb("x2T_lo", [128, KC, B // 2, 128], F32R)
        ones_bf = sb("ones_bf", [128, 128], BF16)

        ones_col = sb("ones_col", [128, 1])
        wst = under("wst", [128, KC, QKV])
        wq_in = sb("wq_in", [128, 128]); wq_hi = sb("wq_hi", [128, 128], F32R); wq_lo = sb("wq_lo", [128, 128], F32R)
        wm_in = sb("wm_in", [128, 128]); wm_hi = sb("wm_hi", [128, 128], F32R); wm_lo = sb("wm_lo", [128, 128], F32R)
        wk = sb("wk", [128, 128]); wv = sb("wv", [128, 128])
        bias_q = sb("bias_q", [128, 1]); bias_m = sb("bias_m", [128, 1])
        bias_k_row = sb("bias_k_row", [1, 128]); bias_v_row = sb("bias_v_row", [1, 128])
        proj = sb("proj", [128, KC, 2 * XK])
        head_mask = sb("head_mask", [128, XH]); value_mask = sb("value_mask", [128, HPT])
        proj_sum_k = sb("proj_sum_k", [1, XK]); proj_sum_v = sb("proj_sum_v", [1, HPT, XK])
        ctxT = [sb(f"ctxT{p}", [128, KC, 128]) for p in (0, 1)]
        values = [sb(f"values{p}", [128, XH // HPT, HPT, XD]) for p in (0, 1)]
        xmax = sb("xmax", [128, 4, XH]); xsum = sb("xsum", [128, 4, XH]); xrec = sb("xrec", [128, 4, XH])
        ctx_k = sb("ctx_k", [128, XK]); ctx_v = sb("ctx_v", [128, HPT, XK])

        self_scope = ExitStack()
        outer_sb = sb

        def sb(name, shape, dt=F32):
            return self_scope.enter_context(nc.sbuf_tensor(name, shape, dt))

        ident_bf = sb("ident_bf", [128, 128], BF16)
        causal = sb("causal", [128, 128])
        causal_bf = sb("causal_bf", [128, REP, 128], BF16)
        rope = sb("rope", [128, 2, HD])
        wqkv_hi = sb("wqkv_hi", [128, KC, QKV], F32R)
        wqkv_lo = sb("wqkv_lo", [128, KC, QKV], F32R)
        wo_in = sb("wo_in", [128, KC, D])
        wo_hi = sb("wo_hi", [128, KC, D], F32R)
        wo_lo = sb("wo_lo", [128, KC, D], F32R)
        xT = sb("xT", [128, 2, KC, 128])
        xT_hi = [sb(f"xT_hi{p}", [128, KC, 128], F32R) for p in (0, 1)]
        xT_lo = [sb(f"xT_lo{p}", [128, KC, 128], F32R) for p in (0, 1)]
        x_in = sb("x_in", [128, 2, D])
        rope_cos = sb("rope_cos", [128, QK_HEADS, 2, HD // 2])
        rope_sin = sb("rope_sin", [128, QK_HEADS, 2, HD // 2])
        rotated = sb("rotated", [128, QK_HEADS, HD])
        stack = sb("stack", [128, QK_HEADS, 4, HD], F32R)
        v_ones = [sb(f"v_ones{p}", [128, NKV, 32]) for p in (0, 1)]
        qT = [sb(f"qT{p}", [128, NQ // 2, 128], F32R) for p in (0, 1)]
        kT = [sb(f"kT{p}", [128, NKV // 2, 128], F32R) for p in (0, 1)]
        qT_half = sb("qT_half", [128, NQ // 2, 128], F16)
        kT_half = sb("kT_half", [128, NKV // 2, 128], F16)
        pv_sb = [sb(f"pv_sb{h}", [128, REP, 128]) for h in (0, 1)]
        neg_max = sb("neg_max", [128, NKV, REP])
        neg_max_parts = sb("neg_max_parts", [128, 4, 2, NKV // 2, REP], F32R)
        maxT = sb("maxT", [64, 128], F32R)
        probs = [sb(f"probs{r}", [128, REP, 128]) for r in range(4)]
        attn_rsum = sb("attn_rsum", [128, 2, REP, 4])
        attn_out = sb("attn_out", [128, 2, NQ // 2, HD])
        oT_hi = sb("oT_hi", [128, KC, 128], F32R)
        oT_lo = sb("oT_lo", [128, KC, 128], F32R)
        y1 = sb("y1", [128, D])
        bn6 = sb("bn6", [128, 6])
        mean_var = sb("mean_var", [128, 2])
        rstd = sb("rstd", [128, 1])
        self_scope.close()
        sb = outer_sb

        gate_in = sb("gate_in", [128, KC, NE]); gate_hi = sb("gate_hi", [128, KC, NE], F32R); gate_lo = sb("gate_lo", [128, KC, NE], F32R)
        logitT = sb("logitT", [NE, HB * 128])
        w_hi = sb("w_hi", [128, SETS, WCH, D], F32R)
        w_raw = under("w_raw", [128, SETS, WCH, D])
        w_lo = sb("w_lo", [128, SETS, WCH, D], F32R)
        count = sb("count", [128, NE]); thresholds = sb("thresholds", [128, 8]); over = sb("over", [128, NE, 8])
        n_slots = sb("n_slots", [128, NE]); slots_to = sb("slots_to", [128, NE]); slot_base = sb("slot_base", [128, NE])
        upto_mask = sb("upto_mask", [128, NE, NE]); prod = sb("prod", [128, NE, NE])
        slot_no = sb("slot_no", [128, 1]); rounds = sb("rounds", [128, len(range(SETS, NE, SETS))])
        passed = sb("passed_experts", [128, NE]); passed_n = sb("passed_n", [128, NE]); over_rounds = sb("over_rounds", [128, len(range(SETS, NE, SETS))])
        in_use = sb("in_use", [128, NE]); used_to = sb("used_to", [128, NE]); last_used = sb("last_used", [128, 1]); slot_no_2 = sb("slot_no_2", [128, 1])
        work = sb("work", [128, 4]); col = sb("col", [128, COLS])
        tab_f = sb("tab_f", [1, NT + 1]); tab = sb("tab", [1, COLS, NT], I32); pad_f = sb("pad_f", [1, NE]); pad_row = sb("pad_row", [1, NE], I32)
        stored_f = sb("stored_f", [1, 2]); stored = sb("stored", [1, 2], I32)
        zeros = sb("zeros", [128, D])
        sh_z = sb("sh_z", [128, D])
        outs = under("outs", [128, 2, D])
        shT_hi = sb("shT_hi", [128, FC, D], F32R); shT_lo = sb("shT_lo", [128, FC, D], F32R)
        bn6c = sb("bn6c", [128, 2, 6]); mean_var3 = sb("mean_var3", [128, 2, 2, 2]); rstd3 = sb("rstd3", [128, 2, 2])
        gathered = [gathered0[:], gathered1[:], x2[:, 0:TOPK], x2[:, TOPK:2 * TOPK]]
        out_sb = [outs[:, q] for q in (0, 1)]
        xs_dram, ys_dram = T["xs"], T["ys"]
        cross_scope = ExitStack()

        def sb(name, shape, dt=F32):
            return cross_scope.enter_context(nc.sbuf_tensor(name, shape, dt))

        keys = sb("keys", [128, XH, XK])
        keys_hi = [sb(f"keys_hi{p}", [128, XH * XK], F32R) for p in (0, 1)]
        keys_lo = [sb(f"keys_lo{p}", [128, XH * XK], F32R) for p in (0, 1)]
        x1_hi = sb("x1_hi", [128, D], F32R); x1_lo = sb("x1_lo", [128, D], F32R)
        xq_hi = sb("xq_hi", [128, D], F32R); xq_lo = sb("xq_lo", [128, D], F32R)
        xprob = [sb(f"xprob{t}", [128, XH, XK]) for t in range(4)]
        xprobT = [sb(f"xprobT{t}", [128, XH // HPT, 128]) for t in (0, 1)]
        xo_hi = sb("xo_hi", [128, D], F32R); xo_lo = sb("xo_lo", [128, D], F32R)
        y2 = sb("y2", [128, D]); x2s = sb("x2s", [128, D])
        bn6b = sb("bn6b", [128, 6]); mean_var2 = sb("mean_var2", [128, 2]); rstd2 = sb("rstd2", [128, 1])
        cross_scope.close()
        sb = outer_sb
        xs_in = [sb(f"xs_in{q}", [128, D]) for q in (0, 1)]
        xsT_hi = [sb(f"xsT_hi{q}", [128, KC, 128], F32R) for q in (0, 1)]
        xsT_lo = [sb(f"xsT_lo{q}", [128, KC, 128], F32R) for q in (0, 1)]
        silu_g = sb("silu_g", [128, FF]); z = sb("z", [128, FF])
        zT_hi = sb("zT_hi", [128, FC, 128], F32R); zT_lo = sb("zT_lo", [128, FC, 128], F32R)
        y_sb = [sb(f"y_sb{q}", [128, D]) for q in (0, 1)]
        diag = [t[:].rearrange("t (j s) -> t j s", j=TOPK) for t in y_sb]

        bank = [ctx.enter_context(nc.psum_tensor(f"bank{i}", [128, 512], F32)) for i in range(2, 8)]
        qkv_ps = ctx.enter_context(nc.psum_tensor("qkv_ps", [128, 1024], F32))
        turn = [bank[0], bank[1]]
        score = [bank[2], bank[3]]
        out_a, out_b = bank[4], bank[5]
        ctx_ps, k_ps, v_ps = qkv_ps[:, 512:512 + 2 * XK], qkv_ps[:, 576:576 + XK], qkv_ps[:, 640:768]

        consts_in = sem("consts_in"); wqkv_in = [sem(f"wqkv_in{c}") for c in range(KC)]; wo_loaded = sem("wo_loaded")
        xT_in = [sem(f"xT_in{p}") for p in (0, 1)]; x_loaded = [sem(f"x_loaded{p}") for p in (0, 1)]
        consts_ready = sem("consts_ready")
        wqkv_hi_ready = sem("wqkv_hi_ready"); wqkv_lo_ready = sem("wqkv_lo_ready")
        wo_hi_ready = sem("wo_hi_ready"); wo_lo_ready = sem("wo_lo_ready")
        xT_hi_ready = sem("xT_hi_ready"); xT_lo_ready = sem("xT_lo_ready")
        qkv_done = sem("qkv_done"); rope_read = sem("rope_read"); v_ready = sem("v_ready")
        rot_ready = sem("rot_ready"); stack_hi = sem("stack_hi"); stack_lo = sem("stack_lo")
        qkT_turned = sem("qkT_turned"); qkT_by_act = sem("qkT_by_act"); qkT_by_dve = sem("qkT_by_dve")
        pass1_done = sem("pass1_done"); max_done = sem("max_done")
        max_hi = sem("max_hi"); max_parts = sem("max_parts"); max_turned = sem("max_turned")
        maxT_ready = sem("maxT_ready"); max_rows = sem("max_rows")
        pass2_done = sem("pass2_done"); exp_done = sem("exp_done"); causal_done = sem("causal_done")
        pv_done = sem("pv_done"); halves_ready = sem("halves_ready"); pv_copied = sem("pv_copied"); pv_turned = sem("pv_turned"); rsum_ready = sem("rsum_ready"); attn_normed = sem("attn_normed")
        oT_turned = sem("oT_turned"); oT_hi_ready = sem("oT_hi_ready"); oT_lo_ready = sem("oT_lo_ready")
        wo_done = sem("wo_done"); y1_ready = sem("y1_ready"); stats = sem("stats"); mv1 = sem("mv1")
        var_eps = sem("var_eps"); rstd1 = sem("rstd1"); x1_ready = sem("x1_ready")
        cross_in = sem("cross_in"); cross_hi = sem("cross_hi"); cross_lo = sem("cross_lo"); cross_masks = sem("cross_masks")
        proj_summed = sem("proj_summed"); proj_sums = sem("proj_sums")
        ctxT_in = [sem(f"ctxT_in{p}") for p in (0, 1)]
        ctx_done = sem("ctx_done"); ctx_copied = sem("ctx_copied"); kv_done = sem("kv_done")
        keys_ready = sem("keys_ready"); values_ready = sem("values_ready"); keys_hi_ready = sem("keys_hi_ready"); keys_lo_ready = sem("keys_lo_ready")
        x1_hi_ready = sem("x1_hi_ready"); x1_lo_ready = sem("x1_lo_ready"); xq_done = sem("xq_done")
        xq_hi_ready = sem("xq_hi_ready"); xq_lo_ready = sem("xq_lo_ready")
        xscore_done = sem("xscore_done"); xmax_ready = sem("xmax_ready"); xsub_done = sem("xsub_done"); xexp_done = sem("xexp_done")
        xsum_ready = sem("xsum_ready"); xrec_ready = sem("xrec_ready"); xprob_ready = sem("xprob_ready")
        xprob_turned = sem("xprob_turned"); xprobT_ready = sem("xprobT_ready"); xpv_done = sem("xpv_done")
        xo_hi_ready = sem("xo_hi_ready"); xo_lo_ready = sem("xo_lo_ready"); wm_done = sem("wm_done")
        y2_ready = sem("y2_ready"); mv2 = sem("mv2"); rstd2_ready = sem("rstd2_ready")
        x2s_ready = sem("x2s_ready"); x2_ready = sem("x2_ready"); x2_turned = sem("x2_turned")
        x2T_hi_ready = sem("x2T_hi_ready"); x2T_lo_ready = sem("x2T_lo_ready")
        moe_in = sem("moe_in"); gate_hi_ready = sem("gate_hi_ready"); gate_lo_ready = sem("gate_lo_ready"); tri_ready = sem("tri_ready")
        logits_done = sem("logits_done"); logitT_ready = sem("logitT_ready"); logits_turned = sem("logits_turned"); logit_exp = sem("logit_exp")
        route = sem("route"); chosen_ready = sem("chosen_ready"); ranks_done = sem("ranks_done"); rows_ready = sem("rows_ready")
        scattered = sem("scattered"); tables_ready = sem("tables_ready"); pads_ready = sem("pads_ready"); columns_ready = sem("columns_ready"); columns_turned = sem("columns_turned"); yrows_ready = sem("yrows_ready"); padded = sem("padded")
        zeros_ready = sem("zeros_ready")
        w_in = sem("w_in"); w_hi_ready = sem("w_hi_ready"); w_lo_ready = sem("w_lo_ready")
        sh_hi_ready = sem("sh_hi_ready"); sh_lo_ready = sem("sh_lo_ready")
        sh_gate_done = sem("sh_gate_done"); sh_up_done = sem("sh_up_done"); sh_silu_done = sem("sh_silu_done"); sh_z_ready = sem("sh_z_ready")
        shT_hi_ready = sem("shT_hi_ready"); shT_lo_ready = sem("shT_lo_ready"); sh_down_done = sem("sh_down_done"); base_ready = sem("base_ready")
        xs_loaded = [sem(f"xs_loaded{q}") for q in (0, 1)]; xs_turned = sem("xs_turned"); xs_hi_ready = sem("xs_hi_ready"); xs_lo_ready = sem("xs_lo_ready")
        gate_up_done = sem("gate_up_done"); silu_done = sem("silu_done"); z_ready = sem("z_ready"); z_turned = sem("z_turned")
        zT_hi_ready = sem("zT_hi_ready"); zT_lo_ready = sem("zT_lo_ready"); slot_done = sem("slot_done"); y_copied = sem("y_copied")
        y_stored = [sem(f"y_stored{q}") for q in (0, 1)]
        gathered_in = [sem(f"gathered_in{q}") for q in range(4)]; combined = sem("combined"); diag_ready = sem("diag_ready"); mv3 = sem("mv3"); rstd3_ready = sem("rstd3_ready")
        results_stored = sem("results_stored"); out_ready = sem("out_ready"); out_in = [sem(f"out_in{q}") for q in (0, 1)]
        held = sem("held")

        block = ctx.enter_context(nc.Block())

        def over_batches(eng, step):
            step(0, 0)
            with eng.Fori(0, (B - 2) // 2) as i:
                step(i * 2 + 1, 1)
                step(i * 2 + 2, 0)
            step(B - 1, 1)

        def half_place(t, b):
            return t[:, :, b % HB] if isinstance(b, int) else t[:, :, bass.ds(b, 1)].rearrange("f c o s -> f c (o s)")

        def slot_steps(eng, step, peeled):
            for t in range(peeled):
                step(t, t % 2)
            with eng.Fori((peeled - 1) // 2, (SURE_STEPS - 1) // 2) as i:
                step(i * 2 + 1, 1)
                step(i * 2 + 2, 0)
            with eng.Fori((SURE_STEPS - 1) // 2, (SLOTS + 1) // 2) as i:
                steps = eng.value_load(tab[0:1, 4, bass.ds(i * 2 + 1, 1)], min_val=0, max_val=2)
                with eng.If(steps > 0):
                    step(i * 2 + 1, 1)
                    with eng.If(steps > 1):
                        step(i * 2 + 2, 0)

        @block.sync
        def _(sp):
            def load_xT(b, p):
                sp.dma_start(xT[:, p], T["xT"][bass.ds(b, 1)].rearrange("o p c s -> (o p) c s")).then_inc(xT_in[p], 16)

            def load_x(b, p):
                sp.dma_start(x_in[:, p], T["x"][bass.ds(b, 1)].rearrange("o s d -> (o s) d")).then_inc(x_loaded[p], 16)

            load_xT(0, 0)
            for c in range(KC):
                sp.dma_start(wst[:, c], T["w_qkv"][:, c]).then_inc(wqkv_in[c], 16)
            sp.dma_start(rope[:], T["rope"]).then_inc(consts_in, 16)
            sp.dma_start(ident[:], T["ident"]).then_inc(consts_in, 16)
            sp.dma_start(causal[:], T["causal"]).then_inc(consts_in, 16)
            load_xT(1, 1)
            load_x(0, 0)
            sp.dma_start(wo_in[:], T["w_o"]).then_inc(wo_loaded, 16)

            def step(b, p):
                sp.wait_ge(maxT_ready, b + 1)
                for a in (0, 1):
                    row = 64 * a + 3 * HD
                    sp.dma_start(qT[p][row:row + 2, :, :].bitcast(F32),
                                 maxT[32 * a:32 * a + 32, :].bitcast(F32)).then_inc(max_rows, 16)
                if not (isinstance(b, int) and b >= B - 2):
                    sp.wait_ge(xT_hi_ready, b + 1)
                    sp.wait_ge(xT_lo_ready, b + 1)
                    load_xT(b + 2, p)
                if not (isinstance(b, int) and b == B - 1):
                    if not isinstance(b, int) or b > 0:
                        sp.wait_ge(y1_ready, b)
                    load_x(b + 1, 1 - p)

            step(0, 0)
            sp.wait_ge(wqkv_lo_ready, KC)
            for tile, name in ((wq_in, "wq"), (wm_in, "wm"), (wk, "wk"), (wv, "wv"), (bias_q, "bq"), (bias_m, "bm"),
                               (bias_k_row, "bk"), (bias_v_row, "bv"), (proj, "proj"), (head_mask, "head_mask"),
                               (value_mask, "value_mask")):
                sp.dma_start(tile[:], T[name]).then_inc(cross_in, 16)

            def load_ctx(b, p):
                if not isinstance(b, int) or b > 1:
                    sp.wait_ge(ctx_done, b - 1)
                sp.dma_start(ctxT[p][:], T["ctxT"][bass.ds(b, 1)].rearrange("o p c s -> (o p) c s")).then_inc(ctxT_in[p], 16)

            load_ctx(0, 0)
            load_ctx(1, 1)
            with sp.Fori(0, (B - 4) // 2) as i:
                step(i * 2 + 1, 1)
                step(i * 2 + 2, 0)
            step(B - 3, 1)
            step(B - 2, 0)
            step(B - 1, 1)
            sp.wait_ge(x1_ready, B)
            sp.wait_ge(wo_done, B)
            MOE_CONSTS = ((gate_in, "gate"), (bias_e, "bias_e"), (region, "region"), (iota16, "iota16"), (tri, "tri"),
                          (thresholds, "thresholds"), (upto_mask, "upto_mask"), (slot_no, "slot_no"), (rounds, "rounds"))
            for tile, name in MOE_CONSTS:
                sp.dma_start(tile[:], T[name]).then_inc(moe_in, 16)
            with sp.Fori(1, B // 2) as i:
                load_ctx(i * 2, 0)
                load_ctx(i * 2 + 1, 1)
            sp.wait_ge(zeros_ready, 1)
            sp.dma_start(xs_dram[IDLE_ROW:IDLE_ROW + SLOT, :], zeros[:]).then_inc(padded, 16)
            with sp.Fori(SURE_STEPS - 1, SLOTS + 1) as t:
                sp.dma_start(ys_dram[bass.ds(t * SLOT, SLOT), :], zeros[:]).then_inc(padded, 16)
            sp.wait_ge(pads_ready, 1)
            with sp.Fori(0, NE // 4) as i:
                rows = [sp.value_load(pad_row[0:1, bass.ds(i * 4 + j, 1)], min_val=0, max_val=IDLE_ROW - SLOT) for j in range(4)]
                for row in rows:
                    sp.dma_start(xs_dram[bass.ds(row, SLOT), :], zeros[:]).then_inc(padded, 16)
            sp.wait_ge(tables_ready, 1)
            sp.wait_ge(padded, 16 * (NE + 1 + SLOTS + 2 - SURE_STEPS))
            sp.wait_ge(scattered, 16 * TOPK * B)

            def load_slot(t, q):
                row = sp.value_load(tab[0:1, 2, bass.ds(t, 1)], min_val=0, max_val=IDLE_ROW)
                sp.dma_start(xs_in[q][:], xs_dram[bass.ds(row, SLOT), :]).then_inc(xs_loaded[q], 16)

            def store_slot(t, q):
                sp.wait_ge(y_copied, t + 1)
                sp.dma_start(ys_dram[bass.ds(t * SLOT, SLOT), :], y_sb[q][:]).then_inc(y_stored[q], 16)

            load_slot(0, 0)
            load_slot(1, 1)

            def step(t, q):
                sp.wait_ge(xs_turned, t + 1)
                load_slot(t + 2, q)
                if not isinstance(t, int) or t > 0:
                    store_slot(t - 1, 1 - q)

            n0 = sp.value_load(stored[0:1, 0:1], min_val=16, max_val=16 * SLOTS)
            n1 = sp.value_load(stored[0:1, 1:2], min_val=16, max_val=16 * SLOTS)
            slot_steps(sp, step, 1)
            sp.wait_ge(y_stored[0], n0)
            sp.sem_inc(held)
            sp.wait_ge(y_stored[1], n1)
            sp.sem_inc(results_stored)
            def store_out(b, p):
                sp.wait_ge(out_ready, b + 1)
                sp.dma_start(T["out"][bass.ds(b, 1)].rearrange("o s d -> (o s) d"), out_sb[p]).then_inc(out_in[p], 16)

            with sp.Fori(0, B // 2) as i:
                store_out(i * 2, 0)
                store_out(i * 2 + 1, 1)
            sp.wait_ge(out_in[0], 16 * (B // 2))
            sp.wait_ge(out_in[1], 16 * (B // 2))

        @block.tensor
        def _(pe):
            def split_product(out, stat_hi, stat_lo, mov_hi, mov_lo, start, stop):
                pe.matmul(out, stat_hi, mov_lo, start=start, stop=False)
                pe.matmul(out, stat_lo, mov_hi, start=False, stop=False)
                return pe.matmul(out, stat_hi, mov_hi, start=False, stop=stop)

            def qkv_chunk(b, p, c):
                if c == 0:
                    pe.wait_ge(xT_hi_ready, b + 1)
                    pe.wait_ge(xT_lo_ready, b + 1)
                    if not isinstance(b, int) or b > 0:
                        pe.wait_ge(rope_read, b)
                        pe.wait_ge(v_ready, b)
                if isinstance(b, int) and b == 0:
                    pe.wait_ge(wqkv_hi_ready, c + 1)
                    pe.wait_ge(wqkv_lo_ready, c + 1)
                for lo, hi in ((0, 512), (512, QKV)):
                    last = split_product(qkv_ps[:, lo:hi], xT_hi[p][:, c], xT_lo[p][:, c],
                                         wqkv_hi[:, c, lo:hi], wqkv_lo[:, c, lo:hi], c == 0, c == KC - 1)
                if c == KC - 1:
                    last.then_inc(qkv_done, 1)

            def turn_qk(b, r):
                if r == 0:
                    pe.wait_ge(stack_hi, 2 * b + 2)
                    pe.wait_ge(stack_lo, 2 * b + 2)
                pairs = stack[:].rearrange("s (j two) a e -> s j (two a e)", two=2).bitcast(F32)
                if r == 1:
                    if not isinstance(b, int) or b > 1:
                        pe.wait_ge(oT_lo_ready, b - 1)
                elif r == 3:
                    pe.wait_ge(qkT_by_dve, 2 * b + 1)
                elif r > 0 or not isinstance(b, int) or b > 0:
                    pe.wait_ge(qkT_by_act, 3 * b + r // 2)
                j0 = NQ // 2 if r == 0 else 4 * (r - 1)
                for j in range(4):
                    t = pe.transpose(turn[r % 2][:, 128 * j:128 * j + 128], pairs[:, j0 + j], ident[:])
                t.then_inc(qkT_turned, 1)

            def pass1(b, p, g):
                u, a = g // 2, g % 2
                rows = slice(64 * a, 64 * a + HD)
                pe.wait_ge(halves_ready, 5 * b + u + 2)
                if g < 2:
                    if not isinstance(b, int) or b > 0:
                        pe.wait_ge(exp_done, 8 * b - 1 + g)
                else:
                    pe.wait_ge(max_done, 8 * b + g - 1)
                pe.matmul(score[g % 2][:], ident_bf[:], causal_bf[:].rearrange("s r t -> s (r t)"), start=True, stop=False)
                for r in range(REP):
                    m = pe.matmul(score[g % 2][:, 128 * r:128 * r + 128], qT_half[rows, 4 * u + r], kT_half[rows, u],
                                  start=False, stop=(r == REP - 1))
                m.then_inc(pass1_done, 1)

            def turn_max(b):
                pe.wait_ge(max_parts, b + 1)
                if not isinstance(b, int) or b > 0:
                    pe.wait_ge(attn_normed, 2 * b)
                pe.transpose(out_b[:, 0:128], neg_max_parts[:].rearrange("s a q u r -> s (a q u r)").bitcast(F32),
                             ident[:]).then_inc(max_turned, 1)

            def pass2(b, p, g):
                u, a = g // 2, g % 2
                rows = slice(64 * a, 64 * a + 3 * HD + 2)
                if g == 0:
                    pe.wait_ge(max_rows, 32 * b + 32)
                if g < 2:
                    pe.wait_ge(max_done, 8 * b + 7 + g)
                else:
                    pe.wait_ge(exp_done, 8 * b + g - 1)
                pe.matmul(score[g % 2][:], kT[p][rows, u], qT[p][rows, 4 * u:4 * u + 4].rearrange("k r s -> k (r s)"),
                          start=True, stop=True).then_inc(pass2_done, 1)

            def pv(b, p, g):
                pe.wait_ge(causal_done, 8 * b + g + 1)
                if g == 0:
                    pe.wait_ge(v_ready, b + 1)
                    if not isinstance(b, int) or b > 0:
                        pe.wait_ge(y1_ready, b)
                if g == 4:
                    pe.wait_ge(maxT_ready, b + 1)
                dst = out_a if g < 4 else out_b
                j = 32 * (g % 4)
                pe.matmul(dst[j:j + 32, :], v_ones[p][:, g], probs[g % 4][:].rearrange("t r s -> t (r s)"),
                          start=True, stop=True).then_inc(pv_done, 1)

            def turn_pv(b, half):
                pe.wait_ge(pv_copied, 2 * b + half + 1)
                for r in range(REP):
                    t = pe.transpose((out_a, out_b)[half][:, 128 * r:128 * r + 128], pv_sb[half][:, r], ident[:])
                t.then_inc(pv_turned, 1)

            def turn_o(b):
                pe.wait_ge(attn_normed, 2 * b + 2)
                pe.wait_ge(qkT_by_dve, 2 * b + 4 if not (isinstance(b, int) and b == B - 1) else 2 * B)
                if isinstance(b, int) and b == B - 1:
                    pe.wait_ge(oT_lo_ready, B - 1)
                o = attn_out[:].rearrange("s a h e -> s (a h e)")
                for c in range(KC):
                    t = pe.transpose(turn[1][:, 128 * c:128 * c + 128], o[:, 128 * c:128 * c + 128], ident[:])
                t.then_inc(oT_turned, 1)

            def w_o(b):
                pe.wait_ge(oT_hi_ready, b + 1)
                pe.wait_ge(oT_lo_ready, b + 1)
                if isinstance(b, int) and b == 0:
                    pe.wait_ge(wo_hi_ready, 1)
                    pe.wait_ge(wo_lo_ready, 1)
                for c in range(KC):
                    last = split_product(out_a[:], oT_hi[:, c], oT_lo[:, c], wo_hi[:, c], wo_lo[:, c], c == 0, c == KC - 1)
                last.then_inc(wo_done, 1)

            pe.wait_ge(consts_ready, 4)
            for c in range(KC):
                qkv_chunk(0, 0, c)
            for r in range(5):
                turn_qk(0, r)

            def step(b, p):
                first, final = isinstance(b, int) and b == 0, isinstance(b, int) and b == B - 1
                for g in range(NKV):
                    pass1(b, p, g)
                    if g == 2 and not first:
                        turn_pv(b - 1, 0)
                        turn_pv(b - 1, 1)
                    if g == 7 and not first:
                        turn_o(b - 1)
                    if g % 2 and not final:
                        qkv_chunk(b + 1, 1 - p, g // 2)
                turn_max(b)
                if not first:
                    w_o(b - 1)
                pass2(b, p, 0)
                pass2(b, p, 1)
                for g in range(NKV):
                    if g < NKV - 2:
                        pass2(b, p, g + 2)
                    pv(b, p, g)
                    if g >= NKV - 5 and not final:
                        turn_qk(b + 1, g - (NKV - 5))

            over_batches(pe, step)
            pe.wait_ge(cross_in, 16 * 11)
            pe.wait_ge(cross_masks, 1)
            pe.wait_ge(rope_read, B)
            pe.wait_ge(v_ready, B)
            for c in range(KC):
                m = pe.matmul(qkv_ps[0:1, 0:2 * XK], ones_col[:], proj[:, c], start=(c == 0), stop=(c == KC - 1))
            m.then_inc(proj_summed, 1)
            turn_pv(B - 1, 0)
            turn_pv(B - 1, 1)
            turn_o(B - 1)
            w_o(B - 1)

            def context(b, p):
                pe.wait_ge(ctxT_in[p], 8 * (b - p) + 16)
                if not isinstance(b, int) or b > 0:
                    pe.wait_ge(ctx_copied, 2 * b)
                    pe.wait_ge(values_ready, b)
                for c in range(KC):
                    m = pe.matmul(ctx_ps, ctxT[p][:, c], proj[:, c], start=(c == 0), stop=(c == KC - 1))
                m.then_inc(ctx_done, 1)

            def keys_values(b):
                pe.wait_ge(ctx_copied, 2 * b + 2)
                pe.matmul(k_ps, wk[:], ctx_k[:], start=True, stop=False)
                pe.matmul(k_ps, bias_k_row[:], proj_sum_k[:], start=False, stop=True)
                pe.matmul(v_ps, ctx_v[:].rearrange("d h k -> d (h k)"), wv[:], start=True, stop=False)
                pe.matmul(v_ps, proj_sum_v[:].rearrange("o h k -> o (h k)"), bias_v_row[:], start=False, stop=True).then_inc(kv_done, 1)

            def cross_q(b):
                pe.wait_ge(x1_hi_ready, b + 1)
                pe.wait_ge(x1_lo_ready, b + 1)
                if isinstance(b, int) and b == 0:
                    pe.wait_ge(y1_ready, B)
                split_product(out_a[:], wq_hi[:], wq_lo[:], x1_hi[:], x1_lo[:], True, True).then_inc(xq_done, 1)

            def cross_score(b, p, t):
                if t == 0:
                    pe.wait_ge(xq_lo_ready, b + 1)
                    pe.wait_ge(keys_lo_ready, b + 1)
                if isinstance(b, int) and b == 0 and t < 2:
                    pe.wait_ge(exp_done, 8 * B)
                else:
                    pe.wait_ge(xsub_done, 4 * b + t - 1)
                n = slice(128 * t, 128 * t + 128)
                split_product(score[t % 2][:], xq_hi[:, n], xq_lo[:, n], keys_hi[p][:], keys_lo[p][:], True, True).then_inc(xscore_done, 1)

            def turn_xprob(b, t):
                pe.wait_ge(xprob_ready, 4 * b + t + 1)
                if t > 1 or not isinstance(b, int) or b > 0:
                    pe.wait_ge(xprobT_ready, 4 * b + t - 1)
                for j in range(XH // HPT):
                    m = pe.transpose(turn[t % 2][:, 128 * j:128 * j + 128], xprob[t][:, HPT * j:HPT * (j + 1)].rearrange("n h k -> n (h k)"), ident[:])
                m.then_inc(xprob_turned, 1)

            def cross_pv(b, p, t):
                pe.wait_ge(xprobT_ready, 4 * b + t + 1)
                if t == 0:
                    pe.wait_ge(values_ready, b + 1)
                    if isinstance(b, int) and b == 0:
                        pe.wait_ge(attn_normed, 2 * B)
                    else:
                        pe.wait_ge(xo_lo_ready, b)
                n = slice(128 * t, 128 * t + 128)
                for j in range(XH // HPT):
                    m = pe.matmul(out_b[32 * j:32 * j + 32, n], values[p][:, j].rearrange("k h d -> k (h d)"), xprobT[t % 2][:, j], start=True, stop=True)
                m.then_inc(xpv_done, 1)

            def cross_m(b):
                pe.wait_ge(xo_lo_ready, b + 1)
                if isinstance(b, int) and b > B - 3:
                    pe.wait_ge(xq_lo_ready, B)
                else:
                    pe.wait_ge(xq_lo_ready, b + 3)
                split_product(out_a[:], wm_hi[:], wm_lo[:], xo_hi[:], xo_lo[:], True, True).then_inc(wm_done, 1)

            def turn_x2(b):
                pe.wait_ge(x2s_ready, b + 1)
                if not isinstance(b, int):
                    pe.wait_ge(xsub_done, 4 * b + 7)
                elif b > 0:
                    pe.wait_ge(x2T_lo_ready, b)
                for c in range(KC):
                    m = pe.transpose(qkv_ps[:, 128 * c:128 * c + 128], x2s[:, 128 * c:128 * c + 128], ident[:])
                m.then_inc(x2_turned, 1)

            pe.wait_ge(cross_lo, 2)
            pe.wait_ge(oT_lo_ready, B)
            pe.wait_ge(proj_sums, 2)

            def cross_step(b, p):
                first, final = isinstance(b, int) and b == 0, isinstance(b, int) and b == B - 1
                cross_score(b, p, 2)
                if not final:
                    context(b + 1, 1 - p)
                if not final:
                    cross_q(b + 1)
                cross_score(b, p, 3)
                if not final:
                    keys_values(b + 1)
                turn_xprob(b, 0)
                turn_xprob(b, 1)
                cross_pv(b, p, 0)
                if not first:
                    cross_m(b - 1)
                turn_xprob(b, 2)
                cross_pv(b, p, 1)
                turn_xprob(b, 3)
                cross_pv(b, p, 2)
                if not final:
                    cross_score(b + 1, 1 - p, 0)
                cross_pv(b, p, 3)
                if not final:
                    cross_score(b + 1, 1 - p, 1)
                if not first:
                    turn_x2(b - 1)

            context(0, 0)
            keys_values(0)
            cross_q(0)
            cross_score(0, 0, 0)
            cross_score(0, 0, 1)

            def logits(half):
                pe.wait_ge(x2T_lo_ready, HB * (half + 1))
                if half == 0:
                    pe.wait_ge(gate_lo_ready, 1)
                for c in range(KC):
                    last = split_product(qkv_ps[0:NE, 0:HB * 128], gate_hi[:, c], gate_lo[:, c],
                                         x2T_hi[:, c].rearrange("f b s -> f (b s)"), x2T_lo[:, c].rearrange("f b s -> f (b s)"), c == 0, c == KC - 1)
                last.then_inc(logits_done, 1)

            def turn_logits(half):
                pe.wait_ge(logitT_ready, half + 1)
                for k in range(HB):
                    m = pe.transpose(qkv_ps[:, NE * k:NE * (k + 1)], logitT[:, 128 * k:128 * (k + 1)], ident[0:NE, 0:NE])
                m.then_inc(logits_turned, 1)

            def ranks(half):
                pe.wait_ge(chosen_ready, half + 1)
                pe.wait_ge(tri_ready, 2)
                b0 = HB * half
                dst = qkv_ps[:, 0:HB * NE]
                pe.matmul(dst, tri_bf[:], chosen_bf[:].rearrange("t b e -> t (b e)"), start=True, stop=False)
                m = pe.matmul(dst, ones_bf[:], before_bf[:, b0:b0 + HB].rearrange("t b e -> t (b e)"), start=False, stop=True)
                if half == 1:
                    m = pe.matmul(qkv_ps[:, 512:512 + NE], ones_bf[:], before_bf[:, B], start=True, stop=True)
                m.then_inc(ranks_done, 1)

            def turn_columns():
                pe.wait_ge(columns_ready, 1)
                for i in range(COLS):
                    m = pe.transpose(qkv_ps[0:1, NT * i:NT * (i + 1)], col[0:NT, i:i + 1], ident[0:NT, 0:NT])
                m.then_inc(columns_turned, 1)

            def shared_gate_up(half, f):
                for j, (bank_, first_) in enumerate(((score[f], sh_gate_done), (turn[f], sh_up_done))):
                    for c in range(KC):
                        w = slice(FF * j + 128 * f, FF * j + 128 * (f + 1))
                        last = split_product(bank_[:], w_hi[:, SETS - 1, c, w], w_lo[:, SETS - 1, c, w],
                                             x2T_hi[:, c].rearrange("f b s -> f (b s)"), x2T_lo[:, c].rearrange("f b s -> f (b s)"), c == 0, c == KC - 1)
                    last.then_inc(first_, 1)

            def shared_down(half, k):
                if k > 1:
                    pe.wait_ge(base_ready, HB * half + k - 1)
                for f in range(FC):
                    t_ = slice(128 * k, 128 * (k + 1))
                    last = split_product((out_a, out_b)[k % 2][:], shT_hi[:, f, t_], shT_lo[:, f, t_], w_hi[:, SETS - 1, KC + f], w_lo[:, SETS - 1, KC + f], f == 0, f == FC - 1)
                last.then_inc(sh_down_done, 1)

            def route_half(half):
                pe.wait_ge(xo_lo_ready, (HB + 1, B)[half])
                if half == 0:
                    pe.wait_ge(xq_lo_ready, HB + 2)
                    pe.wait_ge(xsub_done, 4 * (HB + 1) + 2)
                else:
                    pe.wait_ge(y2_ready, B)
                logits(half)
                turn_logits(half)
                pe.wait_ge(sh_lo_ready, WCH)
                shared_gate_up(half, 0)
                shared_gate_up(half, 1)
                ranks(half)
                if half == 1:
                    turn_columns()
                pe.wait_ge(shT_lo_ready, FC * (half + 1))
                for k in range(HB):
                    shared_down(half, k)
                pe.wait_ge(base_ready, HB * (half + 1))

            cross_step(0, 0)
            with pe.Fori(0, HB // 2) as i:
                cross_step(i * 2 + 1, 1)
                cross_step(i * 2 + 2, 0)
            route_half(0)
            for b in range(HB + 1, B):
                cross_step(b, b % 2)
            cross_m(B - 1)
            turn_x2(B - 1)
            route_half(1)

            def turn_slot(t, q):
                pe.wait_ge(xs_loaded[q], 8 * (t - q) + 16)
                if isinstance(t, int) and t == 0:
                    pe.wait_ge(sh_z_ready, 2 * FC)
                else:
                    pe.wait_ge(xs_lo_ready, t)
                for c in range(KC):
                    m = pe.transpose(turn[0][:, 128 * c:128 * (c + 1)], xs_in[q][:, 128 * c:128 * (c + 1)], ident[:])
                m.then_inc(xs_turned, 1)

            def slot_gate_up(t, q, k, buf):
                pe.wait_ge(w_lo_ready, k * WCH + WCH)
                pe.wait_ge(xs_lo_ready, t + 1)
                if not isinstance(t, int) or t > 1:
                    pe.wait_ge(z_ready, t - 1)
                for c in range(KC):
                    last = split_product(score[q][:], xsT_hi[q][:, c], xsT_lo[q][:, c],
                                         w_hi[:, bass.ds(buf, 1), c].rearrange("k o n -> k (o n)"),
                                         w_lo[:, bass.ds(buf, 1), c].rearrange("k o n -> k (o n)"), c == 0, c == KC - 1)
                last.then_inc(gate_up_done, 1)

            def turn_z(t):
                pe.wait_ge(z_ready, t + 1)
                if not isinstance(t, int) or t > 0:
                    pe.wait_ge(zT_lo_ready, t)
                for f in range(FC):
                    m = pe.transpose(turn[1][:, 128 * f:128 * (f + 1)], z[:, 128 * f:128 * (f + 1)], ident[:])
                m.then_inc(z_turned, 1)

            def slot_down(t, q, buf):
                pe.wait_ge(zT_lo_ready, t + 1)
                if isinstance(t, int) and t < 2:
                    pe.wait_ge(base_ready, B)
                else:
                    pe.wait_ge(y_copied, t - 1)
                for f in range(FC):
                    last = split_product((out_a, out_b)[q][:], zT_hi[:, f], zT_lo[:, f],
                                         w_hi[:, bass.ds(buf, 1), KC + f].rearrange("k o n -> k (o n)"),
                                         w_lo[:, bass.ds(buf, 1), KC + f].rearrange("k o n -> k (o n)"), f == 0, f == FC - 1)
                last.then_inc(slot_done, 1)

            pe.wait_ge(tables_ready, 1)
            turn_slot(0, 0)
            slot_gate_up(0, 0, 0, 0)
            turn_slot(1, 1)

            def step(t, q):
                word = pe.value_load(tab[0:1, 0, bass.ds(t, 1)], min_val=0, max_val=16 * NE - 1)
                k, buf, last = word >> 4, ((word >> 2) % 4).with_bounds(min_val=0, max_val=SETS - 1), (word % 4).with_bounds(min_val=0, max_val=SETS - 1)
                if not isinstance(t, int) or t > 0:
                    slot_down(t - 1, 1 - q, last)
                turn_z(t)
                slot_gate_up(t + 1, 1 - q, k, buf)
                turn_slot(t + 2, q)

            slot_steps(pe, step, 3)

            for b in range(B):
                pe.wait_ge(diag_ready, b + 1)
                if b > 3:
                    pe.wait_ge(out_ready, b - 3)
                total_ps = (score[0], score[1], out_a, out_b)[b % 4][:]
                pe.matmul(total_ps, ident[:], base[:, b], start=True, stop=False)
                pe.wait_ge(gathered_in[b % 4], 64 * (b // 4 + 1))
                for j in range(TOPK):
                    m = pe.matmul(total_ps, diag[b % 2][:, j], gathered[b % 4][:, j], start=False, stop=(j == TOPK - 1))
                m.then_inc(combined, 1)

        @block.vector
        def _(dve):
            dve.memset(stack[:].bitcast(F32)[:, 0:NQ, 3, :], 0.0)
            dve.memset(stack[:].bitcast(F32)[:, NQ:, 3, 2:], 0.0)
            dve.memset(neg_max_parts[:].bitcast(F32)[:, 2:4], 0.0)
            dve.memset(stack[:].bitcast(F32)[:, NQ:, 3, 0:2], 1.0).then_inc(consts_ready, 1)
            for p in (0, 1):
                dve.memset(v_ones[p][:, :, HD:HD + 1], 1.0)
                dve.memset(v_ones[p][:, :, HD + 1:], 0.0)
            dve.memset(ones_col[:], 1.0).then_inc(cross_masks, 1)
            dve.memset(eps[:], EPS)
            dve.memset(neg_half[:], -0.5).then_inc(consts_ready, 1)
            dve.wait_ge(consts_in, 48)
            dve.tensor_copy(ident_bf[:], ident[:]).then_inc(consts_ready, 1)
            dve.tensor_copy(causal_bf[:], causal[:].rearrange("s (o t) -> s o t", o=1).to_broadcast([128, REP, 128])).then_inc(consts_ready, 1)

            def x_lo(b, p):
                dve.wait_ge(xT_hi_ready, b + 1)
                if not isinstance(b, int) or b > 1:
                    dve.wait_ge(qkv_done, b - 1)
                dve.tensor_tensor(xT_lo[p][:], xT[:, p], xT_hi[p][:].bitcast(F32), ALU.subtract).then_inc(xT_lo_ready, 1)

            def rope_products(b, p):
                dve.wait_ge(qkv_done, b + 1)
                if not isinstance(b, int) or b > 0:
                    dve.wait_ge(rot_ready, 2 * b)
                qk = qkv_ps[:, 0:QK_HEADS * HD].rearrange("s (h e) -> s h e", e=HD)
                for j, dst in ((0, rope_cos), (1, rope_sin)):
                    f = rope[:, j:j + 1].to_broadcast([128, QK_HEADS, HD])
                    m = dve.tensor_tensor(dst[:].rearrange("s h a e -> s h (a e)"), qk, f, ALU.mult)
                m.then_inc(rope_read, 1)

            def low_parts(b):
                dve.wait_ge(stack_hi, 2 * b + 2)
                dve.tensor_tensor(stack[:, 0:NQ, 2], rotated[:, 0:NQ], stack[:, 0:NQ, 0].bitcast(F32), ALU.subtract).then_inc(stack_lo, 1)
                dve.tensor_tensor(stack[:, NQ:, 1], rotated[:, NQ:], stack[:, NQ:, 0].bitcast(F32), ALU.subtract).then_inc(stack_lo, 1)

            def qkT_copies(b, p):
                for r in range(5):
                    dst = kT[p][:] if r == 0 else qT[p][:, 4 * r - 4:4 * r]
                    if r % 2:
                        dve.wait_ge(qkT_turned, 5 * b + r + 1)
                        dve.tensor_copy(dst.rearrange("k r s -> k (r s)"), turn[1][:]).then_inc(qkT_by_dve, 1)
                        dve.wait_ge(qkT_by_dve, 2 * b + r // 2 + 1)
                    else:
                        dve.wait_ge(qkT_by_act, 3 * b + r // 2 + 1)
                    if r == 0:
                        dve.tensor_copy(kT_half[:], dst.bitcast(F32)).then_inc(halves_ready, 1)
                    else:
                        dve.tensor_copy(qT_half[:, 4 * r - 4:4 * r], dst.bitcast(F32)).then_inc(halves_ready, 1)

            def maxima(b):
                for g in range(NKV):
                    dve.wait_ge(pass1_done, 8 * b + g + 1)
                    dve.tensor_reduce(neg_max[:, g], score[g % 2][:].rearrange("s (r t) -> s r t", r=REP), AX.X, ALU.max,
                                      negate=True).then_inc(max_done, 1)
                    if not isinstance(b, int) or b > 0:
                        if g == 3:
                            normalise(b - 1, 0)
                            normalise(b - 1, 1)
                        if g == 7:
                            o_lo(b - 1)
                dve.wait_ge(max_done, 8 * b + 8)
                nm = neg_max[:].rearrange("s (u a) r -> s a u r", a=2)
                dve.tensor_copy(neg_max_parts[:, 0:2, 0], nm).then_inc(max_hi, 1)
                dve.wait_ge(max_hi, b + 1)
                dve.tensor_tensor(neg_max_parts[:, 0:2, 1], nm, neg_max_parts[:, 0:2, 0].bitcast(F32), ALU.subtract).then_inc(max_parts, 1)

            def normalise(b, half):
                src = (out_a, out_b)[half][:].rearrange("s (r j e) -> s r j e", r=REP, e=32)
                rs = attn_rsum[:, half]
                dve.wait_ge(pv_turned, 2 * b + half + 1)
                dve.reciprocal(rs, src[:, :, :, HD]).then_inc(rsum_ready, 1)
                dve.wait_ge(rsum_ready, 2 * b + half + 1)
                dst = attn_out[:, half].rearrange("s (j r) e -> s r j e", r=REP)
                dve.tensor_tensor(dst, src[:, :, :, 0:HD], rs.rearrange("s r (j o) -> s r j o", o=1).to_broadcast([128, REP, 4, HD]),
                                  ALU.mult).then_inc(attn_normed, 1)

            def o_lo(b):
                dve.wait_ge(oT_hi_ready, b + 1)
                dve.tensor_tensor(oT_lo[:].rearrange("k c s -> k (c s)"), turn[1][:], oT_hi[:].rearrange("k c s -> k (c s)").bitcast(F32),
                                  ALU.subtract).then_inc(oT_lo_ready, 1)

            def residual1(b, p):
                dve.wait_ge(wo_done, b + 1)
                dve.wait_ge(x_loaded[p], 8 * (b - p) + 16)
                dve.tensor_tensor(y1[:], out_a[:], x_in[:, p], ALU.add).then_inc(y1_ready, 1)
                dve.wait_ge(y1_ready, b + 1)
                dve.bn_stats(bn6[:], y1[:]).then_inc(stats, 1)
                dve.wait_ge(stats, b + 1)
                dve.sem_inc(held)
                dve.bn_aggr(mean_var[:], bn6[:]).then_inc(mv1, 1)

            def x1_write(b):
                dve.wait_ge(rstd1, b + 1)
                dve.wait_ge(mv1, b + 1)
                dve.tensor_scalar(x1[:, bass.ds(b, 1)].rearrange("s o d -> s (o d)"), y1[:], mean_var[:, 0:1], rstd[:, 0:1],
                                  ALU.subtract, ALU.mult).then_inc(x1_ready, 1)

            x_lo(0, 0)
            for c in range(KC):
                dve.wait_ge(wqkv_hi_ready, c + 1)
                dve.tensor_tensor(wqkv_lo[:, c], wst[:, c], wqkv_hi[:, c].bitcast(F32), ALU.subtract).then_inc(wqkv_lo_ready, 1)
            x_lo(1, 1)
            dve.wait_ge(wo_hi_ready, 1)
            dve.tensor_tensor(wo_lo[:], wo_in[:], wo_hi[:].bitcast(F32), ALU.subtract).then_inc(wo_lo_ready, 1)
            rope_products(0, 0)
            low_parts(0)
            qkT_copies(0, 0)

            def step(b, p):
                first, final = isinstance(b, int) and b == 0, isinstance(b, int) and b == B - 1
                maxima(b)
                if not final:
                    rope_products(b + 1, 1 - p)
                if not first:
                    residual1(b - 1, 1 - p)
                if not final:
                    low_parts(b + 1)
                if not first:
                    x1_write(b - 1)
                if not (isinstance(b, int) and b >= B - 2):
                    x_lo(b + 2, p)
                if not final:
                    qkT_copies(b + 1, 1 - p)

            step(0, 0)
            with dve.Fori(0, (B - 4) // 2) as i:
                step(i * 2 + 1, 1)
                step(i * 2 + 2, 0)
            step(B - 3, 1)
            step(B - 2, 0)
            step(B - 1, 1)
            normalise(B - 1, 0)
            normalise(B - 1, 1)
            o_lo(B - 1)
            for j, (w, hi, lo) in enumerate(((wq_in, wq_hi, wq_lo), (wm_in, wm_hi, wm_lo))):
                dve.wait_ge(cross_hi, j + 1)
                dve.tensor_tensor(lo[:], w[:], hi[:].bitcast(F32), ALU.subtract).then_inc(cross_lo, 1)
            residual1(B - 1, 1)
            x1_write(B - 1)

            dve.wait_ge(wo_done, B)
            dve.wait_ge(max_rows, 32 * B)

            def head_keys(b, p):
                dve.wait_ge(kv_done, b + 1)
                if not isinstance(b, int) or b > 0:
                    dve.wait_ge(keys_lo_ready, b)
                    dve.wait_ge(keys_hi_ready, b)
                k = k_ps.rearrange("c (o k) -> c o k", o=1).to_broadcast([128, XH, XK])
                dve.tensor_tensor(keys[:], k, head_mask[:].rearrange("c (h o) -> c h o", o=1).to_broadcast([128, XH, XK]), ALU.mult).then_inc(keys_ready, 1)
                if not isinstance(b, int) or b > 1:
                    dve.wait_ge(xpv_done, 4 * b - 4)
                v = v_ps.rearrange("k (j h d) -> k j h d", j=XH // HPT, h=HPT)
                vm = value_mask[:].rearrange("k (a h d) -> k a h d", a=1, d=1).to_broadcast([128, XH // HPT, HPT, XD])
                dve.tensor_tensor(values[p][:], v, vm, ALU.mult).then_inc(values_ready, 1)

            def keys_low(b, p):
                dve.wait_ge(keys_hi_ready, b + 1)
                dve.tensor_tensor(keys_lo[p][:], keys[:].rearrange("c h k -> c (h k)"), keys_hi[p][:].bitcast(F32), ALU.subtract).then_inc(keys_lo_ready, 1)

            def x1_low(b):
                dve.wait_ge(x1_hi_ready, b + 1)
                dve.tensor_tensor(x1_lo[:], x1[:, bass.ds(b, 1)].rearrange("s o d -> s (o d)"), x1_hi[:].bitcast(F32), ALU.subtract).then_inc(x1_lo_ready, 1)

            def xq_low(b):
                dve.wait_ge(xq_hi_ready, b + 1)
                dve.scalar_tensor_tensor(out=xq_lo[:], in0=out_a[:], scalar=bias_q[:, 0:1], in1=xq_hi[:].bitcast(F32), op0=ALU.add, op1=ALU.subtract).then_inc(xq_lo_ready, 1)

            def xmax_sub(b, t):
                dve.wait_ge(xscore_done, 4 * b + t + 1)
                sc = score[t % 2][:].rearrange("n (h k) -> n h k", k=XK)
                dve.tensor_reduce(xmax[:, t], sc, AX.X, ALU.max).then_inc(xmax_ready, 1)
                dve.wait_ge(xmax_ready, 4 * b + t + 1)
                if not isinstance(b, int) or b > 0:
                    dve.wait_ge(xprob_turned, 4 * b + t - 3)
                dve.tensor_tensor(xprob[t][:], sc, xmax[:, t].rearrange("n (h o) -> n h o", o=1).to_broadcast([128, XH, XK]), ALU.subtract).then_inc(xsub_done, 1)

            def xsum_rec(b, t):
                dve.wait_ge(xexp_done, 4 * b + t + 1)
                if not isinstance(b, int) or b > 0:
                    dve.wait_ge(xprob_ready, 4 * b + t - 3)
                dve.tensor_reduce(xsum[:, t], xprob[t][:], AX.X, ALU.add).then_inc(xsum_ready, 1)
                dve.wait_ge(xsum_ready, 4 * b + t + 1)
                dve.reciprocal(xrec[:, t], xsum[:, t]).then_inc(xrec_ready, 1)

            def xo_low(b):
                dve.wait_ge(xo_hi_ready, b + 1)
                dve.tensor_tensor(xo_lo[:], out_b[:], xo_hi[:].bitcast(F32), ALU.subtract).then_inc(xo_lo_ready, 1)

            def residual2(b):
                dve.wait_ge(wm_done, b + 1)
                dve.scalar_tensor_tensor(out=y2[:], in0=out_a[:], scalar=bias_m[:, 0:1], in1=x1[:, bass.ds(b, 1)].rearrange("s o d -> s (o d)"),
                                         op0=ALU.add, op1=ALU.add).then_inc(y2_ready, 1)
                dve.wait_ge(y2_ready, b + 1)
                dve.bn_stats(bn6b[:], y2[:]).then_inc(stats, 1)
                dve.wait_ge(stats, b + B + 1)
                dve.sem_inc(held)
                dve.bn_aggr(mean_var2[:], bn6b[:]).then_inc(mv2, 1)

            def x2_write(b):
                dve.wait_ge(rstd2_ready, b + 1)
                dve.wait_ge(mv2, b + 1)
                dve.tensor_scalar(x2s[:], y2[:], mean_var2[:, 0:1], rstd2[:, 0:1], ALU.subtract, ALU.mult).then_inc(x2s_ready, 1)
                dve.wait_ge(x2s_ready, b + 1)

            def x2T_low(b):
                dve.wait_ge(x2T_hi_ready, b + 1)
                lo, hi = (half_place(t, b) for t in (x2T_lo, x2T_hi))
                dve.tensor_tensor(lo, qkv_ps[:, 0:D].rearrange("f (c s) -> f c s", c=KC), hi.bitcast(F32), ALU.subtract).then_inc(x2T_lo_ready, 1)

            def cross_step(b, p):
                first, final = isinstance(b, int) and b == 0, isinstance(b, int) and b == B - 1
                if not final:
                    x1_low(b + 1)
                xsum_rec(b, 0)
                xmax_sub(b, 2)
                xsum_rec(b, 1)
                xmax_sub(b, 3)
                if not final:
                    xq_low(b + 1)
                xsum_rec(b, 2)
                xsum_rec(b, 3)
                if not final:
                    head_keys(b + 1, 1 - p)
                if not first:
                    residual2(b - 1)
                if not final:
                    keys_low(b + 1, 1 - p)
                    xmax_sub(b + 1, 0)
                if not first:
                    x2_write(b - 1)
                xo_low(b)
                if not final:
                    xmax_sub(b + 1, 1)
                if not first:
                    x2T_low(b - 1)

            dve.wait_ge(cross_in, 16 * 11)
            x1_low(0)
            head_keys(0, 0)
            keys_low(0, 0)
            xq_low(0)
            xmax_sub(0, 0)
            xmax_sub(0, 1)

            routed = [0]

            def link(ins):
                routed[0] += 1
                ins.then_inc(route, 1)
                dve.wait_ge(route, routed[0])

            def wide(ap, n):
                return ap.rearrange("t (b o) -> t b o", o=1).to_broadcast([128, HB, n])

            def choose(half, meanwhile):
                bs = slice(HB * half, HB * (half + 1))
                dve.wait_ge(logit_exp, half + 1)
                link(dve.tensor_scalar(e_score[:], e_score[:], 1.0, None, ALU.add))
                link(dve.reciprocal(e_score[:], e_score[:]))
                link(dve.tensor_tensor(e_score[:], e_score[:], bias_e[:].rearrange("t (o e) -> t o e", o=1).to_broadcast([128, HB, NE]), ALU.add))
                for j in range(TOPK):
                    best, one = weight[:, j, bs], picked[:, j, bs]
                    link(dve.tensor_reduce(best, e_score[:], AX.X, ALU.max))
                    link(dve.tensor_tensor(e_eq[:], e_score[:], wide(best, NE), ALU.is_equal))
                    io = iota16[:].rearrange("t (o e) -> t o e", o=1).to_broadcast([128, HB, NE])
                    link(dve.tensor_tensor(e_eq[:], e_eq[:], io, ALU.mult))
                    link(dve.tensor_reduce(e_low[:], e_eq[:], AX.X, ALU.min))
                    link(dve.tensor_tensor(one, io, wide(e_low[:], NE), ALU.is_equal))
                    link(dve.scalar_tensor_tensor(out=e_score[:], in0=one, scalar=MASKED, in1=e_score[:], op0=ALU.mult, op1=ALU.add))
                    if j == 1:
                        meanwhile()
                link(dve.tensor_scalar(chosen[:], e_score[:], MASKED / 10, None, ALU.is_lt))
                link(dve.tensor_copy(chosen_bf[:], chosen[:]))
                for k in range(HB):
                    b = HB * half + k
                    link(dve.tensor_tensor(before[:, b + 1], before[:, b], chosen[:, k], ALU.add))
                m = dve.tensor_copy(before_bf[:, HB * half:HB * (half + 1) + 1], before[:, HB * half:HB * (half + 1) + 1])
                m.then_inc(chosen_ready, 1)
                link(dve.tensor_reduce(w_sum[:], weight[:, :, bs].rearrange("t j b -> t b j"), AX.X, ALU.add))
                link(dve.tensor_scalar(w_sum[:], w_sum[:], 1e-20, None, ALU.add))
                link(dve.reciprocal(w_rec[:], w_sum[:]))
                link(dve.tensor_tensor(weight[:, :, bs], weight[:, :, bs], w_rec[:].rearrange("t (o b) -> t o b", o=1).to_broadcast([128, TOPK, HB]), ALU.mult))

            def place_rows(half):
                bs = slice(HB * half, HB * (half + 1))
                dve.wait_ge(ranks_done, half + 1)
                m = dve.tensor_copy(rank[:, bs], qkv_ps[:, 0:HB * NE].rearrange("t (b e) -> t b e", e=NE))
                link(m)
                if half == 1:
                    link(dve.tensor_copy(count[:], qkv_ps[:, 512:512 + NE]))
                link(dve.tensor_tensor(place[:, bs], rank[:, bs], region[:].rearrange("t (o e) -> t o e", o=1).to_broadcast([128, HB, NE]), ALU.add))
                for j in range(TOPK):
                    link(dve.tensor_tensor(picked_place[:, j, bs], picked[:, j, bs], place[:, bs], ALU.mult))
                link(dve.tensor_reduce(row_f[:, :, bs], picked_place[:, :, bs], AX.X, ALU.add))
                dve.tensor_copy(row_of[:, :, bs], row_f[:, :, bs]).then_inc(rows_ready, 1)

            def slot_tables():
                cb = count[:].rearrange("t (e o) -> t e o", o=1).to_broadcast([128, NE, 8])
                link(dve.tensor_tensor(pad_f[:], count[0:1], region[0:1], ALU.add))
                dve.tensor_copy(pad_row[:], pad_f[:]).then_inc(pads_ready, 1)
                link(dve.tensor_tensor(over[:], cb, thresholds[:].rearrange("t (o k) -> t o k", o=1).to_broadcast([128, NE, 8]), ALU.is_gt))
                link(dve.tensor_reduce(n_slots[:], over[:], AX.X, ALU.add))
                link(dve.tensor_scalar(n_slots[:, 0:2], n_slots[:, 0:2], 1.0, None, ALU.max))
                link(dve.tensor_tensor(prod[:], n_slots[:].rearrange("t (o e) -> t o e", o=1).to_broadcast([128, NE, NE]), upto_mask[:], ALU.mult))
                link(dve.tensor_reduce(slots_to[:], prod[:], AX.X, ALU.add))
                link(dve.tensor_tensor(slot_base[:], slots_to[:], n_slots[:], ALU.subtract))
                link(dve.tensor_scalar(in_use[:], n_slots[:], 0.0, None, ALU.is_gt))
                link(dve.tensor_tensor(prod[:], in_use[:].rearrange("t (o e) -> t o e", o=1).to_broadcast([128, NE, NE]), upto_mask[:], ALU.mult))
                link(dve.tensor_reduce(used_to[:], prod[:], AX.X, ALU.add))
                link(dve.tensor_scalar(last_used[:], used_to[:, NE - 1:NE], -1.0, None, ALU.add))
                link(dve.tensor_scalar(slot_no_2[:], slot_no[:], -2.0, None, ALU.add))

                def total(dst, values=None):
                    if values is not None:
                        link(dve.tensor_tensor(passed_n[:], passed[:], values[:], ALU.mult))
                    link(dve.tensor_reduce(dst, (passed if values is None else passed_n)[:], AX.X, ALU.add))

                def column(i):
                    return col[:, i:i + 1]

                link(dve.tensor_scalar(passed[:], slots_to[:], slot_no[:, 0:1], None, ALU.is_le))
                total(column(0), in_use)
                total(work[:, 0:1])
                total(work[:, 1:2], n_slots)
                link(dve.tensor_tensor(column(0), column(0), last_used[:], ALU.min))
                link(dve.tensor_tensor(work[:, 1:2], slot_no[:], work[:, 1:2], ALU.subtract))
                link(dve.tensor_scalar(work[:, 2:3], work[:, 1:2], float(SLOT), None, ALU.mult))
                link(dve.scalar_tensor_tensor(out=work[:, 0:1], in0=work[:, 0:1], scalar=float(REGION), in1=work[:, 2:3], op0=ALU.mult, op1=ALU.add))
                link(dve.tensor_scalar(column(2), work[:, 0:1], float(IDLE_ROW), None, ALU.min))
                link(dve.tensor_scalar(work[:, 1:2], work[:, 1:2], 0.0, None, ALU.is_equal))
                link(dve.tensor_tensor(work[:, 2:3], column(0), last_used[:], ALU.is_lt))
                link(dve.tensor_tensor(work[:, 1:2], work[:, 1:2], work[:, 2:3], ALU.mult))
                link(dve.tensor_tensor(work[:, 3:4], slots_to[:, NE - 1:NE], slot_no[:], ALU.subtract))
                link(dve.tensor_scalar(work[:, 3:4], work[:, 3:4], 1.0, 2.0, ALU.add, ALU.min))
                link(dve.tensor_scalar(column(4), work[:, 3:4], 0.0, None, ALU.max))
                link(dve.tensor_tensor(work[:, 3:4], slot_no[:], slots_to[:, NE - 1:NE], ALU.is_lt))
                link(dve.tensor_scalar(column(6), work[:, 3:4], 16.0, None, ALU.mult))
                link(dve.tensor_scalar(over_rounds[:], rounds[:], column(0), None, ALU.is_le))
                link(dve.tensor_reduce(work[:, 3:4], over_rounds[:], AX.X, ALU.add))
                link(dve.scalar_tensor_tensor(out=column(1), in0=work[:, 3:4], scalar=-float(SETS), in1=column(0), op0=ALU.mult, op1=ALU.add))
                link(dve.tensor_scalar(work[:, 3:4], column(1), float(SETS - 1), -float(SETS), ALU.is_ge, ALU.mult))
                link(dve.scalar_tensor_tensor(out=work[:, 2:3], in0=column(1), scalar=1.0, in1=work[:, 3:4], op0=ALU.add, op1=ALU.add))
                link(dve.scalar_tensor_tensor(out=work[:, 3:4], in0=column(0), scalar=4.0, in1=work[:, 2:3], op0=ALU.mult, op1=ALU.add))
                link(dve.scalar_tensor_tensor(out=column(3), in0=work[:, 3:4], scalar=4.0, in1=work[:, 1:2], op0=ALU.add, op1=ALU.mult))
                link(dve.scalar_tensor_tensor(out=column(0), in0=column(0), scalar=4.0, in1=column(1), op0=ALU.mult, op1=ALU.add))
                link(dve.tensor_scalar(passed[:], used_to[:], slot_no[:, 0:1], None, ALU.is_le))
                total(work[:, 0:1])
                link(dve.tensor_scalar(column(7), work[:, 0:1], float(NE - 1), None, ALU.min))
                link(dve.tensor_scalar(column(8), work[:, 0:1], float(NE), None, ALU.is_lt))
                link(dve.tensor_scalar(passed[:], used_to[:], slot_no_2[:, 0:1], None, ALU.is_le))
                link(dve.tensor_tensor(passed_n[:], passed[:], n_slots[:], ALU.mult))
                dve.tensor_reduce(column(9), passed_n[:], AX.X, ALU.add).then_inc(columns_ready, 1)
                dve.wait_ge(columns_turned, 1)
                link(dve.tensor_reduce(stored_f[:], qkv_ps[0:1, 6 * NT:7 * NT].rearrange("o (t q) -> o q t", q=2), AX.X, ALU.add))
                dve.tensor_copy(stored[:], stored_f[:])
                link(dve.memset(tab_f[:], 0.0))
                link(dve.tensor_copy(tab_f[:, 1:], qkv_ps[0:1, NT:2 * NT]))
                link(dve.scalar_tensor_tensor(out=tab_f[:, 0:NT - 1], in0=qkv_ps[0:1, 1:NT], scalar=4.0, in1=tab_f[:, 0:NT - 1], op0=ALU.mult, op1=ALU.add))
                dve.tensor_copy(tab[:, 0], tab_f[:, 0:NT])
                dve.tensor_copy(tab[:, 1:], qkv_ps[0:1, NT:COLS * NT].rearrange("o (i t) -> o i t", t=NT)).then_inc(tables_ready, 1)

            def result_rows():
                link(dve.tensor_scalar(slot_base[:], slot_base[:], float(SLOT), None, ALU.mult))
                link(dve.tensor_tensor(place[:], rank[:], slot_base[:].rearrange("t (o e) -> t o e", o=1).to_broadcast([128, B, NE]), ALU.add))
                for j in range(TOPK):
                    link(dve.tensor_tensor(picked_place[:, j], picked[:, j], place[:], ALU.mult))
                link(dve.tensor_reduce(row_f[:], picked_place[:], AX.X, ALU.add))
                dve.tensor_copy(yrow_of[:], row_f[:]).then_inc(yrows_ready, 1)

            def split_low(buf, hi_sem, lo_sem, have, chunks=range(WCH)):
                for c in chunks:
                    dve.wait_ge(hi_sem, have + c + 1)
                    dve.sem_inc(held)
                    hi, lo = (w[:, bass.ds(buf, 1), bass.ds(c, 1)].rearrange("k o c n -> k (o c n)") for w in (w_hi, w_lo))
                    raw = w_raw[:, bass.ds(buf, 1), bass.ds(c, 1)].rearrange("k o c n -> k (o c n)")
                    dve.tensor_tensor(lo, raw, hi.bitcast(F32), ALU.subtract).then_inc(lo_sem, 1)

            def shared_z(half, f):
                n = FC * half + f
                dve.wait_ge(sh_silu_done, n + 1)
                dve.wait_ge(sh_up_done, n + 1)
                dve.tensor_tensor(sh_z[:], turn[f][:], sh_z[:], ALU.mult).then_inc(sh_z_ready, 1)
                dve.wait_ge(shT_hi_ready, n + 1)
                dve.tensor_tensor(shT_lo[:, f], sh_z[:], shT_hi[:, f].bitcast(F32), ALU.subtract).then_inc(shT_lo_ready, 1)

            def shared_base(half, k):
                b = HB * half + k
                dve.wait_ge(sh_down_done, b + 1)
                dve.wait_ge(x2_ready, b + 1)
                dve.tensor_tensor(base[:, b], (out_a, out_b)[k % 2][:], x2[:, b], ALU.add).then_inc(base_ready, 1)

            dve.memset(before[:, 0], 0.0)
            dve.memset(ones_bf[:], 1.0).then_inc(tri_ready, 1)
            dve.memset(zeros[:], 0.0).then_inc(zeros_ready, 1)
            dve.wait_ge(moe_in, 16 * 9)
            dve.tensor_copy(tri_bf[:], tri[:]).then_inc(tri_ready, 1)
            dve.wait_ge(gate_hi_ready, 1)
            dve.tensor_tensor(gate_lo[:], gate_in[:], gate_hi[:].bitcast(F32), ALU.subtract).then_inc(gate_lo_ready, 1)

            def route_half(half):
                dve.wait_ge(logits_done, half + 1)
                if half == 1:
                    dve.wait_ge(logits_turned, 1)
                dve.tensor_copy(logitT[:], qkv_ps[0:NE, 0:HB * 128]).then_inc(logitT_ready, 1)
                choose(half, lambda: shared_z(half, 0))
                if half == 0:
                    shared_z(half, 1)
                place_rows(half)
                if half == 1:
                    slot_tables()
                    shared_z(half, 1)
                for k in range(HB):
                    shared_base(half, k)

            cross_step(0, 0)
            with dve.Fori(0, HB // 2) as i:
                cross_step(i * 2 + 1, 1)
                split_low(SETS - 1, sh_hi_ready, sh_lo_ready, 0, [i * 3 + c for c in range(WCH // 2)])
                cross_step(i * 2 + 2, 0)
            route_half(0)
            for b in range(HB + 1, B):
                cross_step(b, b % 2)
                k = 2 * (b - HB - 1)
                split_low(0, w_hi_ready, w_lo_ready, 0, range(k, k + 2))
            residual2(B - 1)
            x2_write(B - 1)
            x2T_low(B - 1)
            route_half(1)
            result_rows()

            def slot_x_low(t, q):
                dve.wait_ge(xs_hi_ready, t + 1)
                if not isinstance(t, int) or t > 1:
                    dve.wait_ge(gate_up_done, t - 1)
                dve.tensor_tensor(xsT_lo[q][:].rearrange("f c s -> f (c s)"), turn[0][:], xsT_hi[q][:].rearrange("f c s -> f (c s)").bitcast(F32),
                                  ALU.subtract).then_inc(xs_lo_ready, 1)

            def slot_z(t, q):
                dve.wait_ge(silu_done, t + 1)
                if not isinstance(t, int) or t > 0:
                    dve.wait_ge(z_turned, t)
                dve.tensor_tensor(z[:], silu_g[:], score[q][:, FF:2 * FF], ALU.mult).then_inc(z_ready, 1)

            def slot_z_low(t):
                dve.wait_ge(zT_hi_ready, t + 1)
                if not isinstance(t, int) or t > 0:
                    dve.wait_ge(slot_done, t)
                dve.tensor_tensor(zT_lo[:].rearrange("f c s -> f (c s)"), turn[1][:, 0:FF], zT_hi[:].rearrange("f c s -> f (c s)").bitcast(F32),
                                  ALU.subtract).then_inc(zT_lo_ready, 1)

            def next_expert_low(t, word, chunks):
                with dve.If(word > 0):
                    k, buf = (word >> 2) - 1, (word % 4).with_bounds(min_val=0, max_val=SETS - 1)
                    split_low(buf, w_hi_ready, w_lo_ready, (k + 1) * WCH, chunks)

            slot_x_low(0, 0)

            def step(t, q):
                word = dve.value_load(tab[0:1, 3, bass.ds(t, 1)], min_val=0, max_val=4 * NE)
                next_expert_low(t, word, EARLY)
                slot_z(t, q)
                slot_x_low(t + 1, 1 - q)
                next_expert_low(t, word, LATE)
                slot_z_low(t)

            slot_steps(dve, step, 1)

            def diagonals(b):
                if b > 1:
                    dve.wait_ge(combined, b - 1)
                for j in range(TOPK):
                    m = dve.tensor_scalar(diag[b % 2][:, j], ident[:], weight[:, j, b:b + 1], None, ALU.mult)
                m.then_inc(diag_ready, 1)

            def statistics(b):
                dve.wait_ge(combined, b + 1)
                dve.bn_stats(bn6c[:, b % 2], (score[0], score[1], out_a, out_b)[b % 4][:]).then_inc(stats, 1)
                dve.wait_ge(stats, b + 2 * B + 1)
                dve.bn_aggr(mean_var3[:, b // 2 % 2, b % 2], bn6c[:, b % 2]).then_inc(mv3, 1)

            def out_write(b):
                dve.wait_ge(rstd3_ready, b // 2 + 1)
                if b > 1:
                    dve.wait_ge(out_in[b % 2], 16 * (b // 2))
                pair = b // 2 % 2
                dve.tensor_scalar(out_sb[b % 2], (score[0], score[1], out_a, out_b)[b % 4][:], mean_var3[:, pair, b % 2, 0:1], rstd3[:, pair, b % 2:b % 2 + 1],
                                  ALU.subtract, ALU.mult).then_inc(out_ready, 1)

            dve.wait_ge(results_stored, 1)
            diagonals(0)
            diagonals(1)
            for b in range(0, B, 2):
                statistics(b)
                if b + 2 < B:
                    diagonals(b + 2)
                statistics(b + 1)
                if b + 2 < B:
                    diagonals(b + 3)
                out_write(b)
                out_write(b + 1)

        @block.scalar
        def _(act):
            def x_hi(b, p):
                act.wait_ge(xT_in[p], 8 * (b - p) + 16)
                if not isinstance(b, int) or b > 1:
                    act.wait_ge(qkv_done, b - 1)
                act.copy(xT_hi[p][:], xT[:, p]).then_inc(xT_hi_ready, 1)

            def v_copy(b, p):
                act.wait_ge(rope_read, b + 1)
                if not isinstance(b, int) or b > 1:
                    act.wait_ge(pv_done, 8 * b - 8)
                act.copy(v_ones[p][:, :, 0:HD], qkv_ps[:, QK_HEADS * HD:QKV].rearrange("s (g e) -> s g e", e=HD)).then_inc(v_ready, 1)

            def high_parts(b):
                act.wait_ge(rot_ready, 2 * b + 2)
                if not isinstance(b, int) or b > 0:
                    act.wait_ge(qkT_turned, 5 * b)
                r = rotated[:].rearrange("s h (o e) -> s h o e", o=1)
                act.copy(stack[:, 0:NQ, 0:2], r[:, 0:NQ].to_broadcast([128, NQ, 2, HD])).then_inc(stack_hi, 1)
                act.copy(stack[:, NQ:, 0:3:2], r[:, NQ:].to_broadcast([128, NKV, 2, HD])).then_inc(stack_hi, 1)

            def qkT_copies(b, p, rounds=(0, 2, 4)):
                for r in rounds:
                    act.wait_ge(qkT_turned, 5 * b + r + 1)
                    dst = kT[p][:] if r == 0 else qT[p][:, 4 * r - 4:4 * r]
                    act.copy(dst.rearrange("k r s -> k (r s)"), turn[0][:]).then_inc(qkT_by_act, 1)

            def maxT_copy(b):
                act.wait_ge(max_turned, b + 1)
                if not isinstance(b, int) or b > 0:
                    act.wait_ge(max_rows, 32 * b)
                act.copy(maxT[:], out_b[0:64, 0:128]).then_inc(maxT_ready, 1)

            def exps(b, groups):
                for g in groups:
                    act.wait_ge(pass2_done, 8 * b + g + 1)
                    if g >= 4 or not isinstance(b, int) or b > 0:
                        act.wait_ge(pv_done, 8 * b + g - 3)
                    act.activation(probs[g % 4][:].rearrange("t r s -> t (r s)"), score[g % 2][:], ACT.Exp,
                                   scale=float(HD) ** -0.5).then_inc(exp_done, 1)

            def pv_copy(b, half):
                act.wait_ge(pv_done, 8 * b + 4 * half + 4)
                act.copy(pv_sb[half][:].rearrange("k r s -> k (r s)"), (out_a, out_b)[half][:]).then_inc(pv_copied, 1)

            def o_hi(b):
                act.wait_ge(oT_turned, b + 1)
                act.copy(oT_hi[:].rearrange("k c s -> k (c s)"), turn[1][:]).then_inc(oT_hi_ready, 1)

            x_hi(0, 0)
            for c in range(KC):
                act.wait_ge(wqkv_in[c], 16)
                act.copy(wqkv_hi[:, c], wst[:, c]).then_inc(wqkv_hi_ready, 1)
            x_hi(1, 1)
            act.wait_ge(wo_loaded, 16)
            act.copy(wo_hi[:], wo_in[:]).then_inc(wo_hi_ready, 1)
            v_copy(0, 0)
            high_parts(0)
            qkT_copies(0, 0)

            def step(b, p):
                final = isinstance(b, int) and b == B - 1
                if not isinstance(b, int) or b > 0:
                    pv_copy(b - 1, 0)
                    pv_copy(b - 1, 1)
                    o_hi(b - 1)
                maxT_copy(b)
                if not final:
                    v_copy(b + 1, 1 - p)
                    high_parts(b + 1)
                exps(b, range(4))
                if not (isinstance(b, int) and b >= B - 2):
                    x_hi(b + 2, p)
                exps(b, range(4, NKV - 2))
                if not final:
                    qkT_copies(b + 1, 1 - p, (0,))
                exps(b, (NKV - 2,))
                exps(b, (NKV - 1,))
                if not final:
                    qkT_copies(b + 1, 1 - p, (2, 4))

            step(0, 0)
            with act.Fori(0, (B - 4) // 2) as i:
                step(i * 2 + 1, 1)
                step(i * 2 + 2, 0)
            step(B - 3, 1)
            step(B - 2, 0)
            step(B - 1, 1)

            pv_copy(B - 1, 0)
            pv_copy(B - 1, 1)
            o_hi(B - 1)

            act.wait_ge(cross_in, 16 * 11)
            act.copy(wq_hi[:], wq_in[:]).then_inc(cross_hi, 1)
            act.copy(wm_hi[:], wm_in[:]).then_inc(cross_hi, 1)
            act.wait_ge(proj_summed, 1)
            act.copy(proj_sum_k[:], qkv_ps[0:1, 0:XK]).then_inc(proj_sums, 1)
            act.copy(proj_sum_v[:], qkv_ps[0:1, XK:2 * XK].rearrange("o (a k) -> o a k", a=1).to_broadcast([1, HPT, XK])).then_inc(proj_sums, 1)

            def ctx_copy(b):
                act.wait_ge(ctx_done, b + 1)
                if not isinstance(b, int) or b > 0:
                    act.wait_ge(kv_done, b)
                act.copy(ctx_k[:], ctx_ps[:, 0:XK]).then_inc(ctx_copied, 1)
                act.copy(ctx_v[:], ctx_ps[:, XK:2 * XK].rearrange("d (a k) -> d a k", a=1).to_broadcast([128, HPT, XK])).then_inc(ctx_copied, 1)

            def x1_high(b):
                if not isinstance(b, int) or b > 0:
                    act.wait_ge(xq_done, b)
                act.copy(x1_hi[:], x1[:, bass.ds(b, 1)].rearrange("s o d -> s (o d)")).then_inc(x1_hi_ready, 1)

            def xq_high(b):
                act.wait_ge(xq_done, b + 1)
                if not isinstance(b, int) or b > 0:
                    act.wait_ge(xscore_done, 4 * b)
                act.activation(xq_hi[:], out_a[:], ACT.Identity, bias=bias_q[:, 0:1]).then_inc(xq_hi_ready, 1)

            def keys_high(b, p):
                act.wait_ge(keys_ready, b + 1)
                if not isinstance(b, int) or b > 1:
                    act.wait_ge(xscore_done, 4 * b - 4)
                act.copy(keys_hi[p][:], keys[:].rearrange("c h k -> c (h k)")).then_inc(keys_hi_ready, 1)

            def xexp(b, t):
                act.wait_ge(xsub_done, 4 * b + t + 1)
                act.activation(xprob[t][:], xprob[t][:], ACT.Exp, scale=float(XD) ** -0.5).then_inc(xexp_done, 1)

            def xprobT_copy(b, t):
                act.wait_ge(xprob_turned, 4 * b + t + 1)
                if not (isinstance(b, int) and b == 0 and t < 2):
                    act.wait_ge(xpv_done, 4 * b + t - 1)
                act.copy(xprobT[t % 2][:], turn[t % 2][:].rearrange("k (j n) -> k j n", n=128)).then_inc(xprobT_ready, 1)

            def xo_high(b):
                act.wait_ge(xpv_done, 4 * b + 4)
                if not isinstance(b, int) or b > 0:
                    act.wait_ge(wm_done, b)
                act.copy(xo_hi[:], out_b[:]).then_inc(xo_hi_ready, 1)

            def x2T_high(b):
                act.wait_ge(x2_turned, b + 1)
                act.copy(half_place(x2T_hi, b), qkv_ps[:, 0:D].rearrange("f (c s) -> f c s", c=KC)).then_inc(x2T_hi_ready, 1)


            def cross_step(b, p):
                first, final = isinstance(b, int) and b == 0, isinstance(b, int) and b == B - 1
                xexp(b, 0)
                if not final:
                    x1_high(b + 1)
                    ctx_copy(b + 1)
                xexp(b, 1)
                xexp(b, 2)
                if not final:
                    xq_high(b + 1)
                xprobT_copy(b, 0)
                xexp(b, 3)
                xprobT_copy(b, 1)
                if not final:
                    keys_high(b + 1, 1 - p)
                xprobT_copy(b, 2)
                xprobT_copy(b, 3)
                xo_high(b)
                if not first:
                    x2T_high(b - 1)

            ctx_copy(0)
            act.wait_ge(x1_ready, B)
            act.wait_ge(wo_done, B)
            x1_high(0)
            keys_high(0, 0)
            xq_high(0)

            def split_high(buf, hi_sem, chunks=range(WCH)):
                for c in chunks:
                    hi, raw = (w[:, bass.ds(buf, 1), bass.ds(c, 1)].rearrange("k o c n -> k (o c n)") for w in (w_hi, w_raw))
                    act.copy(hi, raw).then_inc(hi_sem, 1)

            def shared_high(half, f):
                n = FC * half + f
                act.wait_ge(sh_gate_done, n + 1)
                if n > 0:
                    act.wait_ge(shT_lo_ready, n)
                act.activation(sh_z[:], score[f][:], ACT.Silu).then_inc(sh_silu_done, 1)
                act.wait_ge(sh_z_ready, n + 1)
                if half == 1 and f == 0:
                    act.wait_ge(sh_down_done, HB)
                act.copy(shT_hi[:, f], sh_z[:]).then_inc(shT_hi_ready, 1)

            act.wait_ge(moe_in, 16 * 9)
            act.copy(gate_hi[:], gate_in[:]).then_inc(gate_hi_ready, 1)

            def route_half(half):
                act.wait_ge(logits_turned, half + 1)
                if half == 1:
                    act.wait_ge(rows_ready, 1)
                act.activation(e_score[:], qkv_ps[:, 0:HB * NE].rearrange("t (b e) -> t b e", e=NE), ACT.Exp, scale=-1.0).then_inc(logit_exp, 1)
                shared_high(half, 0)
                shared_high(half, 1)

            cross_step(0, 0)
            act.wait_ge(w_in, 16)
            with act.Fori(0, HB // 2) as i:
                cross_step(i * 2 + 1, 1)
                split_high(SETS - 1, sh_hi_ready, [i * 3 + c for c in range(WCH // 2)])
                cross_step(i * 2 + 2, 0)
            route_half(0)
            act.wait_ge(w_in, 32)
            for b in range(HB + 1, B):
                cross_step(b, b % 2)
                k = 2 * (b - HB - 1)
                split_high(0, w_hi_ready, range(k, k + 2))
            x2T_high(B - 1)
            route_half(1)

            act.wait_ge(tables_ready, 1)

            def slot_x_high(t, q):
                act.wait_ge(xs_turned, t + 1)
                if not isinstance(t, int) or t > 1:
                    act.wait_ge(gate_up_done, t - 1)
                act.copy(xsT_hi[q][:].rearrange("f c s -> f (c s)"), turn[0][:]).then_inc(xs_hi_ready, 1)

            def slot_silu(t, q):
                act.wait_ge(gate_up_done, t + 1)
                if not isinstance(t, int) or t > 0:
                    act.wait_ge(z_ready, t)
                act.activation(silu_g[:], score[q][:, 0:FF], ACT.Silu).then_inc(silu_done, 1)

            def slot_z_high(t):
                act.wait_ge(z_turned, t + 1)
                if not isinstance(t, int) or t > 0:
                    act.wait_ge(slot_done, t)
                act.copy(zT_hi[:].rearrange("f c s -> f (c s)"), turn[1][:, 0:FF]).then_inc(zT_hi_ready, 1)

            def y_copy(t, q):
                act.wait_ge(slot_done, t + 1)
                if not isinstance(t, int) or t > 1:
                    act.wait_ge(y_stored[q], 8 * (t - q))
                act.copy(y_sb[q][:], (out_a, out_b)[q][:]).then_inc(y_copied, 1)

            def next_expert_high(t, word, chunks):
                with act.If(word > 0):
                    k, buf = (word >> 2) - 1, (word % 4).with_bounds(min_val=0, max_val=SETS - 1)
                    act.wait_ge(w_in, k * 16 + 48)
                    split_high(buf, w_hi_ready, chunks)

            slot_x_high(0, 0)

            def step(t, q):
                word = act.value_load(tab[0:1, 3, bass.ds(t, 1)], min_val=0, max_val=4 * NE)
                next_expert_high(t, word, EARLY)
                slot_silu(t, q)
                slot_x_high(t + 1, 1 - q)
                next_expert_high(t, word, LATE)
                if not isinstance(t, int) or t > 0:
                    y_copy(t - 1, 1 - q)
                slot_z_high(t)

            slot_steps(act, step, 3)

        @block.gpsimd
        def _(pool):
            pool.wait_ge(consts_ready, 4)

            def rotate(b):
                pool.wait_ge(rope_read, b + 1)
                if not isinstance(b, int) or b > 0:
                    pool.wait_ge(stack_lo, 2 * b)
                r = rotated[:].rearrange("s h (a e) -> s h a e", a=2)
                pool.tensor_tensor(r[:, :, 0], rope_cos[:, :, 0], rope_sin[:, :, 1], ALU.subtract).then_inc(rot_ready, 1)
                pool.tensor_tensor(r[:, :, 1], rope_cos[:, :, 1], rope_sin[:, :, 0], ALU.add).then_inc(rot_ready, 1)

            def mask_probs(b, groups):
                for g in groups:
                    pool.wait_ge(exp_done, 8 * b + g + 1)
                    pool.sem_inc(held)
                    pr = probs[g % 4][:]
                    pool.affine_select(out=pr, in_=pr, pattern=[[0, REP], [1, 128]], compare_op=ALU.is_ge, fill=0.0,
                                       base=0, channel_multiplier=-1).then_inc(causal_done, 1)

            def rstd_1(b):
                pool.wait_ge(mv1, b + 1)
                pool.tensor_tensor(rstd[:], mean_var[:, 1:2], eps[:], ALU.add).then_inc(var_eps, 1)
                pool.wait_ge(var_eps, b + 1)
                pool.tensor_tensor(rstd[:], rstd[:], neg_half[:], ALU.pow).then_inc(rstd1, 1)

            rotate(0)

            def step(b, p):
                first, final = isinstance(b, int) and b == 0, isinstance(b, int) and b == B - 1
                if not final:
                    rotate(b + 1)
                mask_probs(b, (0,))
                if not first:
                    rstd_1(b - 1)
                mask_probs(b, range(1, NKV))

            over_batches(pool, step)
            rstd_1(B - 1)

            def xnormalise(b, t):
                pool.wait_ge(xrec_ready, 4 * b + t + 1)
                pr = xprob[t][:]
                pool.tensor_tensor(pr, pr, xrec[:, t].rearrange("n (h o) -> n h o", o=1).to_broadcast([128, XH, XK]), ALU.mult).then_inc(xprob_ready, 1)

            def rstd_2(b):
                pool.wait_ge(mv2, b + 1)
                pool.tensor_tensor(rstd2[:], mean_var2[:, 1:2], eps[:], ALU.add).then_inc(var_eps, 1)
                pool.wait_ge(var_eps, b + B + 1)
                pool.tensor_tensor(rstd2[:], rstd2[:], neg_half[:], ALU.pow).then_inc(rstd2_ready, 1)

            def x2_keep(b):
                pool.wait_ge(x2s_ready, b + 1)
                pool.tensor_copy(x2[:, bass.ds(b, 1)].rearrange("s o d -> s (o d)"), x2s[:]).then_inc(x2_ready, 1)

            def cross_step(b):
                first = isinstance(b, int) and b == 0
                for t in range(4):
                    xnormalise(b, t)
                if not first:
                    rstd_2(b - 1)
                    x2_keep(b - 1)

            def load_weights(src, buf):
                pool.dma_start(w_raw[:, buf], src).then_inc(w_in, 16)

            pool.wait_ge(x1_ready, B)
            pool.wait_ge(wo_done, B)
            load_weights(T["shared"], SETS - 1)
            pool.wait_ge(w_in, 16)
            load_weights(T["experts"][0], 0)
            pool.wait_ge(w_in, 32)
            load_weights(T["experts"][1], 1)
            pool.wait_ge(w_in, 48)

            def load_expert(k, buf):
                e = pool.value_load(tab[0:1, 7, bass.ds(k, 1)], min_val=0, max_val=NE - 1)
                load_weights(T["experts"][bass.ds(e, 1)].rearrange("o p c n -> (o p) c n"), buf)

            def scatter(b, j):
                if j == 0:
                    pool.wait_ge(x2_ready, b + 1)
                pool.indirect_dma_start(xs_dram, bass.IndirectOffsetOnAxis(ap=row_of[:, j, b:b + 1], axis=0), x2[:, b], None).then_inc(scattered, 16)

            cross_step(0)
            with pool.Fori(1, HB + 1) as b:
                cross_step(b)
            for b in range(HB + 1, B):
                cross_step(b)
                if b == HB + 1:
                    pool.wait_ge(rows_ready, 1)
                for j in range(TOPK):
                    scatter(b - HB - 1, j)
            rstd_2(B - 1)
            x2_keep(B - 1)
            for j in range(TOPK):
                scatter(HB - 1, j)
            pool.wait_ge(rows_ready, 2)
            for b in range(HB, B):
                for j in range(TOPK):
                    scatter(b, j)
            pool.wait_ge(tables_ready, 1)
            pool.wait_ge(sh_down_done, B)
            pool.wait_ge(xs_turned, 1)
            load_expert(2, 2)

            with pool.Fori(1, -(-NE // SETS)) as i:
                for j in range(SETS):
                    k = i * SETS + j
                    used = pool.value_load(tab[0:1, 8, bass.ds(k, 1)], min_val=0, max_val=1)
                    with pool.If(used > 0):
                        pool.wait_ge(w_in, k * 16 + 16)
                        done = pool.value_load(tab[0:1, 9, bass.ds(k, 1)], min_val=1, max_val=SLOTS)
                        pool.wait_ge(slot_done, done)
                        load_expert(k, j)

            pool.wait_ge(yrows_ready, 1)
            pool.wait_ge(results_stored, 1)

            def gather(b, p):
                if b > 3:
                    pool.wait_ge(combined, b - 3)
                for j in range(TOPK):
                    pool.indirect_dma_start(gathered[p][:, j], None, ys_dram, bass.IndirectOffsetOnAxis(ap=yrow_of[:, j, b:b + 1], axis=0)).then_inc(gathered_in[p], 16)

            def rstd_3(pair):
                pool.wait_ge(mv3, 2 * pair + 2)
                r = rstd3[:, pair % 2]
                pool.tensor_tensor(r, mean_var3[:, pair % 2, :, 1], eps[:].to_broadcast([128, 2]), ALU.add).then_inc(var_eps, 1)
                pool.wait_ge(var_eps, pair + 2 * B + 1)
                pool.tensor_tensor(r, r, neg_half[:].to_broadcast([128, 2]), ALU.pow).then_inc(rstd3_ready, 1)

            for b in range(B):
                gather(b, b % 4)
                if b % 2 and b > 2:
                    rstd_3(b // 2 - 1)
            rstd_3(B // 2 - 1)


def lay_out(inputs):
    f = {k: np.asarray(v) for k, v in inputs.items()}
    x = f["x"]
    w = f["L0_attn_w_qkv"]
    half = np.concatenate([np.arange(0, HD, 2), np.arange(1, HD, 2)])
    heads = np.arange(NQ).reshape(NKV // 2, 2, REP).transpose(0, 2, 1).ravel()
    heads = np.concatenate([heads, np.arange(NQ, QK_HEADS)])
    cols = np.concatenate([(heads[:, None] * HD + half[None, :]).ravel(), np.arange(QK_HEADS * HD, QKV)])
    rows = lambda m: m.reshape(m.shape[0] // 128, 128, -1).transpose(1, 0, 2)
    arrays = {
        "x": x,
        "xT": x.transpose(0, 2, 1).reshape(B, KC, 128, S).transpose(0, 2, 1, 3),
        "w_qkv": rows(w[:, cols]),
        "w_o": rows(f["L0_attn_w_o"]),
    }
    ch = np.arange(D // KC).reshape(XD, XH).T.ravel()
    arrays.update({
        "wq": f["L0_xattn_Wq"][ch].T, "wk": f["L0_xattn_Wk"][ch].T, "wv": f["L0_xattn_Wv"][ch].T,
        "wm": f["L0_xattn_Wm"][:, ch].T,
        "bq": f["L0_xattn_bq"][ch][:, None], "bk": f["L0_xattn_bk"][ch][None], "bv": f["L0_xattn_bv"][ch][None],
        "bm": f["L0_xattn_bm"][:, None],
        "proj": rows(np.concatenate([f["L0_xattn_proj_k"], f["L0_xattn_proj_v"]], 1)),
        "ctxT": f["ctx_4096"].transpose(0, 2, 1).reshape(B, KC, 128, S).transpose(0, 2, 1, 3),
    })
    wt = lambda w: rows(w.T)
    ffn = lambda g, u, d: np.concatenate([np.concatenate([wt(g), wt(u)], 2), wt(d)], 1)
    arrays.update({
        "gate": rows(f["L0_ffn_gate_w"].T),
        "bias_e": np.broadcast_to(f["L0_ffn_bias"][None], (128, NE)),
        "experts": np.stack([ffn(f["L0_ffn_Wg"][e], f["L0_ffn_Wu"][e], f["L0_ffn_Wd"][e]) for e in range(NE)]),
        "shared": ffn(f["L0_ffn_Sg"], f["L0_ffn_Su"], f["L0_ffn_Sd"]),
    })
    arrays.update(tables())
    return {k: np.ascontiguousarray(v) for k, v in arrays.items()}


def kernel(**inputs):
    import concourse.bacc as bacc
    from concourse.bass_utils import run_bass_kernel_spmd

    arrays = lay_out(inputs)
    nc = bacc.Bacc("TRN2", target_bir_lowering=False, num_devices=1)
    T = {n: nc.dram_tensor(f"in_{n}", a.shape, mybir.dt.from_np(a.dtype), kind="ExternalInput").ap() for n, a in arrays.items()}
    T["out"] = nc.dram_tensor("out_0", (B, S, D), F32, kind="ExternalOutput").ap()
    program(nc, T)
    r = run_bass_kernel_spmd(nc, [{f"in_{n}": a for n, a in arrays.items()}], core_ids=[0])
    return r.results[0]["out_0"]
```
